# Optimizing a Trainium2 kernel written in Bass

```python
import numpy as np
import jax
import jax.numpy as jnp

def _softmax(x, axis=-1):
    return jax.nn.softmax(x, axis=axis)

def _gelu(x):
    return jax.nn.gelu(x, approximate=True)

def _silu(x):
    return jax.nn.silu(x)

def _sigmoid(x):
    return jax.nn.sigmoid(x)

def _layernorm(x, axis=-1, eps=1e-05):
    m = jnp.mean(x, axis=axis, keepdims=True)
    v = jnp.var(x, axis=axis, keepdims=True)
    return (x - m) / jnp.sqrt(v + eps)

def _scatter_add(tgt, idx, src, axis=0):
    return tgt.at[idx].add(src)

def _segment_sum(src, seg, n):
    return jax.ops.segment_sum(src, seg, n)
kernel_name = 'mk_xattn_seq_d2_seqx_r8_dc13a5'

def setup_inputs(seed: int=0):
    np.random.seed(seed)
    _w = jnp.asarray

    def _rec_inputs():
        import jax
        import jax.numpy as jnp
        _rk = jax.random.key(seed)
        x = -0.0001951 + 1 * jax.random.normal(jax.random.fold_in(_rk, 1), (32, 56, 128), jnp.float32)
        _lenS = 56 - jax.random.randint(jax.random.fold_in(_rk, 7), (32,), 0, max(1, 56 // 4) + 1, jnp.int32)
        _lenS2 = 1500 - jax.random.randint(jax.random.fold_in(_rk, 8), (32,), 0, max(1, 1500 // 4) + 1, jnp.int32)
        _ctx_1024P = jax.random.normal(jax.random.fold_in(_rk, 11), (32, 16, 128), jnp.float32)
        _ctx_1024c = jax.random.dirichlet(jax.random.fold_in(_rk, 511), 0.3 * jnp.ones((16,), jnp.float32), (32, 1500))
        _ctx_1024t = jnp.einsum('bsk,bkd->bsd', _ctx_1024c, _ctx_1024P)
        _ctx_1024t = _ctx_1024t * jax.lax.rsqrt(jnp.mean(jnp.square(_ctx_1024t)) + 1e-12) * 0.953939
        ctx_1024 = -4.82715e-05 + 0.999928 * (_ctx_1024t + 0.3 * jax.random.normal(jax.random.fold_in(_rk, 611), (32, 1500, 128), jnp.float32))
        _validS = jnp.arange(56)[None, :] < _lenS[:, None]
        _validS2 = jnp.arange(1500)[None, :] < _lenS2[:, None]
        _causal = jnp.tril(jnp.ones((56, 56), dtype=bool))
        mask_BxS_bf0 = jnp.logical_not(jnp.ones((32, 56), dtype=bool))
        return (x, ctx_1024, mask_BxS_bf0)
    x, ctx_1024, mask_BxS_bf0 = _rec_inputs()

    def _L0_xattn_setup():
        import jax, jax.numpy as jnp
        import numpy as np
        B, T, J, C, H = (16, 56, 56, 128, 16)
        HD = C // H
        NEG_INF = float('-inf')

        def _layernorm(x, g, b, eps=1e-05):
            mu = jnp.mean(x, axis=-1, keepdims=True)
            var = jnp.var(x, axis=-1, keepdims=True)
            return (x - mu) * jax.lax.rsqrt(var + eps) * g + b

        def _heads(x):
            Bv, S, _ = x.shape
            return x.reshape(Bv, S, H, HD).transpose(0, 2, 1, 3)

        def _merge(x):
            Bv, _, S, _ = x.shape
            return x.transpose(0, 2, 1, 3).reshape(Bv, S, C)

        def _forward(tgt, src, sa_wqkv, sa_wproj, sa_bproj, ed_wkv, ed_wq, ed_wproj, ed_bproj, ff_w1, ff_b1, ff_w2, ff_b2, ln1_g, ln1_b, ln2_g, ln2_b, ln3_g, ln3_b, tgt_padding_mask):
            scale = C ** (-0.5)
            x = _layernorm(tgt, ln1_g, ln1_b)
            qkv = x @ sa_wqkv
            q, k, v = (_heads(t) for t in jnp.split(qkv, 3, axis=-1))
            wei = jnp.einsum('bhtd,bhsd->bhts', q, k) * scale
            causal = jnp.tril(jnp.ones((T, T), bool))
            wei = jnp.where(causal[None, None], wei, NEG_INF)
            wei = jnp.where(tgt_padding_mask[:, None, None, :], NEG_INF, wei)
            wei = jax.nn.softmax(wei, axis=-1)
            sa_out = _merge(jnp.einsum('bhts,bhsd->bhtd', wei, v)) @ sa_wproj + sa_bproj
            result = tgt + sa_out
            xq = _layernorm(result, ln2_g, ln2_b)
            xs = _layernorm(src, ln2_g, ln2_b)
            kv = xs @ ed_wkv
            k2, v2 = (_heads(t) for t in jnp.split(kv, 2, axis=-1))
            q2 = _heads(xq @ ed_wq)
            wei2 = jnp.einsum('bhtd,bhjd->bhtj', q2, k2) * scale
            wei2 = jax.nn.softmax(wei2, axis=-1)
            ed_out = _merge(jnp.einsum('bhtj,bhjd->bhtd', wei2, v2)) @ ed_wproj + ed_bproj
            result = result + ed_out
            h = jax.nn.relu(_layernorm(tgt, ln3_g, ln3_b) @ ff_w1 + ff_b1)
            result = result + (h @ ff_w2 + ff_b2)
            return result
        key = jax.random.key(seed)
        ks = jax.random.split(key, 16)
        s = 0.02
        return {'tgt': jax.random.normal(ks[0], (B, T, C), jnp.float32), 'src': jax.random.normal(ks[1], (B, J, C), jnp.float32), 'sa_wqkv': jax.random.normal(ks[2], (C, 3 * C), jnp.float32) * s, 'sa_wproj': jax.random.normal(ks[3], (C, C), jnp.float32) * s, 'sa_bproj': jnp.zeros((C,), jnp.float32), 'ed_wkv': jax.random.normal(ks[4], (C, 2 * C), jnp.float32) * s, 'ed_wq': jax.random.normal(ks[5], (C, C), jnp.float32) * s, 'ed_wproj': jax.random.normal(ks[6], (C, C), jnp.float32) * s, 'ed_bproj': jnp.zeros((C,), jnp.float32), 'ff_w1': jax.random.normal(ks[7], (C, 4 * C), jnp.float32) * s, 'ff_b1': jnp.zeros((4 * C,), jnp.float32), 'ff_w2': jax.random.normal(ks[8], (4 * C, C), jnp.float32) * s, 'ff_b2': jnp.zeros((C,), jnp.float32), 'ln1_g': jnp.ones((C,), jnp.float32), 'ln1_b': jnp.zeros((C,), jnp.float32), 'ln2_g': jnp.ones((C,), jnp.float32), 'ln2_b': jnp.zeros((C,), jnp.float32), 'ln3_g': jnp.ones((C,), jnp.float32), 'ln3_b': jnp.zeros((C,), jnp.float32), 'tgt_padding_mask': jnp.zeros((B, T), bool)}
    _L0_xattn_all = _L0_xattn_setup()
    _L0_xattn_in = {k: v for k, v in _L0_xattn_all.items() if k in ('sa_wqkv', 'sa_wproj', 'sa_bproj', 'ed_wkv', 'ed_wq', 'ed_wproj', 'ed_bproj', 'ff_w1', 'ff_b1', 'ff_w2', 'ff_b2', 'ln1_g', 'ln1_b', 'ln2_g', 'ln2_b', 'ln3_g', 'ln3_b')}
    del _L0_xattn_all

    def _L1_xattn_setup():
        import jax, jax.numpy as jnp
        import numpy as np
        B, N, DIM = (2, 256, 128)
        HEADS, DH = (16, 64)
        SEG = 64
        NPM = 16
        NM = 16
        DFF = int(DIM * 4 * 2 / 3)
        EPS = 1.1920929e-07

        def rms_norm(x, w):
            return x * jax.lax.rsqrt(jnp.mean(x * x, axis=-1, keepdims=True) + EPS) * w
        key = jax.random.key(seed)
        ks = jax.random.split(key, 10)
        p = lambda i, shape: jax.random.normal(ks[i], shape, jnp.float32) * 0.02
        return {'x': jax.random.normal(ks[0], (B, N, DIM), jnp.float32), 'mem_out': jax.random.normal(ks[1], (B, N, DIM), jnp.float32), 'attn_norm_w': jnp.ones((DIM,), jnp.float32), 'to_qkv_w': p(2, (DIM, 3 * HEADS * DH)), 'to_out_w': p(3, (HEADS * DH, DIM)), 'persist_mem': jax.random.normal(ks[4], (HEADS, NPM, DH), jnp.float32), 'mem_pool_norm_w': jnp.ones((DIM,), jnp.float32), 'to_mem_tokens_w': p(5, (DIM, DIM)), 'ff_norm_w': jnp.ones((DIM,), jnp.float32), 'ff_w1': p(6, (DIM, 2 * DFF)), 'ff_b1': jnp.zeros((2 * DFF,), jnp.float32), 'ff_w2': p(7, (DFF, DIM)), 'ff_b2': jnp.zeros((DIM,), jnp.float32)}
    _L1_xattn_all = _L1_xattn_setup()
    _L1_xattn_in = {k: v for k, v in _L1_xattn_all.items() if k in ('attn_norm_w', 'to_qkv_w', 'to_out_w', 'persist_mem', 'mem_pool_norm_w', 'to_mem_tokens_w', 'ff_norm_w', 'ff_w1', 'ff_b1', 'ff_w2', 'ff_b2')}
    del _L1_xattn_all
    return {'x': x, 'ctx_1024': ctx_1024, 'mask_BxS_bf0': mask_BxS_bf0, 'L0_xattn_sa_wqkv': _L0_xattn_in['sa_wqkv'], 'L0_xattn_sa_wproj': _L0_xattn_in['sa_wproj'], 'L0_xattn_sa_bproj': _L0_xattn_in['sa_bproj'], 'L0_xattn_ed_wkv': _L0_xattn_in['ed_wkv'], 'L0_xattn_ed_wq': _L0_xattn_in['ed_wq'], 'L0_xattn_ed_wproj': _L0_xattn_in['ed_wproj'], 'L0_xattn_ed_bproj': _L0_xattn_in['ed_bproj'], 'L0_xattn_ff_w1': _L0_xattn_in['ff_w1'], 'L0_xattn_ff_b1': _L0_xattn_in['ff_b1'], 'L0_xattn_ff_w2': _L0_xattn_in['ff_w2'], 'L0_xattn_ff_b2': _L0_xattn_in['ff_b2'], 'L0_xattn_ln1_g': _L0_xattn_in['ln1_g'], 'L0_xattn_ln1_b': _L0_xattn_in['ln1_b'], 'L0_xattn_ln2_g': _L0_xattn_in['ln2_g'], 'L0_xattn_ln2_b': _L0_xattn_in['ln2_b'], 'L0_xattn_ln3_g': _L0_xattn_in['ln3_g'], 'L0_xattn_ln3_b': _L0_xattn_in['ln3_b'], 'L1_xattn_attn_norm_w': _L1_xattn_in['attn_norm_w'], 'L1_xattn_to_qkv_w': _L1_xattn_in['to_qkv_w'], 'L1_xattn_to_out_w': _L1_xattn_in['to_out_w'], 'L1_xattn_persist_mem': _L1_xattn_in['persist_mem'], 'L1_xattn_mem_pool_norm_w': _L1_xattn_in['mem_pool_norm_w'], 'L1_xattn_to_mem_tokens_w': _L1_xattn_in['to_mem_tokens_w'], 'L1_xattn_ff_norm_w': _L1_xattn_in['ff_norm_w'], 'L1_xattn_ff_w1': _L1_xattn_in['ff_w1'], 'L1_xattn_ff_b1': _L1_xattn_in['ff_b1'], 'L1_xattn_ff_w2': _L1_xattn_in['ff_w2'], 'L1_xattn_ff_b2': _L1_xattn_in['ff_b2']}

def reference(x, ctx_1024, mask_BxS_bf0, L0_xattn_sa_wqkv, L0_xattn_sa_wproj, L0_xattn_sa_bproj, L0_xattn_ed_wkv, L0_xattn_ed_wq, L0_xattn_ed_wproj, L0_xattn_ed_bproj, L0_xattn_ff_w1, L0_xattn_ff_b1, L0_xattn_ff_w2, L0_xattn_ff_b2, L0_xattn_ln1_g, L0_xattn_ln1_b, L0_xattn_ln2_g, L0_xattn_ln2_b, L0_xattn_ln3_g, L0_xattn_ln3_b, L1_xattn_attn_norm_w, L1_xattn_to_qkv_w, L1_xattn_to_out_w, L1_xattn_persist_mem, L1_xattn_mem_pool_norm_w, L1_xattn_to_mem_tokens_w, L1_xattn_ff_norm_w, L1_xattn_ff_w1, L1_xattn_ff_b1, L1_xattn_ff_w2, L1_xattn_ff_b2):
    import jax
    import jax.numpy as jnp

    def _L0_xattn_ref(tgt, src, sa_wqkv, sa_wproj, sa_bproj, ed_wkv, ed_wq, ed_wproj, ed_bproj, ff_w1, ff_b1, ff_w2, ff_b2, ln1_g, ln1_b, ln2_g, ln2_b, ln3_g, ln3_b, tgt_padding_mask):
        import jax, jax.numpy as jnp
        import numpy as np
        B, T, J, C, H = (16, 56, 56, 128, 16)
        HD = C // H
        NEG_INF = float('-inf')

        def _layernorm(x, g, b, eps=1e-05):
            mu = jnp.mean(x, axis=-1, keepdims=True)
            var = jnp.var(x, axis=-1, keepdims=True)
            return (x - mu) * jax.lax.rsqrt(var + eps) * g + b

        def _heads(x):
            Bv, S, _ = x.shape
            return x.reshape(Bv, S, H, HD).transpose(0, 2, 1, 3)

        def _merge(x):
            Bv, _, S, _ = x.shape
            return x.transpose(0, 2, 1, 3).reshape(Bv, S, C)

        def _forward(tgt, src, sa_wqkv, sa_wproj, sa_bproj, ed_wkv, ed_wq, ed_wproj, ed_bproj, ff_w1, ff_b1, ff_w2, ff_b2, ln1_g, ln1_b, ln2_g, ln2_b, ln3_g, ln3_b, tgt_padding_mask):
            scale = C ** (-0.5)
            x = _layernorm(tgt, ln1_g, ln1_b)
            qkv = x @ sa_wqkv
            q, k, v = (_heads(t) for t in jnp.split(qkv, 3, axis=-1))
            wei = jnp.einsum('bhtd,bhsd->bhts', q, k) * scale
            causal = jnp.tril(jnp.ones((T, T), bool))
            wei = jnp.where(causal[None, None], wei, NEG_INF)
            wei = jnp.where(tgt_padding_mask[:, None, None, :], NEG_INF, wei)
            wei = jax.nn.softmax(wei, axis=-1)
            sa_out = _merge(jnp.einsum('bhts,bhsd->bhtd', wei, v)) @ sa_wproj + sa_bproj
            result = tgt + sa_out
            xq = _layernorm(result, ln2_g, ln2_b)
            xs = _layernorm(src, ln2_g, ln2_b)
            kv = xs @ ed_wkv
            k2, v2 = (_heads(t) for t in jnp.split(kv, 2, axis=-1))
            q2 = _heads(xq @ ed_wq)
            wei2 = jnp.einsum('bhtd,bhjd->bhtj', q2, k2) * scale
            wei2 = jax.nn.softmax(wei2, axis=-1)
            ed_out = _merge(jnp.einsum('bhtj,bhjd->bhtd', wei2, v2)) @ ed_wproj + ed_bproj
            result = result + ed_out
            h = jax.nn.relu(_layernorm(tgt, ln3_g, ln3_b) @ ff_w1 + ff_b1)
            result = result + (h @ ff_w2 + ff_b2)
            return result
        return _forward(tgt, src, sa_wqkv, sa_wproj, sa_bproj, ed_wkv, ed_wq, ed_wproj, ed_bproj, ff_w1, ff_b1, ff_w2, ff_b2, ln1_g, ln1_b, ln2_g, ln2_b, ln3_g, ln3_b, tgt_padding_mask)

    def _L1_xattn_ref(x, mem_out, attn_norm_w, to_qkv_w, to_out_w, persist_mem, mem_pool_norm_w, to_mem_tokens_w, ff_norm_w, ff_w1, ff_b1, ff_w2, ff_b2):
        import jax, jax.numpy as jnp
        import numpy as np
        B, N, DIM = (2, 256, 128)
        HEADS, DH = (16, 64)
        SEG = 64
        NPM = 16
        NM = 16
        DFF = int(DIM * 4 * 2 / 3)
        EPS = 1.1920929e-07

        def rms_norm(x, w):
            return x * jax.lax.rsqrt(jnp.mean(x * x, axis=-1, keepdims=True) + EPS) * w
        b, n, _ = x.shape
        split_heads = lambda t: t.reshape(b, -1, HEADS, DH).transpose(0, 2, 1, 3)
        pooled = rms_norm(mem_out.mean(axis=1), mem_pool_norm_w)
        mem_tok = jnp.broadcast_to((pooled @ to_mem_tokens_w)[:, None, :], (b, NM, DIM))
        _, k_c, v_c = jnp.split(mem_tok @ to_qkv_w, 3, axis=-1)
        k_extra, v_extra = (split_heads(k_c), split_heads(v_c))
        xn = rms_norm(x, attn_norm_w)
        q, k, v = jnp.split(xn @ to_qkv_w, 3, axis=-1)
        q, k, v = (split_heads(q), split_heads(k), split_heads(v))
        pos = jnp.arange(n)
        inv = 1.0 / 10000.0 ** (jnp.arange(0, DH, 2, dtype=jnp.float32) / DH)
        ang = jnp.repeat(pos[:, None].astype(jnp.float32) * inv[None, :], 2, axis=-1)
        cos, sin = (jnp.cos(ang), jnp.sin(ang))

        def rope(t):
            z = t.reshape(t.shape[:-1] + (-1, 2))
            rh = jnp.stack([-z[..., 1], z[..., 0]], axis=-1).reshape(t.shape)
            return t * cos + rh * sin
        q, k = (rope(q), rope(k))
        pm = jnp.broadcast_to(persist_mem[None], (b, HEADS, NPM, DH))
        kf = jnp.concatenate([k_extra, pm, k], axis=2)
        vf = jnp.concatenate([v_extra, pm, v], axis=2)
        P = NPM + NM
        ki = jnp.arange(kf.shape[2])[None, :]
        qi = pos[:, None]
        causal = qi >= ki - P
        seg = qi // SEG == (ki - P) // SEG
        mask = causal & seg | (ki < P)
        scores = jnp.einsum('bhid,bhjd->bhij', q, kf) * DH ** (-0.5)
        scores = jnp.where(mask[None, None], scores, -1e+30)
        probs = jax.nn.softmax(scores, axis=-1)
        o = jnp.einsum('bhij,bhjd->bhid', probs, vf)
        attn_out = o.transpose(0, 2, 1, 3).reshape(b, n, HEADS * DH) @ to_out_w
        x = x + attn_out
        h = rms_norm(x, ff_norm_w) @ ff_w1 + ff_b1
        a, g = jnp.split(h, 2, axis=-1)
        x = x + jax.nn.silu(g) * a @ ff_w2 + ff_b2
        return x
    x = _L0_xattn_ref(x, ctx_1024, L0_xattn_sa_wqkv, L0_xattn_sa_wproj, L0_xattn_sa_bproj, L0_xattn_ed_wkv, L0_xattn_ed_wq, L0_xattn_ed_wproj, L0_xattn_ed_bproj, L0_xattn_ff_w1, L0_xattn_ff_b1, L0_xattn_ff_w2, L0_xattn_ff_b2, L0_xattn_ln1_g, L0_xattn_ln1_b, L0_xattn_ln2_g, L0_xattn_ln2_b, L0_xattn_ln3_g, L0_xattn_ln3_b, mask_BxS_bf0)
    x = _L1_xattn_ref(x, ctx_1024, L1_xattn_attn_norm_w, L1_xattn_to_qkv_w, L1_xattn_to_out_w, L1_xattn_persist_mem, L1_xattn_mem_pool_norm_w, L1_xattn_to_mem_tokens_w, L1_xattn_ff_norm_w, L1_xattn_ff_w1, L1_xattn_ff_b1, L1_xattn_ff_w2, L1_xattn_ff_b2)
    return x

_drawn_inputs = setup_inputs


def setup_inputs(seed=0):
    import zlib

    import numpy as np

    out = dict(_drawn_inputs(seed))
    spreads = {'L0_xattn_sa_bproj': (0.0, 0.1),
     'L0_xattn_ed_bproj': (0.0, 0.1),
     'L0_xattn_ff_b1': (0.0, 0.1),
     'L0_xattn_ff_b2': (0.0, 0.1),
     'L0_xattn_ln1_g': (1.0, 0.6),
     'L0_xattn_ln1_b': (0.0, 0.8),
     'L0_xattn_ln2_g': (1.0, 0.6),
     'L0_xattn_ln2_b': (0.0, 0.8),
     'L0_xattn_ln3_g': (1.0, 0.6),
     'L0_xattn_ln3_b': (0.0, 0.8),
     'L1_xattn_attn_norm_w': (1.0, 0.6),
     'L1_xattn_mem_pool_norm_w': (1.0, 0.6),
     'L1_xattn_ff_norm_w': (1.0, 0.6),
     'L1_xattn_ff_b1': (0.0, 0.8),
     'L1_xattn_ff_b2': (0.0, 0.1)}
    factors = {'L0_xattn_sa_wqkv': 3.559,
     'L0_xattn_sa_wproj': 3.525,
     'L0_xattn_ed_wq': 200.0,
     'L1_xattn_to_mem_tokens_w': 5.988,
     'L1_xattn_ff_w1': 4.641,
     'L1_xattn_ff_w2': 4.566}
    for name, (base, spread) in spreads.items():
        noise = np.random.default_rng([zlib.crc32(name.encode()), seed]).standard_normal(out[name].shape)
        drawn = base * np.exp(spread * noise) if base else spread * noise
        out[name] = jnp.asarray(drawn.astype(out[name].dtype))
    for name, factor in factors.items():
        out[name] = (out[name] * factor).astype(out[name].dtype)
    return out
```

```python
from contextlib import ExitStack

import numpy as np

import concourse.bass as bass
from concourse import mybir

F32 = mybir.dt.float32
F16 = mybir.dt.float16
I32 = mybir.dt.int32
ALU = mybir.AluOpType
ACT = mybir.ActivationFunctionType
AX = mybir.AxisListType

B, T, C = 32, 56, 128
J = 1500
H0, D0 = 16, 8
H1, D1 = 16, 64
NPAIR = B // 2
TP = 64
KT, KP = 12, 125
FF0 = 512
DFF, DFFP = 341, 384
PREFIX, NM = 32, 16
NK1 = TP + PREFIX
EPS0, EPS1 = 1e-5, 1.1920929e-07


def constants():
    p = np.arange(128)
    ident = np.eye(128, dtype=np.float32)
    own_head = (p[:, None] // D0 == np.arange(H0)[None]).astype(np.float32)
    own_in_group = ((p[:, None] % 32) // D0 == np.arange(4)[None]).astype(np.float32)
    own_half = (p[:, None] // 64 == np.arange(2)[None]).astype(np.float32)
    t = p % TP
    s = np.arange(TP)
    later = s[None] > t[:, None]
    causal0 = np.where(later, -1e30, 0.0).astype(np.float32)
    causal1 = np.zeros((128, NK1), np.float32)
    causal1[:, :TP] = np.where(later, -1e30, 0.0)
    d = p % D1
    inv = (1.0 / 10000.0 ** (np.arange(0, D1, 2, dtype=np.float32) / D1)).astype(np.float32)
    ang = (np.arange(TP, dtype=np.float32)[None] * inv[d // 2][:, None]).astype(np.float32)
    cos = np.cos(ang).astype(np.float32)
    sin = np.sin(ang).astype(np.float32)
    sin = np.where(d[:, None] % 2 == 0, -sin, sin).astype(np.float32)
    table = np.concatenate([ident, own_head, own_in_group, own_half, causal0, causal1, cos, sin], 1)
    return np.ascontiguousarray(table.astype(np.float32))


CONST_WIDTH = 128 + 16 + 4 + 2 + 64 + NK1 + 64 + 64


def program(nc, dram):
    ctx = ExitStack()
    with ctx:
        def sb(name, shape, dt=F32):
            return ctx.enter_context(nc.sbuf_tensor(name + "_sb", shape, dt))

        def sem(name):
            return ctx.enter_context(nc.semaphore(name))

        ps_a = ctx.enter_context(nc.psum_tensor("ps_a", [128, 1024], F32))
        ps_b = ctx.enter_context(nc.psum_tensor("ps_b", [128, 1024], F32))
        ps_c = ctx.enter_context(nc.psum_tensor("ps_c", [128, 1024], F32))
        ps_d = ctx.enter_context(nc.psum_tensor("ps_d", [128, 1024], F32))

        const = sb("const", [128, CONST_WIDTH])
        at = 0
        ident = const[:, at:at + 128]; at += 128
        own_head = const[:, at:at + 16]; at += 16
        own_in_group = const[:, at:at + 4]; at += 4
        own_half = const[:, at:at + 2]; at += 2
        causal0 = const[:, at:at + 64]; at += 64
        causal1 = const[:, at:at + NK1]; at += NK1
        cos = const[:, at:at + 64]; at += 64
        sin = const[:, at:at + 64]; at += 64
        w_qkv0 = sb("w_qkv0", [128, 3 * C])
        w_proj0 = sb("w_proj0", [128, C])
        w_kv = sb("w_kv", [128, 2 * C])
        w_q = sb("w_q", [128, C])
        w_projx = sb("w_projx", [128, C])
        w_up0 = sb("w_up0", [128, FF0])
        w_down0 = sb("w_down0", [128, 4, C])
        cols = sb("cols", [128, 6])
        b_up0 = sb("b_up0", [128, 4])
        rows0 = sb("rows0", [128, 3, C])
        b_rest = sb("b_rest", [128, C])

        x_all = sb("x_all", [128, NPAIR, C])
        q_split = sb("q_split", [128, B, 2, 4 * T], F16)
        on_all = sb("on_all", [128, B, TP])
        pool_all = sb("pool_all", [128, B])

        small = sb("small", [128, 64])
        loaded = sem("loaded")
        steps_counted = sem("steps_counted")
        n_loads = [0]

        def alone(eng):
            eng.sem_inc(steps_counted, 1)

        def rsqrt(ve, link, y, v, tmp, eps):
            link(nc.vector.tensor_scalar(v, v, eps, None, ALU.add))
            link(nc.vector.tensor_scalar(y.bitcast(I32), v.bitcast(I32), -0.5, 1597463007.0, ALU.mult, ALU.add))
            for _ in range(3):
                link(nc.vector.tensor_tensor(tmp, y, y, ALU.mult))
                link(nc.vector.scalar_tensor_tensor(tmp, tmp, -0.5, v, ALU.mult, ALU.mult))
                link(nc.vector.scalar_tensor_tensor(y, tmp, 1.5, y, ALU.add, ALU.mult))

        def chain(eng, semaphore, base, per):
            count = [0]

            def link(ins):
                count[0] += 1
                ins.then_inc(semaphore, 1)
                eng.wait_ge(semaphore, base + count[0])

            def ends():
                assert count[0] == per, (semaphore.name if hasattr(semaphore, "name") else "", count[0], per)
            return link, ends

        pad_word = sb("pad_word", [128, NPAIR, TP], I32)
        mask0 = sb("mask0", [128, NPAIR, TP])
        x_clear = sem("x_clear")
        pre_dve = sem("pre_dve")
        with nc.Block() as block:
            @block.gpsimd
            def _(pool):
                nc.gpsimd.memset(x_all[:], 0.0).then_inc(x_clear, 1)
                nc.gpsimd.memset(pad_word[:], 0).then_inc(x_clear, 1)

            @block.sync
            def _(sp):
                def load(dst, src):
                    n_loads[0] += 16
                    sp.dma_start(dst, src).then_inc(loaded, 16)
                load(const[:], dram["const"])
                load(w_qkv0[:], dram["w_qkv0"])
                load(w_proj0[:], dram["w_proj0"])
                load(w_kv[:], dram["w_kv"])
                load(w_q[:], dram["w_q"])
                load(w_projx[:], dram["w_projx"])
                load(w_up0[:], dram["w_up0"])
                load(w_down0[:], dram["w_down0"].rearrange("(j p) n -> p j n", p=128))
                load(cols[:], dram["cols"])
                load(b_up0[:], dram["b_up0"])
                load(rows0[:], dram["rows0"].broadcast_to([128, 3, C]))
                sp.wait_ge(x_clear, 2)
                for b2 in range(2):
                    load(x_all[64 * b2:64 * b2 + T, :, :],
                         dram["x"].rearrange("(p b) t c -> b t p c", b=2)[b2])
                    load(pad_word[64 * b2:64 * b2 + 64, :, 0:T],
                         dram["mask"].rearrange("a (p b) t -> b a p t", b=2)[b2].broadcast_to([64, NPAIR, T]))
                sp.wait_ge(loaded, n_loads[0])

            @block.vector
            def _(ve):
                ve.wait_ge(loaded, 16 * 15)
                link, _ = chain(ve, pre_dve, 0, 0)
                link(nc.vector.tensor_tensor(b_rest[:], rows0[:, 1, :], rows0[:, 2, :], ALU.add))
                link(nc.vector.tensor_copy(mask0[:], pad_word[:]))
                link(nc.vector.tensor_scalar(mask0[:], mask0[:], -1e30, None, ALU.mult))
                link(nc.vector.tensor_tensor(mask0[:], mask0[:],
                                             causal0.unsqueeze(1).broadcast_to([128, NPAIR, TP]), ALU.add))

        with ExitStack() as p1:
            def sb1(name, shape, dt=F32):
                return p1.enter_context(nc.sbuf_tensor(name + "_sb", shape, dt))
            x_now = sb1("x_now", [128, C])
            stats = small[:, 0:6]
            meanvar = small[:, 6:8]
            rstd = small[:, 8:9]
            newton = small[:, 9:10]
            z = sb1("z", [128, C])
            xn1 = sb1("xn1", [128, 128])
            xn3 = sb1("xn3", [128, 128])
            q0 = sb1("q0", [128, 128])
            k_wide = sb1("k_wide", [128, 2, H0, TP])
            v_wide = sb1("v_wide", [128, 2, 8, 2, D0])
            s0 = sb1("s0", [128, H0, TP])
            e0 = sb1("e0", [128, H0, TP])
            s_max = sb1("s_max", [128, H0])
            s_sum = sb1("s_sum", [128, H0])
            e0_t = sb1("e0_t", [128, 8, 128])
            o0 = sb1("o0", [128, C])
            o0_t = sb1("o0_t", [128, 128])
            r1 = sb1("r1", [128, C])
            z2 = sb1("z2", [128, C])
            xq = sb1("xq", [128, 128])
            q_wide = sb1("q_wide", [128, 2, 4, T])
            up0 = sb1("up0", [128, 4, 128])
            names = ["z_ready", "zt_done", "xn1_ready", "xn3_ready", "qkv_done", "q0_ready", "kv_ready", "s0_done",
                     "e0_ready", "s0_ready", "et_done", "et_ready", "o0_done", "o0_ready", "o0t_done",
                     "o0t_ready", "sa_done", "z2_ready", "z2t_done", "xq_ready", "q2_done", "q2_read",
                     "up_done", "up_ready", "down_done", "dve1", "p1_out"]
            S = {n: sem(n) for n in names}
            NL = 41
            with nc.Block() as block:
                @block.tensor
                def _(pe):
                    with pe.Fori(0, NPAIR) as i:
                        def wait(n, k=1, per=1):
                            pe.wait_ge(S[n], i * per + k)
                        wait("z_ready")
                        nc.tensor.transpose(ps_a[:, 0:128], z[:], ident).then_inc(S["zt_done"], 1)
                        wait("xn1_ready")
                        nc.tensor.matmul(ps_b[:, 0:128], w_qkv0[:, 0:128], xn1[:], start=True, stop=True)
                        nc.tensor.matmul(ps_b[:, 512:640], w_qkv0[:, 128:256], xn1[:], start=True, stop=True)
                        for b2 in range(2):
                            for half in range(2):
                                last = nc.tensor.matmul(ps_c[64 * half:64 * half + 64, 512 * b2:512 * b2 + 128],
                                                        xn1[:, 64 * b2:64 * b2 + 64], w_qkv0[:, 256:384],
                                                        start=True, stop=True)
                        last.then_inc(S["qkv_done"], 1)
                        wait("xn3_ready")
                        for j in range(4):
                            last = nc.tensor.matmul(ps_d[:, 128 * j:128 * j + 128], w_up0[:, 128 * j:128 * j + 128],
                                                    xn3[:], start=True, stop=True)
                        last.then_inc(S["up_done"], 1)
                        wait("q0_ready")
                        wait("kv_ready")
                        for half in range(2):
                            for b2 in range(2):
                                last = nc.tensor.matmul(ps_a[64 * b2:64 * b2 + 64, 512 * half:512 * half + 512],
                                                        q0[:, 64 * b2:64 * b2 + 64],
                                                        k_wide[:, b2, 8 * half:8 * half + 8, :].rearrange("p h s -> p (h s)"),
                                                        start=True, stop=True)
                        last.then_inc(S["s0_done"], 1)
                        wait("up_ready")
                        for j in range(4):
                            last = nc.tensor.matmul(ps_d[:, 512:640], up0[:, j, :], w_down0[:, j, :],
                                                    start=(j == 0), stop=(j == 3))
                        last.then_inc(S["down_done"], 1)
                        wait("e0_ready")
                        for c in range(8):
                            last = nc.tensor.transpose((ps_b if c < 4 else ps_c)[:, 128 * (c % 4):128 * (c % 4) + 128],
                                                       e0[:, 2 * c:2 * c + 2, :].rearrange("p h s -> p (h s)"), ident)
                        last.then_inc(S["et_done"], 1)
                        wait("et_ready", 2, 2)
                        for b2 in range(2):
                            for c in range(8):
                                last = nc.tensor.matmul(ps_a[64 * b2:64 * b2 + 64, 16 * c:16 * c + 16],
                                                        e0_t[:, c, 64 * b2:64 * b2 + 64],
                                                        v_wide[:, b2, c, :, :].rearrange("p h d -> p (h d)"),
                                                        start=True, stop=True)
                        last.then_inc(S["o0_done"], 1)
                        wait("o0_ready")
                        nc.tensor.transpose(ps_b[:, 0:128], o0[:], ident).then_inc(S["o0t_done"], 1)
                        wait("o0t_ready")
                        nc.tensor.matmul(ps_c[:, 0:128], o0_t[:], w_proj0[:], start=True, stop=True).then_inc(S["sa_done"], 1)
                        wait("z2_ready")
                        nc.tensor.transpose(ps_b[:, 512:640], z2[:], ident).then_inc(S["z2t_done"], 1)
                        wait("xq_ready")
                        nc.tensor.matmul(ps_c[:, 512:640], w_q[:], xq[:], start=True, stop=True).then_inc(S["q2_done"], 1)

                @block.scalar
                def _(act):
                    with act.Fori(0, NPAIR) as i:
                        def wait(n, k=1, per=1):
                            act.wait_ge(S[n], i * per + k)
                        wait("zt_done")
                        nc.scalar.activation(xn3[:], ps_a[:, 0:128], ACT.Identity, bias=cols[:, 5:6],
                                             scale=cols[:, 4:5]).then_inc(S["xn3_ready"], 1)
                        wait("qkv_done")
                        nc.scalar.mul(q0[:], ps_b[:, 0:128], float(C) ** -0.5).then_inc(S["q0_ready"], 1)
                        wait("up_done")
                        for j in range(4):
                            last = nc.scalar.activation(up0[:, j, :], ps_d[:, 128 * j:128 * j + 128], ACT.Relu,
                                                        bias=b_up0[:, j:j + 1])
                        last.then_inc(S["up_ready"], 1)
                        wait("s0_ready")
                        nc.scalar.activation(e0[:], s0[:], ACT.Exp).then_inc(S["e0_ready"], 1)
                        wait("et_done")
                        nc.scalar.copy(e0_t[:, 0:4, :], ps_b[:, 0:512].rearrange("p (c t) -> p c t", c=4)).then_inc(S["et_ready"], 1)
                        nc.scalar.copy(e0_t[:, 4:8, :], ps_c[:, 0:512].rearrange("p (c t) -> p c t", c=4)).then_inc(S["et_ready"], 1)

                @block.vector
                def _(ve):
                    with ve.Fori(0, NPAIR) as i:
                        def wait(n, k=1, per=1):
                            ve.wait_ge(S[n], i * per + k)
                        link, ends = chain(ve, S["dve1"], i * NL, NL)
                        link(nc.vector.tensor_copy(x_now[:], x_all[:, i, :]))
                        link(nc.vector.bn_stats(stats, x_now[:]))
                        alone(ve)
                        link(nc.vector.bn_aggr(meanvar, stats))
                        rsqrt(ve, link, rstd, meanvar[:, 1:2], newton, EPS0)
                        nc.vector.tensor_scalar(z[:], x_now[:], meanvar[:, 0:1], rstd, ALU.subtract,
                                                ALU.mult).then_inc(S["z_ready"], 1)
                        wait("xn3_ready")
                        nc.vector.tensor_scalar(xn1[:], ps_a[:, 0:128], cols[:, 0:1], cols[:, 1:2], ALU.mult,
                                                ALU.add).then_inc(S["xn1_ready"], 1)
                        wait("qkv_done")
                        for b2 in range(2):
                            link(nc.vector.tensor_tensor(
                                k_wide[:, b2, :, :],
                                ps_b[:, 512 + 64 * b2:576 + 64 * b2].unsqueeze(1).broadcast_to([128, H0, TP]),
                                own_head.unsqueeze(2).broadcast_to([128, H0, TP]), ALU.mult))
                        for b2 in range(2):
                            last = nc.vector.tensor_tensor(
                                v_wide[:, b2, :, :, :],
                                ps_c[:, 512 * b2:512 * b2 + 128].rearrange("p (c h d) -> p c h d", h=2, d=D0),
                                own_half.unsqueeze(1).unsqueeze(3).broadcast_to([128, 8, 2, D0]), ALU.mult)
                            if b2 == 0:
                                link(last)
                        last.then_inc(S["kv_ready"], 1)
                        wait("s0_done")
                        link(nc.vector.tensor_tensor(s0[:], ps_a[:, :].rearrange("p (h s) -> p h s", h=H0),
                                                     mask0[:, i, :].unsqueeze(1).broadcast_to([128, H0, TP]), ALU.add))
                        link(nc.vector.reduce_max(s_max[:], s0[:], AX.X))
                        nc.vector.tensor_tensor(s0[:], s0[:], s_max[:].unsqueeze(2).broadcast_to([128, H0, TP]),
                                                ALU.subtract).then_inc(S["s0_ready"], 1)
                        wait("e0_ready")
                        link(nc.vector.reduce_sum(s_sum[:], e0[:], AX.X))
                        link(nc.vector.reciprocal(s_sum[:], s_sum[:]))
                        wait("o0_done")
                        nc.vector.tensor_tensor(o0[:].rearrange("p (h d) -> p h d", h=H0),
                                                ps_a[:, 0:128].rearrange("p (h d) -> p h d", h=H0),
                                                s_sum[:].unsqueeze(2).broadcast_to([128, H0, D0]),
                                                ALU.mult).then_inc(S["o0_ready"], 1)
                        wait("o0t_done")
                        nc.vector.tensor_copy(o0_t[:], ps_b[:, 0:128]).then_inc(S["o0t_ready"], 1)
                        link(nc.vector.tensor_tensor(x_now[:], x_now[:], rows0[:, 0, :], ALU.add))
                        wait("sa_done")
                        link(nc.vector.tensor_tensor(r1[:], ps_c[:, 0:128], x_now[:], ALU.add))
                        link(nc.vector.bn_stats(stats, r1[:]))
                        alone(ve)
                        link(nc.vector.bn_aggr(meanvar, stats))
                        rsqrt(ve, link, rstd, meanvar[:, 1:2], newton, EPS0)
                        nc.vector.tensor_scalar(z2[:], r1[:], meanvar[:, 0:1], rstd, ALU.subtract,
                                                ALU.mult).then_inc(S["z2_ready"], 1)
                        link(nc.vector.tensor_tensor(r1[:], r1[:], b_rest[:], ALU.add))
                        wait("down_done")
                        link(nc.vector.tensor_tensor(x_all[:, i, :], ps_d[:, 512:640], r1[:], ALU.add))
                        wait("z2t_done")
                        nc.vector.tensor_scalar(xq[:], ps_b[:, 512:640], cols[:, 2:3], cols[:, 3:4], ALU.mult,
                                                ALU.add).then_inc(S["xq_ready"], 1)
                        wait("q2_done")
                        link(nc.vector.scalar_tensor_tensor(
                            q_wide[:, 0, :, :],
                            ps_c[:, 512:512 + T].unsqueeze(1).broadcast_to([128, 4, T]), float(C) ** -0.5,
                            own_in_group.unsqueeze(2).broadcast_to([128, 4, T]), ALU.mult, ALU.mult))
                        link(nc.vector.scalar_tensor_tensor(
                            q_wide[:, 1, :, :],
                            ps_c[:, 576:576 + T].unsqueeze(1).broadcast_to([128, 4, T]), float(C) ** -0.5,
                            own_in_group.unsqueeze(2).broadcast_to([128, 4, T]), ALU.mult, ALU.mult))
                        qw = q_wide[:].rearrange("p b h t -> p b (h t)")
                        q2 = q_split[:].rearrange("p (i b) s n -> p i b s n", b=2)
                        link(nc.vector.tensor_copy(q2[:, i, :, 0, :], qw))
                        nc.vector.tensor_tensor(q2[:, i, :, 1, :], qw, q2[:, i, :, 0, :],
                                                ALU.subtract).then_inc(S["p1_out"], 1)
                        ve.wait_ge(S["p1_out"], i + 1)
                        ends()

        with ExitStack() as p2:
            def sb2(name, shape, dt=F32):
                return p2.enter_context(nc.sbuf_tensor(name + "_sb", shape, dt))
            GROUPS, GN = 4, 4 * T
            ROWS = 96
            W = H0 * T
            context = [sb2(f"context{r}", [KP, KT, C]) for r in range(3)]
            keys = [sb2(f"keys{r}", [ROWS + 2, GROUPS, J], F16) for r in range(3)]
            queries = [sb2(f"queries{r}", [ROWS + 2, W], F16) for r in range(3)]
            values = [sb2(f"values{r}", [KP, KT, 8, 32]) for r in range(3)]
            xs_t = sb2("xs_t", [128, J])
            k_split = sb2("k_split", [128, 2, J], F16)
            best = sb2("best", [KP, W])
            probs = [sb2(f"probs{r}", [KP, W]) for r in range(2)]
            neg_max = sb2("neg_max", [128, 7])
            shift = sb2("shift", [7, 2, 128], F16)
            o_wide = sb2("o_wide", [128, 4 * T])
            o_rec = sb2("o_rec", [T, 16])
            o_rows = sb2("o_rows", [T, C])
            st = sb2("st", [KP, KT, 6])
            ln = sb2("ln", [KP, 6, KT])
            ones = sb2("ones", [KP, 1])
            per = dict(context_in=16, pool_done=1, pooled=1, stats_ready=1, z_ready=3, t_done=3, xs_ready=3,
                       k_done=3, khigh_ready=3, klow_ready=3, keys_in=192, v_done=3, values_ready=3,
                       queries_in=192, scan_done=12, best_ready=12, best_t_done=2, neg_ready=2, neg_t_done=1,
                       shift_ready=1, shift_in=32, scores_done=12, probs_ready=12, pv_done=12, o_read=1,
                       o_t_done=1, o_rows_ready=1, o_rows_t_done=1, on_ready=1)
            Q = {n: [sem(f"cross_{n}{r}") for r in range(3)] if n.endswith("_in") else sem("cross_" + n) for n in per}
            cleared = sem("cleared")
            ln_chain = sem("ln_chain")
            o_chain = sem("o_chain")
            m_chain = sem("m_chain")
            NLN = 7 + 11
            ring = [ps_c[:, 0:512], ps_c[:, 512:1024]]
            o_bank = ps_d[:, 0:4 * T]
            misc = ps_d[:, 512:1024]

            def halves(ps):
                return ps.rearrange("p (e n) -> p e n", e=2)[:, :, 0:448]

            def steps(eng, emit):
                def one(b, r, turn):
                    emit(b, r, lambda d, b=b: not isinstance(b, int) or 0 <= b + d < B, turn)
                for b in range(-4, 1):
                    one(b, b % 3, lambda d, b=b: (b + d) // 3)
                with eng.Fori(0, 9) as i:
                    for r in range(1, 4):
                        one(i * 3 + r, r % 3, lambda d, r=r: i + (r + d) // 3)
                for b in range(28, B + 1):
                    one(b, b % 3, lambda d, b=b: (b + d) // 3)

            def landed(n, d, r):
                return Q[n][(r + d) % 3]

            def waiter(eng, b, r, turn):
                def wait(n, d, k):
                    if n.endswith("_in"):
                        if k == 0:
                            d, k = d - 1, per[n]
                            if isinstance(b, int) and b + d < 0:
                                return
                        eng.wait_ge(landed(n, d, r), turn(d) * per[n] + k)
                        return
                    value = (b + d) * per[n] + k
                    assert isinstance(b, int) or (1 + d) * per[n] + k > 0, "the loop starts at batch 1"
                    if not isinstance(value, int) or value > 0:
                        eng.wait_ge(Q[n], value)
                return wait

            with nc.Block() as block:
                @block.gpsimd
                def _(pool):
                    fills = [(ones[:], 1.0), (on_all[:], 0.0)]
                    for r in range(3):
                        fills += [(keys[r][ROWS:ROWS + 2, :, :], 1.0), (values[r][:, :, :, 17:32], 0.0),
                                  (values[r][:, :, :, 16:17], 1.0)]
                    for n, (where, value) in enumerate(fills):
                        nc.gpsimd.memset(where, value).then_inc(cleared, 1)
                        pool.wait_ge(cleared, n + 1)

                    def emit(b, r, has, turn):
                        wait = waiter(pool, b, r, turn)
                        if has(3):
                            wait("stats_ready", 3, 1)
                            wait("pool_done", 3, 1)
                            alone(pool)
                            for k in range(KT):
                                tile = context[r][:, k, :]
                                ins = nc.gpsimd.tensor_scalar(tile, tile, ln[:, 4, k:k + 1], ln[:, 5, k:k + 1],
                                                              ALU.mult, ALU.add)
                                if k % 4 == 3:
                                    ins.then_inc(Q["z_ready"], 1)
                    steps(pool, emit)

                @block.sync
                def _(sp):
                    def emit(b, r, has, turn):
                        wait = waiter(sp, b, r, turn)
                        r1, r2 = (r + 1) % 3, (r + 2) % 3
                        if has(4):
                            wait("t_done", 1, 3)
                            sp.dma_start(context[r1][:], dram["ctx"][b + 4].rearrange("(p k) c -> p k c", k=KT)
                                         ).then_inc(landed("context_in", 4, r), 16)
                        if has(2):
                            wait("scores_done", 0, 0)
                            for block_, half in ((0, 0), (1, 1), (2, 0)):
                                for g in range(GROUPS):
                                    sp.dma_start(queries[r2][32 * block_:32 * block_ + 32, GN * g:GN * g + GN],
                                                 q_split[32 * g:32 * g + 32, b + 2, half, :]).then_inc(landed("queries_in", 2, r), 16)
                            wait("khigh_ready", 2, 3)
                            for block_, half in ((0, 0), (1, 0), (2, 1)):
                                if half:
                                    wait("klow_ready", 2, 3)
                                for g in range(GROUPS):
                                    sp.dma_start(keys[r2][32 * block_:32 * block_ + 32, g, :],
                                                 k_split[32 * g:32 * g + 32, half, :]).then_inc(landed("keys_in", 2, r), 16)
                        if has(1):
                            wait("shift_ready", 1, 1)
                            for half in range(2):
                                sp.dma_start(queries[r1][ROWS + half:ROWS + half + 1, :],
                                             shift[:, half, :]).then_inc(landed("shift_in", 1, r), 16)
                    steps(sp, emit)

                @block.tensor
                def _(pe):
                    pe.wait_ge(cleared, 11)

                    def pv(b, d, k, r, wait):
                        wait("probs_ready", d, k + 1)
                        if k == 0:
                            wait("values_ready", d, 3)
                            wait("o_read", d, 0)
                        for g in range(8):
                            last = nc.tensor.matmul(o_bank[32 * (g % 4):32 * (g % 4) + 32, 112 * (g // 4):112 * (g // 4) + 112],
                                                    values[r][:, k, g, :], probs[k % 2][:, 112 * g:112 * g + 112],
                                                    start=(k == 0 and g < 4), stop=(k == KT - 1),
                                                    tile_position=(0, 32 * (g % 4)), skip_group_check=True)
                        last.then_inc(Q["pv_done"], 1)

                    def scores(out, r, k, rows):
                        for g in range(GROUPS):
                            col = 512 * (g // 2) + GN * (g % 2)
                            last = nc.tensor.matmul(out[0:KP, col:col + GN], keys[r][0:rows, g, KP * k:KP * k + KP],
                                                    queries[r][0:rows, GN * g:GN * g + GN], start=True, stop=True)
                        return last

                    def emit(b, r, has, turn):
                        wait = waiter(pe, b, r, turn)
                        r1, r2 = (r + 1) % 3, (r + 2) % 3

                        def scan(k):
                            if k == 0:
                                wait("keys_in", 1, 192)
                                wait("queries_in", 1, 192)
                            wait("best_ready", 1, k)
                            scores(ps_b, r1, k, ROWS).then_inc(Q["scan_done"], 1)

                        for s in range(KT):
                            if has(0):
                                if s == 0:
                                    wait("shift_in", 0, 32)
                                wait("probs_ready", 0, s)
                                scores(ps_a, r, s, ROWS + 2).then_inc(Q["scores_done"], 1)
                            if has(1) and s < 6:
                                scan(2 * s)
                            if s == 0 and has(-1):
                                pv(b, -1, KT - 1, r2, wait)
                            if s > 0 and has(0):
                                pv(b, 0, s - 1, r, wait)
                            if has(1) and s < 6:
                                scan(2 * s + 1)
                            if has(2) and s < 3:
                                wait("z_ready", 2, s + 1)
                                if s == 0:
                                    wait("values_ready", 1, 3)
                                elif s == 1:
                                    wait("pooled", 2, 1)
                                else:
                                    wait("xs_ready", 2, 1)
                                for k in range(4):
                                    last = nc.tensor.transpose(ring[s % 2][:, KP * k:KP * k + KP],
                                                               context[r2][:, 4 * s + k, :], ident[0:KP, 0:KP])
                                last.then_inc(Q["t_done"], 1)
                            if has(2) and 3 <= s < 6:
                                u = s - 3
                                wait("xs_ready", 2, 2 if u == 0 else 3)
                                if u == 2:
                                    wait("klow_ready", 2, 1)
                                nc.tensor.matmul(ring[s % 2][:, 0:500], w_kv[:, 0:128], xs_t[:, 500 * u:500 * u + 500],
                                                 start=True, stop=True).then_inc(Q["k_done"], 1)
                            if has(2) and 6 <= s < 9:
                                u = s - 6
                                if u < 2:
                                    wait("klow_ready", 2, u + 2)
                                else:
                                    wait("values_ready", 2, 1)
                                for k in range(4):
                                    last = nc.tensor.matmul(ring[s % 2][0:KP, 128 * k:128 * k + 128],
                                                            xs_t[:, 500 * u + KP * k:500 * u + KP * k + KP],
                                                            w_kv[:, 128:256], start=True, stop=True)
                                last.then_inc(Q["v_done"], 1)
                            if has(3) and s == 9:
                                wait("context_in", 3, 16)
                                wait("values_ready", 2, 2)
                                for k in range(KT):
                                    last = nc.tensor.matmul(ring[1][:, 0:1], context[r][:, k, :], ones[:],
                                                            start=(k == 0), stop=(k == KT - 1))
                                last.then_inc(Q["pool_done"], 1)
                            if has(-1) and s == 2:
                                wait("o_read", -1, 1)
                                if has(0):
                                    wait("shift_ready", 0, 1)
                                else:
                                    wait("on_ready", -2, 1)
                                alone(pe)
                                for e in range(4):
                                    last = nc.tensor.transpose(misc[0:T, 128 * e:128 * e + 128],
                                                               o_wide[:, T * e:T * e + T], ident)
                                last.then_inc(Q["o_t_done"], 1)
                            if has(-1) and s == 4:
                                wait("o_rows_ready", -1, 1)
                                alone(pe)
                                nc.tensor.transpose(misc[:, 0:T], o_rows[:], ident[0:T, 0:T]).then_inc(Q["o_rows_t_done"], 1)
                            if has(1) and s in (6, 7):
                                if s == 6:
                                    wait("best_ready", 1, KT)
                                    wait("on_ready", -1, 1)
                                else:
                                    wait("neg_ready", 1, 1)
                                chunks = range(0, 4) if s == 6 else range(4, 7)
                                for n, c in enumerate(chunks):
                                    last = nc.tensor.transpose(misc[:, KP * n:KP * n + KP],
                                                               best[:, 128 * c:128 * c + 128], ident[0:KP, 0:KP])
                                last.then_inc(Q["best_t_done"], 1)
                            if has(1) and s == 8:
                                wait("neg_ready", 1, 2)
                                nc.tensor.transpose(misc[0:7, 0:128], neg_max[:], ident).then_inc(Q["neg_t_done"], 1)
                    steps(pe, emit)

                @block.scalar
                def _(act):
                    act.wait_ge(cleared, 11)

                    def emit(b, r, has, turn):
                        wait = waiter(act, b, r, turn)
                        r1, r2 = (r + 1) % 3, (r + 2) % 3
                        for s in range(KT):
                            if has(0):
                                wait("scores_done", 0, s + 1)
                                wait("pv_done", 0, s - 1)
                                nc.scalar.activation(probs[s % 2][:].rearrange("p (e n) -> p e n", e=2),
                                                     halves(ps_a[0:KP, :]), ACT.Exp).then_inc(Q["probs_ready"], 1)
                            if s == 0 and has(-1):
                                wait("pv_done", -1, KT)
                                nc.scalar.copy(o_wide[:], o_bank).then_inc(Q["o_read"], 1)
                            if has(2) and s < 3:
                                wait("t_done", 2, s + 1)
                                wait("v_done", 2, 0)
                                nc.scalar.activation(xs_t[:, 500 * s:500 * s + 500], ring[s % 2][:, 0:500], ACT.Identity,
                                                     bias=cols[:, 3:4], scale=cols[:, 2:3]).then_inc(Q["xs_ready"], 1)
                            if has(2) and 3 <= s < 6:
                                u = s - 3
                                wait("k_done", 2, u + 1)
                                wait("keys_in", 2, 0)
                                nc.scalar.copy(k_split[:, 0, 500 * u:500 * u + 500], ring[s % 2][:, 0:500]
                                               ).then_inc(Q["khigh_ready"], 1)
                            if has(2) and 6 <= s < 9:
                                u = s - 6
                                wait("v_done", 2, u + 1)
                                wait("pv_done", -1, KT)
                                nc.scalar.copy(values[r2][:, 4 * u:4 * u + 4, :, 0:16],
                                               ring[s % 2][0:KP, :].rearrange("p (k g n) -> p k g n", k=4, g=8)
                                               ).then_inc(Q["values_ready"], 1)
                            if has(3) and s == 9:
                                wait("pool_done", 3, 1)
                                nc.scalar.copy(pool_all[:, bass.ds(b + 3, 1)] if not isinstance(b, int) else
                                               pool_all[:, b + 3:b + 4], ring[1][:, 0:1]).then_inc(Q["pooled"], 1)
                    steps(act, emit)

                @block.vector
                def _(ve):
                    ve.wait_ge(cleared, 11)

                    def emit(b, r, has, turn):
                        wait = waiter(ve, b, r, turn)
                        ln_link, ln_ends = chain(ve, ln_chain, (b + 3) * NLN, NLN)
                        o_link, _ = chain(ve, o_chain, b - 1, 1)
                        m_link, _ = chain(ve, m_chain, b + 1, 1)

                        def keep_best(k):
                            wait("scan_done", 1, k + 1)
                            both = best[:].rearrange("p (e n) -> p e n", e=2)
                            if k == 0:
                                wait("best_t_done", 1, 0)
                                ins = nc.vector.tensor_copy(both, halves(ps_b[0:KP, :]))
                            else:
                                wait("best_ready", 1, k)
                                ins = nc.vector.tensor_tensor(both, halves(ps_b[0:KP, :]), both, ALU.max)
                            ins.then_inc(Q["best_ready"], 1)

                        for s in range(KT):
                            if has(1) and s < 6:
                                keep_best(2 * s)
                                keep_best(2 * s + 1)
                            if has(-1) and s == 2:
                                wait("o_t_done", -1, 1)
                                t4 = misc[0:T, :].rearrange("p (e h q r) -> p e h q r", e=2, h=2, q=4)
                                rec = o_rec[:].rearrange("p (e h q) -> p e h q", e=2, h=2)
                                o_link(nc.vector.reciprocal(o_rec[:], misc[0:T, :].rearrange("p (n r) -> p n r", r=32)[:, :, 16]))
                                rows = o_rows[:].rearrange("p (e q h d) -> p e q h d", e=2, q=4, h=2)
                                for h in range(2):
                                    ins = nc.vector.tensor_tensor(rows[:, :, :, h, :], t4[:, :, h, :, 8 * h:8 * h + 8],
                                                                  rec[:, :, h, :].unsqueeze(3).broadcast_to([T, 2, 4, 8]),
                                                                  ALU.mult)
                                ins.then_inc(Q["o_rows_ready"], 1)
                            if has(-1) and s == 4:
                                wait("o_rows_t_done", -1, 1)
                                nc.vector.tensor_copy(on_all[:, b - 1, 0:T], misc[:, 0:T]).then_inc(Q["on_ready"], 1)
                            if has(2) and 3 <= s < 6:
                                u = s - 3
                                wait("khigh_ready", 2, u + 1)
                                wait("keys_in", 2, 0)
                                nc.vector.tensor_tensor(k_split[:, 1, 500 * u:500 * u + 500], ring[s % 2][:, 0:500],
                                                        k_split[:, 0, 500 * u:500 * u + 500], ALU.subtract
                                                        ).then_inc(Q["klow_ready"], 1)
                            if has(1) and s in (6, 7):
                                wait("best_t_done", 1, s - 5)
                                n = 4 if s == 6 else 3
                                nc.vector.tensor_reduce(neg_max[:, 4 * (s - 6):4 * (s - 6) + n],
                                                        misc[:, 0:KP * n].rearrange("p (c j) -> p c j", c=n),
                                                        axis=AX.X, op=ALU.max, negate=True).then_inc(Q["neg_ready"], 1)
                            if has(1) and s == 8:
                                wait("neg_t_done", 1, 1)
                                wait("shift_in", 1, 0)
                                m_link(nc.vector.tensor_copy(shift[:, 0, :], misc[0:7, 0:128]))
                                nc.vector.tensor_tensor(shift[:, 1, :], misc[0:7, 0:128], shift[:, 0, :],
                                                        ALU.subtract).then_inc(Q["shift_ready"], 1)
                            if has(3) and 5 <= s < 9:
                                if s == 5:
                                    wait("context_in", 3, 16)
                                for k in range(3 * (s - 5), 3 * (s - 5) + 3):
                                    ins = nc.vector.bn_stats(st[:, k, :], context[r][:, k, :])
                                if s == 8:
                                    ln_link(ins)
                            if has(3) and s == 9:
                                mu, var, rstd, tmp = ln[:, 0, :], ln[:, 1, :], ln[:, 2, :], ln[:, 3, :]
                                wait("z_ready", 3, 0)
                                ln_link(nc.vector.tensor_tensor(mu, st[:, :, 1], st[:, :, 4], ALU.add))
                                ln_link(nc.vector.tensor_tensor(tmp, st[:, :, 1], st[:, :, 4], ALU.subtract))
                                ln_link(nc.vector.tensor_tensor(var, st[:, :, 2], st[:, :, 5], ALU.add))
                                ln_link(nc.vector.tensor_tensor(tmp, tmp, tmp, ALU.mult))
                                ln_link(nc.vector.tensor_scalar(tmp, tmp, 0.25, None, ALU.mult))
                                ln_link(nc.vector.scalar_tensor_tensor(var, var, 1.0 / C, tmp, ALU.mult, ALU.add))
                                rsqrt(ve, ln_link, ln[:, 4, :], var, tmp, EPS0)
                                nc.vector.scalar_tensor_tensor(ln[:, 5, :], mu, -0.5, ln[:, 4, :], ALU.mult,
                                                               ALU.mult).then_inc(Q["stats_ready"], 1)
                                ln_ends()
                    steps(ve, emit)

        with ExitStack() as p3:
            def sb3(name, shape, dt=F32):
                return p3.enter_context(nc.sbuf_tensor(name + "_sb", shape, dt))
            NJ = 8
            w_qk1 = sb3("w_qk1", [128, 2, 1024])
            w_turn = sb3("w_turn", [128, 2, 1024])
            w_v1 = sb3("w_v1", [128, 1024])
            w_out1 = sb3("w_out1", [128, NJ, C])
            w_mem = sb3("w_mem", [128, C])
            w_up1 = sb3("w_up1", [128, 6, 128])
            w_down1 = sb3("w_down1", [128, 3, C])
            cols1 = sb3("cols1", [128, 3 + 6])
            neg_gate_b = sb3("neg_gate_b", [128, 3])
            row_b1 = sb3("row_b1", [128, C])
            persist_v = sb3("persist_v", [PREFIX + TP, 1024])
            mem_rows = sb3("mem_rows", [B, C])
            mem_st = sb3("mem_st", [B, 12])
            mem_cols = sb3("mem_cols", [128, B])
            mem_t = sb3("mem_t", [128, B])
            mem_wide = sb3("mem_wide", [128, B, PREFIX])
            mem_k = sb3("mem_k", [128, NJ, B])
            x0 = sb3("x0", [128, C])
            on_now = sb3("on_now", [128, 128])
            mem_now = sb3("mem_now", [128, 2, PREFIX])
            st1 = sb3("st1", [128, 12])
            xn = sb3("xn", [128, C])
            xn_t = sb3("xn_t", [128, 128])
            turn_a = [sb3(f"turn_a{n}", [128, 8, TP]) for n in range(2)]
            turn_b = [sb3(f"turn_b{n}", [128, 8, TP]) for n in range(2)]
            q1 = sb3("q1", [128, NJ, 128])
            k1 = sb3("k1", [128, NJ, 2, NK1])
            v1 = sb3("v1", [NK1, 2, 1024])
            s1 = sb3("s1", [128, 16, NK1])
            e1 = sb3("e1", [128, 16, NK1])
            s1_max = sb3("s1_max", [128, 16])
            s1_sum = sb3("s1_sum", [128, 16])
            e1_t = sb3("e1_t", [NK1, 16, 128])
            o1_t = sb3("o1_t", [128, NJ, 128])
            x1 = sb3("x1", [128, C])
            h_n = sb3("h_n", [128, C])
            h_t = sb3("h_t", [128, 128])
            gate_e = sb3("gate_e", [128, 3, 128])
            gate = sb3("gate", [128, 3, 128])
            up1 = sb3("up1", [128, 3, 128])
            y = sb3("y", [128, C])
            names = ["on_now", "projx_done", "xn_ready", "xnt_done", "xnt_ready", "turn_done", "turn_read",
                     "rotated", "v_done", "v_copied", "v_ready", "s_done", "s_ready", "e_ready", "sum_ready",
                     "e_normal", "et_done", "et_ready", "o_done", "o_ready", "out_done", "hn_ready", "ht_done",
                     "ht_ready", "up_done", "gate_ready", "up_ready", "down_done", "y_ready"]
            R = {n: sem("seg_" + n) for n in names}
            stored = sem("stored")
            loaded1 = sem("loaded1")
            dve3 = sem("dve3")
            mem_pe = sem("mem_pe")
            mem_dve = sem("mem_dve")
            ND3 = 45
            n_loads1 = 16 * 12

            with nc.Block() as block:
                @block.sync
                def _(sp):
                    def load(dst, src):
                        sp.dma_start(dst, src).then_inc(loaded1, 16)
                    load(w_mem[:], dram["w_mem"])
                    load(w_qk1[:], dram["w_qkv1"][:, 0:2048].rearrange("p (a n) -> p a n", a=2))
                    load(w_turn[:], dram["w_turn"])
                    load(w_v1[:], dram["w_qkv1"][:, 2048:3072])
                    load(w_out1[:], dram["w_out1"].rearrange("(j p) n -> p j n", p=128))
                    load(w_up1[:], dram["w_up1"])
                    load(w_down1[:], dram["w_down1"].rearrange("(j p) n -> p j n", p=128))
                    load(cols1[:], dram["cols1"])
                    load(row_b1[:], dram["row_b1"].broadcast_to([128, C]))
                    sp.wait_ge(mem_dve, 1)
                    load(persist_v[TP + NM:NK1, :], dram["persist_v"])
                    for b2 in range(2):
                        load(k1[:, :, b2, TP + NM:NK1], dram["persist_k"])
                    sp.wait_ge(loaded1, n_loads1)
                    sp.sem_inc(stored, 1)
                    with sp.Fori(0, NPAIR) as i:
                        sp.wait_ge(R["y_ready"], i + 1)
                        for b2 in range(2):
                            sp.dma_start(dram["out"].rearrange("(p b) t c -> p b t c", b=2)[i, b2],
                                         y[64 * b2:64 * b2 + T, :]).then_inc(stored, 16)
                    sp.wait_ge(stored, 32 * NPAIR + 1)

                @block.gpsimd
                def _(pool):
                    with pool.Fori(0, NPAIR) as i:
                        for n in range(4):
                            pool.wait_ge(R["turn_read"], i * 4 + n + 1)
                            if n < 2:
                                dst = q1[:, 4 * n:4 * n + 4, :].rearrange("p j (b t) -> p (j b) t", b=2)
                            else:
                                dst = k1[:, 4 * (n - 2):4 * (n - 2) + 4, :, 0:TP].rearrange("p j b t -> p (j b) t")
                            nc.gpsimd.tensor_tensor(dst, turn_a[n % 2][:], turn_b[n % 2][:], ALU.add).then_inc(R["rotated"], 1)
                        pool.wait_ge(R["sum_ready"], i + 1)
                        nc.gpsimd.tensor_tensor(e1[:], e1[:], s1_sum[:].unsqueeze(2).broadcast_to([128, 16, NK1]),
                                                ALU.mult).then_inc(R["e_normal"], 1)

                @block.tensor
                def _(pe):
                    nc.tensor.transpose(ps_a[0:B, 0:128], pool_all[:], ident).then_inc(mem_pe, 1)
                    pe.wait_ge(mem_dve, 2)
                    nc.tensor.transpose(ps_a[:, 512:512 + B], mem_rows[:], ident[0:B, 0:B]).then_inc(mem_pe, 1)
                    pe.wait_ge(mem_dve, 3)
                    nc.tensor.matmul(ps_b[:, 0:B], w_mem[:], mem_cols[:], start=True, stop=True).then_inc(mem_pe, 1)
                    pe.wait_ge(mem_dve, 4)
                    for j in range(NJ):
                        last = nc.tensor.matmul(ps_b[:, 512 + B * j:512 + B * j + B], w_qk1[:, 1, 128 * j:128 * j + 128],
                                                mem_t[:], start=True, stop=True)
                    last.then_inc(mem_pe, 1)
                    pe.wait_ge(mem_dve, 5)
                    with pe.Fori(0, NPAIR) as i:
                        def wait(n, k=1, per=1):
                            pe.wait_ge(R[n], i * per + k)
                        wait("on_now")
                        nc.tensor.matmul(ps_a[:, 0:128], on_now[:], w_projx[:], start=True, stop=True).then_inc(R["projx_done"], 1)
                        wait("xn_ready")
                        nc.tensor.transpose(ps_a[:, 512:640], xn[:], ident).then_inc(R["xnt_done"], 1)
                        wait("xnt_ready")
                        for n in range(4):
                            ps = (ps_a, ps_b)[n % 2]
                            if n >= 2:
                                wait("turn_read", n - 1, 4)
                            for j in range(4):
                                cut = slice(512 * (n % 2) + 128 * j, 512 * (n % 2) + 128 * j + 128)
                                nc.tensor.matmul(ps[:, 128 * j:128 * j + 128], w_qk1[:, n // 2, cut], xn_t[:],
                                                 start=True, stop=True)
                                last = nc.tensor.matmul(ps[:, 512 + 128 * j:640 + 128 * j], w_turn[:, n // 2, cut],
                                                        xn_t[:], start=True, stop=True)
                            last.then_inc(R["turn_done"], 1)
                            if n == 1:
                                for b2 in range(2):
                                    ps = (ps_c, ps_d)[b2]
                                    for half in range(2):
                                        w = w_v1[:, 512 * half:512 * half + 512]
                                        nc.tensor.matmul(ps[0:TP, 512 * half:512 * half + 512],
                                                         xn_t[:, 64 * b2:64 * b2 + 64], w, start=True, stop=True)
                                        last = nc.tensor.matmul(ps[TP:NK1, 512 * half:512 * half + 512],
                                                                mem_now[:, b2, :], w, start=True, stop=True)
                                last.then_inc(R["v_done"], 1)
                        wait("turn_read", 4, 4)
                        wait("rotated", 4, 4)
                        alone(pe)
                        for half in range(2):
                            ps = (ps_a, ps_b)[half]
                            for j4 in range(4):
                                j = 4 * half + j4
                                for r in range(2):
                                    for b2 in range(2):
                                        last = nc.tensor.matmul(ps[64 * b2:64 * b2 + 64, 512 * r + NK1 * j4:512 * r + NK1 * j4 + NK1],
                                                                q1[64 * r:64 * r + 64, j, 64 * b2:64 * b2 + 64],
                                                                k1[64 * r:64 * r + 64, j, b2, :], start=True, stop=True)
                            last.then_inc(R["s_done"], 1)
                        wait("s_ready", 2, 2)
                        wait("e_normal")
                        for half in range(2):
                            ps = (ps_a, ps_b)[half]
                            for n in range(8):
                                last = nc.tensor.transpose(ps[0:NK1, 128 * n:128 * n + 128], e1[:, 8 * half + n, :], ident)
                            last.then_inc(R["et_done"], 1)
                        wait("v_ready")
                        for half in range(2):
                            wait("et_ready", half + 1, 2)
                            for r in range(2):
                                for j4 in range(4):
                                    j = 4 * half + j4
                                    h = 2 * j + r
                                    for b2 in range(2):
                                        last = nc.tensor.matmul(ps_c[64 * r:64 * r + 64, 128 * j + 64 * b2:128 * j + 64 * b2 + 64],
                                                                v1[:, b2, D1 * h:D1 * h + D1],
                                                                e1_t[:, 8 * half + 4 * r + j4, 64 * b2:64 * b2 + 64],
                                                                start=True, stop=True)
                            last.then_inc(R["o_done"], 1)
                        wait("o_ready", 2, 2)
                        for j in range(NJ):
                            last = nc.tensor.matmul(ps_d[:, 0:128], o1_t[:, j, :], w_out1[:, j, :], start=(j == 0),
                                                    stop=(j == NJ - 1))
                        last.then_inc(R["out_done"], 1)
                        wait("hn_ready")
                        nc.tensor.transpose(ps_d[:, 512:640], h_n[:], ident).then_inc(R["ht_done"], 1)
                        wait("ht_ready")
                        for n in range(6):
                            col = 512 * (n // 3) + 128 * (n % 3)
                            last = nc.tensor.matmul(ps_a[:, col:col + 128], w_up1[:, n, :], h_t[:], start=True, stop=True)
                        last.then_inc(R["up_done"], 1)
                        wait("up_ready")
                        for n in range(3):
                            last = nc.tensor.matmul(ps_b[:, 0:128], up1[:, n, :], w_down1[:, n, :], start=(n == 0), stop=(n == 2))
                        last.then_inc(R["down_done"], 1)

                @block.scalar
                def _(act):
                    with act.Fori(0, NPAIR) as i:
                        def wait(n, k=1, per=1):
                            act.wait_ge(R[n], i * per + k)
                        wait("xnt_done")
                        nc.scalar.activation(xn_t[:], ps_a[:, 512:640], ACT.Identity, scale=cols1[:, 0:1]).then_inc(R["xnt_ready"], 1)
                        wait("v_done")
                        for b2 in range(2):
                            last = nc.scalar.copy(v1[0:TP, b2, :], (ps_c, ps_d)[b2][0:TP, :])
                        last.then_inc(R["v_copied"], 1)
                        wait("s_ready", 3, 3)
                        nc.scalar.activation(e1[:], s1[:], ACT.Exp, scale=float(D1) ** -0.5).then_inc(R["e_ready"], 1)
                        for half in range(2):
                            wait("et_done", half + 1, 2)
                            nc.scalar.copy(e1_t[:, 8 * half:8 * half + 8, :],
                                           (ps_a, ps_b)[half][0:NK1, :].rearrange("p (n t) -> p n t", n=8)).then_inc(R["et_ready"], 1)
                        for half in range(2):
                            wait("o_done", half + 1, 2)
                            nc.scalar.copy(o1_t[:, 4 * half:4 * half + 4, :],
                                           ps_c[:, 512 * half:512 * half + 512].rearrange("p (n t) -> p n t", n=4)).then_inc(R["o_ready"], 1)
                        wait("ht_done")
                        nc.scalar.activation(h_t[:], ps_d[:, 512:640], ACT.Identity, scale=cols1[:, 2:3]).then_inc(R["ht_ready"], 1)
                        wait("up_done")
                        for n in range(3):
                            last = nc.scalar.activation(gate_e[:, n, :], ps_a[:, 512 + 128 * n:640 + 128 * n], ACT.Exp,
                                                        bias=neg_gate_b[:, n:n + 1], scale=-1.0)
                        last.then_inc(R["gate_ready"], 1)

                @block.vector
                def _(ve):
                    link, _ = chain(ve, sem("mem_chain"), 0, 0)
                    link(nc.vector.memset(persist_v[:], 0.0))
                    nc.vector.memset(mem_wide[:], 0.0).then_inc(mem_dve, 1)
                    ve.wait_ge(mem_pe, 1)
                    ve.wait_ge(loaded1, n_loads1)
                    link(nc.vector.tensor_scalar(neg_gate_b[:], cols1[:, 6:9], -1.0, None, ALU.mult))
                    link(nc.vector.tensor_scalar(mem_rows[:], ps_a[0:B, 0:128], 1.0 / J, None, ALU.mult))
                    link(nc.vector.bn_stats(mem_st[:, 0:6], mem_rows[:]))
                    link(nc.vector.bn_aggr(mem_st[:, 6:8], mem_st[:, 0:6]))
                    link(nc.vector.tensor_tensor(mem_st[:, 8:9], mem_st[:, 6:7], mem_st[:, 6:7], ALU.mult))
                    link(nc.vector.tensor_tensor(mem_st[:, 8:9], mem_st[:, 8:9], mem_st[:, 7:8], ALU.add))
                    rsqrt(ve, link, mem_st[:, 9:10], mem_st[:, 8:9], mem_st[:, 10:11], EPS1)
                    nc.vector.tensor_scalar(mem_rows[:], mem_rows[:], mem_st[:, 9:10], None, ALU.mult).then_inc(mem_dve, 1)
                    ve.wait_ge(mem_pe, 2)
                    nc.vector.tensor_scalar(mem_cols[:], ps_a[:, 512:512 + B], cols1[:, 1:2], None, ALU.mult).then_inc(mem_dve, 1)
                    ve.wait_ge(mem_pe, 3)
                    nc.vector.tensor_copy(mem_t[:], ps_b[:, 0:B]).then_inc(mem_dve, 1)
                    ve.wait_ge(mem_dve, 4)
                    link(nc.vector.tensor_copy(mem_wide[:, :, 0:NM], mem_t[:].unsqueeze(2).broadcast_to([128, B, NM])))
                    ve.wait_ge(mem_pe, 4)
                    nc.vector.tensor_copy(mem_k[:], ps_b[:, 512:768].rearrange("p (j b) -> p j b", j=NJ)).then_inc(mem_dve, 1)
                    ve.wait_ge(mem_dve, 5)
                    with ve.Fori(0, NPAIR) as i:
                        def wait(n, k=1, per=1):
                            ve.wait_ge(R[n], i * per + k)
                        link, ends = chain(ve, dve3, i * ND3, ND3)

                        def rms(out, x, n):
                            link(nc.vector.bn_stats(st1[:, 0:6], x))
                            alone(ve)
                            link(nc.vector.bn_aggr(st1[:, 6:8], st1[:, 0:6]))
                            link(nc.vector.tensor_tensor(st1[:, 8:9], st1[:, 6:7], st1[:, 6:7], ALU.mult))
                            link(nc.vector.tensor_tensor(st1[:, 8:9], st1[:, 8:9], st1[:, 7:8], ALU.add))
                            rsqrt(ve, link, st1[:, 9:10], st1[:, 8:9], st1[:, 10:11], EPS1)
                            nc.vector.tensor_scalar(out, x, st1[:, 9:10], None, ALU.mult).then_inc(R[n], 1)

                        pairs = on_all[:].rearrange("p (i b) t -> p i (b t)", b=2)
                        nc.vector.tensor_copy(on_now[:], pairs[:, i, :]).then_inc(R["on_now"], 1)
                        wide = mem_wide[:].rearrange("p (i b) n -> p i b n", b=2)
                        link(nc.vector.tensor_copy(mem_now[:], wide[:, i, :, :]))
                        mk = mem_k[:].rearrange("p j (i b) -> p i j b", b=2)
                        for b2 in range(2):
                            link(nc.vector.tensor_copy(k1[:, :, b2, TP:TP + NM],
                                                       mk[:, i, :, b2].unsqueeze(2).broadcast_to([128, NJ, NM])))
                        wait("projx_done")
                        link(nc.vector.tensor_tensor(x0[:], ps_a[:, 0:128], x_all[:, i, :], ALU.add))
                        rms(xn[:], x0[:], "xn_ready")
                        for n in range(4):
                            ps = (ps_a, ps_b)[n % 2]
                            wait("turn_done", n + 1, 4)
                            if n >= 2:
                                wait("rotated", n - 1, 4)
                            for dst, half, table in ((turn_a, 0, cos), (turn_b, 1, sin)):
                                ins = nc.vector.tensor_tensor(dst[n % 2][:],
                                                              ps[:, 512 * half:512 * half + 512].rearrange("p (n t) -> p n t", n=8),
                                                              table.unsqueeze(1).broadcast_to([128, 8, TP]), ALU.mult)
                            ins.then_inc(R["turn_read"], 1)
                            if n == 1:
                                wait("v_copied")
                                for b2 in range(2):
                                    ins = nc.vector.tensor_tensor(v1[TP:NK1, b2, :], (ps_c, ps_d)[b2][TP:NK1, :],
                                                                  persist_v[TP:NK1, :], ALU.add)
                                ins.then_inc(R["v_ready"], 1)
                        for half in range(2):
                            wait("s_done", half + 1, 2)
                            for r in range(2):
                                at_ = 8 * half + 4 * r
                                ins = nc.vector.tensor_tensor(s1[:, at_:at_ + 4, :],
                                                              (ps_a, ps_b)[half][:, 512 * r:512 * r + 4 * NK1].rearrange("p (j k) -> p j k", j=4),
                                                              causal1.unsqueeze(1).broadcast_to([128, 4, NK1]), ALU.add)
                                if r == 0:
                                    link(ins)
                            ins.then_inc(R["s_ready"], 1)
                        ve.wait_ge(R["s_ready"], i * 3 + 2)
                        link(nc.vector.reduce_max(s1_max[:], s1[:], AX.X))
                        nc.vector.tensor_tensor(s1[:], s1[:], s1_max[:].unsqueeze(2).broadcast_to([128, 16, NK1]),
                                                ALU.subtract).then_inc(R["s_ready"], 1)
                        wait("e_ready")
                        link(nc.vector.reduce_sum(s1_sum[:], e1[:], AX.X))
                        nc.vector.reciprocal(s1_sum[:], s1_sum[:]).then_inc(R["sum_ready"], 1)
                        wait("out_done")
                        link(nc.vector.tensor_tensor(x1[:], ps_d[:, 0:128], x0[:], ALU.add))
                        rms(h_n[:], x1[:], "hn_ready")
                        wait("gate_ready")
                        link(nc.vector.tensor_tensor(gate[:], ps_a[:, 512:896].rearrange("p (n t) -> p n t", n=3),
                                                     cols1[:, 6:9].unsqueeze(2).broadcast_to([128, 3, 128]), ALU.add))
                        link(nc.vector.tensor_scalar(gate_e[:], gate_e[:], 1.0, None, ALU.add))
                        link(nc.vector.reciprocal(gate_e[:], gate_e[:]))
                        link(nc.vector.tensor_tensor(gate[:], gate[:], gate_e[:], ALU.mult))
                        link(nc.vector.tensor_tensor(up1[:], ps_a[:, 0:384].rearrange("p (n t) -> p n t", n=3),
                                                     cols1[:, 3:6].unsqueeze(2).broadcast_to([128, 3, 128]), ALU.add))
                        nc.vector.tensor_tensor(up1[:], up1[:], gate[:], ALU.mult).then_inc(R["up_ready"], 1)
                        wait("down_done")
                        link(nc.vector.tensor_tensor(x1[:], x1[:], row_b1[:], ALU.add))
                        ve.wait_ge(stored, i * 32 + 1)
                        nc.vector.tensor_tensor(y[:], ps_b[:, 0:128], x1[:], ALU.add).then_inc(R["y_ready"], 1)
                        ve.wait_ge(R["y_ready"], i + 1)
                        ends()


def as_words(a):
    words = np.zeros(a.shape + (4,), np.uint8)
    words[..., 0] = a.view(np.uint8)
    return words.view(np.int32)[..., 0]


INPUTS = {
    "x": ("x", lambda a: a),
    "ctx": ("ctx_1024", lambda a: a),
    "mask": ("mask_BxS_bf0", lambda a: as_words(a).reshape(1, B, T)),
    "w_qkv0": ("L0_xattn_sa_wqkv", lambda a: a),
    "w_proj0": ("L0_xattn_sa_wproj", lambda a: a),
    "w_kv": ("L0_xattn_ed_wkv", lambda a: a),
    "w_q": ("L0_xattn_ed_wq", lambda a: a),
    "w_projx": ("L0_xattn_ed_wproj", lambda a: a),
    "w_up0": ("L0_xattn_ff_w1", lambda a: a),
    "w_down0": ("L0_xattn_ff_w2", lambda a: a),
    "b_up0": ("L0_xattn_ff_b1", lambda a: a.reshape(4, 128).T),
}


def layout(inputs):
    g = {k: np.asarray(v) for k, v in inputs.items()}
    out = {n: np.ascontiguousarray(f(g[k])) for n, (k, f) in INPUTS.items()}
    out["cols"] = np.ascontiguousarray(np.stack(
        [g[f"L0_xattn_ln{n}_{v}"] for n in (1, 2, 3) for v in "gb"], 1))
    out["rows0"] = np.ascontiguousarray(np.stack(
        [g["L0_xattn_sa_bproj"], g["L0_xattn_ed_bproj"], g["L0_xattn_ff_b2"]]).reshape(1, 3, C))
    w = g["L1_xattn_to_qkv_w"]
    out["w_qkv1"] = w
    out["w_turn"] = w[:, :2048].reshape(128, 2, 512, 2)[..., ::-1].reshape(128, 2, 1024)
    out["w_out1"] = g["L1_xattn_to_out_w"]
    out["w_mem"] = g["L1_xattn_to_mem_tokens_w"]
    persist = g["L1_xattn_persist_mem"]
    out["persist_k"] = persist.reshape(8, 2, NM, D1).transpose(1, 3, 0, 2).reshape(128, 8, NM)
    out["persist_v"] = persist.transpose(1, 0, 2).reshape(NM, H1 * D1)
    up = np.zeros((128, 2, DFFP), np.float32)
    up[:, :, :DFF] = g["L1_xattn_ff_w1"].reshape(128, 2, DFF)
    out["w_up1"] = up.reshape(128, 6, 128)
    up_b = np.zeros((2, DFFP), np.float32)
    up_b[:, :DFF] = g["L1_xattn_ff_b1"].reshape(2, DFF)
    down = np.zeros((DFFP, C), np.float32)
    down[:DFF] = g["L1_xattn_ff_w2"]
    out["w_down1"] = down
    norms = np.stack([g[f"L1_xattn_{n}_norm_w"] for n in ("attn", "mem_pool", "ff")], 1)
    out["cols1"] = np.concatenate([norms, up_b.reshape(6, 128).T], 1)
    out["row_b1"] = g["L1_xattn_ff_b2"].reshape(1, C)
    out["const"] = constants()
    out = {n: np.ascontiguousarray(a) for n, a in out.items()}
    return out


def kernel(**inputs):
    import concourse.bacc as bacc
    from concourse.bass_utils import run_bass_kernel_spmd

    nc = bacc.Bacc("TRN2", target_bir_lowering=False, num_devices=1)
    arrays = layout(inputs)
    dram = {n: nc.dram_tensor(f"in_{n}", a.shape, mybir.dt.from_np(a.dtype), kind="ExternalInput").ap()
            for n, a in arrays.items()}
    dram["out"] = nc.dram_tensor("out", (B, T, C), F32, kind="ExternalOutput").ap()
    program(nc, dram)
    result = run_bass_kernel_spmd(nc, [{f"in_{n}": a for n, a in arrays.items()}], core_ids=[0])
    return result.results[0]["out"]
```

```python
from contextlib import ExitStack

import numpy as np

import concourse.bass as bass
from concourse import mybir

F32 = mybir.dt.float32
F16 = mybir.dt.float16
I32 = mybir.dt.int32
ALU = mybir.AluOpType
ACT = mybir.ActivationFunctionType
AX = mybir.AxisListType

B, T, C = 32, 56, 128
J = 1500
H0, D0 = 16, 8
H1, D1 = 16, 64
NPAIR = B // 2
TP = 64
KT, KP = 12, 125
FF0 = 512
U = 4
DFF, DFFP = 341, 384
PREFIX, NM = 32, 16
NK1 = TP + PREFIX
EPS0, EPS1 = 1e-5, 1.1920929e-07


def constants():
    p = np.arange(128)
    ident = np.eye(128, dtype=np.float32)
    own_head = (p[:, None] // D0 == np.arange(H0)[None]).astype(np.float32)
    own_in_group = ((p[:, None] % 32) // D0 == np.arange(4)[None]).astype(np.float32)
    own_half = (p[:, None] // 64 == np.arange(2)[None]).astype(np.float32)
    t = p % TP
    s = np.arange(TP)
    later = s[None] > t[:, None]
    causal0 = np.where(later, -1e30, 0.0).astype(np.float32)
    causal1 = np.zeros((128, NK1), np.float32)
    causal1[:, :TP] = np.where(later, -1e30, 0.0)
    d = p % D1
    inv = (1.0 / 10000.0 ** (np.arange(0, D1, 2, dtype=np.float32) / D1)).astype(np.float32)
    ang = (np.arange(TP, dtype=np.float32)[None] * inv[d // 2][:, None]).astype(np.float32)
    cos = np.cos(ang).astype(np.float32)
    sin = np.sin(ang).astype(np.float32)
    sin = np.where(d[:, None] % 2 == 0, -sin, sin).astype(np.float32)
    table = np.concatenate([ident, own_head, own_in_group, own_half, causal0, causal1, cos, sin], 1)
    return np.ascontiguousarray(table.astype(np.float32))


CONST_WIDTH = 128 + 16 + 4 + 2 + 64 + NK1 + 64 + 64


def program(nc, dram):
    ctx = ExitStack()
    with ctx:
        def sb(name, shape, dt=F32):
            return ctx.enter_context(nc.sbuf_tensor(name + "_sb", shape, dt))

        def sem(name):
            return ctx.enter_context(nc.semaphore(name))

        ps_a = ctx.enter_context(nc.psum_tensor("ps_a", [128, 1024], F32))
        ps_b = ctx.enter_context(nc.psum_tensor("ps_b", [128, 1024], F32))
        ps_c = ctx.enter_context(nc.psum_tensor("ps_c", [128, 1024], F32))
        ps_d = ctx.enter_context(nc.psum_tensor("ps_d", [128, 1024], F32))

        banks = [(ps_a, ps_b, ps_c, ps_d)[n // 2][:, 512 * (n % 2):512 * (n % 2) + 512] for n in range(8)]

        const = sb("const", [128, CONST_WIDTH])
        at = 0
        ident = const[:, at:at + 128]; at += 128
        own_head = const[:, at:at + 16]; at += 16
        own_in_group = const[:, at:at + 4]; at += 4
        own_half = const[:, at:at + 2]; at += 2
        causal0 = const[:, at:at + 64]; at += 64
        causal1 = const[:, at:at + NK1]; at += NK1
        cos = const[:, at:at + 64]; at += 64
        sin = const[:, at:at + 64]; at += 64
        w_projx = sb("w_projx", [128, C])
        x_all = sb("x_all", [128, NPAIR, C])
        on_all = sb("on_all", [128, B, TP])
        pool_all = sb("pool_all", [128, B])

        early = ExitStack()

        def sbe(name, shape, dt=F32):
            return early.enter_context(nc.sbuf_tensor(name + "_sb", shape, dt))
        w_qkv0 = sbe("w_qkv0", [128, 3 * C])
        w_proj0 = sbe("w_proj0", [128, C])
        w_kv = sbe("w_kv", [128, 2 * C])
        w_q = sbe("w_q", [128, C])
        w_up0 = sbe("w_up0", [128, FF0])
        w_down0 = sbe("w_down0", [128, 4, C])
        cols = sbe("cols", [128, 6])
        b_up0 = sbe("b_up0", [128, 4])
        rows0 = sbe("rows0", [128, 3, C])
        b_rest = sbe("b_rest", [128, C])
        q_split = sbe("q_split", [128, B, 2, 4 * T], F16)

        loaded = sem("loaded")
        steps_counted = sem("steps_counted")
        n_loads = [0]

        def alone(eng):
            eng.sem_inc(steps_counted, 1)

        def rsqrt(ve, link, y, v, tmp, eps):
            link(nc.vector.tensor_scalar(v, v, eps, None, ALU.add))
            link(nc.vector.tensor_scalar(y.bitcast(I32), v.bitcast(I32), -0.5, 1597463007.0, ALU.mult, ALU.add))
            for _ in range(3):
                link(nc.vector.tensor_tensor(tmp, y, y, ALU.mult))
                link(nc.vector.scalar_tensor_tensor(tmp, tmp, -0.5, v, ALU.mult, ALU.mult))
                link(nc.vector.scalar_tensor_tensor(y, tmp, 1.5, y, ALU.add, ALU.mult))

        def chain(eng, semaphore, base, per):
            count = [0]

            def link(ins):
                count[0] += 1
                ins.then_inc(semaphore, 1)
                eng.wait_ge(semaphore, base + count[0])

            def ends():
                assert count[0] == per, (semaphore.name if hasattr(semaphore, "name") else "", count[0], per)
            return link, ends

        masks = ExitStack()
        pad_word = masks.enter_context(nc.sbuf_tensor("pad_word_sb", [128, NPAIR, TP], I32))
        mask0 = masks.enter_context(nc.sbuf_tensor("mask0_sb", [128, NPAIR, TP], F32))
        x_clear = sem("x_clear")
        pre_dve = sem("pre_dve")
        with nc.Block() as block:
            @block.gpsimd
            def _(pool):
                nc.gpsimd.memset(x_all[:], 0.0).then_inc(x_clear, 1)
                nc.gpsimd.memset(pad_word[:], 0).then_inc(x_clear, 1)

            @block.sync
            def _(sp):
                def load(dst, src):
                    n_loads[0] += 16
                    sp.dma_start(dst, src).then_inc(loaded, 16)
                load(const[:], dram["const"])
                load(w_qkv0[:], dram["w_qkv0"])
                load(w_proj0[:], dram["w_proj0"])
                load(w_kv[:], dram["w_kv"])
                load(w_q[:], dram["w_q"])
                load(w_projx[:], dram["w_projx"])
                load(w_up0[:], dram["w_up0"])
                load(w_down0[:], dram["w_down0"].rearrange("(j p) n -> p j n", p=128))
                load(cols[:], dram["cols"])
                load(b_up0[:], dram["b_up0"])
                load(rows0[:], dram["rows0"].broadcast_to([128, 3, C]))
                sp.wait_ge(x_clear, 2)
                for b2 in range(2):
                    load(x_all[64 * b2:64 * b2 + T, :, :],
                         dram["x"].rearrange("(p b) t c -> b t p c", b=2)[b2])
                    load(pad_word[64 * b2:64 * b2 + 64, :, 0:T],
                         dram["mask"].rearrange("a (p b) t -> b a p t", b=2)[b2].broadcast_to([64, NPAIR, T]))
                sp.wait_ge(loaded, n_loads[0])

            @block.vector
            def _(ve):
                ve.wait_ge(loaded, 16 * 15)
                link, _ = chain(ve, pre_dve, 0, 0)
                link(nc.vector.tensor_tensor(b_rest[:], rows0[:, 1, :], rows0[:, 2, :], ALU.add))
                link(nc.vector.tensor_copy(mask0[:], pad_word[:]))
                link(nc.vector.tensor_scalar(mask0[:], mask0[:], -1e30, None, ALU.mult))
                link(nc.vector.tensor_tensor(mask0[:], mask0[:],
                                             causal0.unsqueeze(1).broadcast_to([128, NPAIR, TP]), ALU.add))

        with masks, ExitStack() as p1:
            def sb1(name, shape, dt=F32):
                return p1.enter_context(nc.sbuf_tensor(name + "_sb", shape, dt))
            stats = sb1("stats", [128, U, 6])
            meanvar = sb1("meanvar", [128, U, 2])
            rstd = sb1("rstd", [128, U])
            newton = sb1("newton", [128, U])
            z = sb1("z", [128, U, C])
            xn1 = sb1("xn1", [128, U * 128])
            xn3 = sb1("xn3", [128, U * 128])
            q0 = sb1("q0", [128, U * 128])
            k_wide = [sb1(f"k_wide{n}", [128, 2, H0, TP]) for n in range(2)]
            v_wide = sb1("v_wide", [128, 2 * U, 8, 2, D0])
            s0 = [sb1(f"s0_{u}", [128, H0, TP]) for u in range(U)]
            s_max = sb1("s_max", [128, U, H0])
            s_sum = sb1("s_sum", [128, U, H0])
            e0_t = [sb1(f"e0_t{n}", [128, 8, 128]) for n in range(2)]
            o0 = sb1("o0", [128, U * C])
            o0_t = sb1("o0_t", [128, U * 128])
            r1 = sb1("r1", [128, U, C])
            z2 = sb1("z2", [128, U, C])
            xq = sb1("xq", [128, U * 128])
            q_halves = sb1("q_halves", [128, 2, U * 128], F16)
            up0 = sb1("up0", [128, 4, U * 128])
            per1 = dict(k_ready=U, s0_done=U, s0_max=U, s0_ready=U, e0_ready=U, et_done=2 * U, et_ready=2 * U,
                        up_done=4, up_ready=4, pv0_done=U - 1)
            names = ["z_ready", "zt_done", "xn1_ready", "xn3_ready", "qk_done", "v_done", "q0_ready", "v_ready",
                     "o0_done", "o0_ready", "o0t_done", "o0t_ready", "sa_done", "z2_ready", "z2t_done",
                     "xq_ready", "q2_done", "q_high", "q_low", "q_out", "down_done", *per1]
            S = {n: sem("self_" + n) for n in names}
            dve1 = sem("dve1")
            NL = 36
            NIT = NPAIR // U

            def waiter1(eng, i):
                def wait(n, k=1):
                    eng.wait_ge(S[n], i * per1.get(n, 1) + k)
                return wait
            with nc.Block() as block:
                @block.tensor
                def _(pe):
                    def values0(pe, i, u):
                        wait = waiter1(pe, i)
                        wait("et_ready", 2 * u + 2)
                        for b2 in range(2):
                            for c in range(8):
                                last = nc.tensor.matmul(banks[0][64 * b2:64 * b2 + 64, 128 * u + 16 * c:128 * u + 16 * c + 16],
                                                        e0_t[u % 2][:, c, 64 * b2:64 * b2 + 64],
                                                        v_wide[:, 2 * u + b2, c, :, :].rearrange("p h d -> p (h d)"),
                                                        start=True, stop=True)
                        if u < U - 1:
                            last.then_inc(S["pv0_done"], 1)
                        return last

                    with pe.Fori(0, NIT) as i:
                        wait = waiter1(pe, i)
                        wait("z_ready")
                        for u in range(U):
                            last = nc.tensor.transpose(banks[0][:, 128 * u:128 * u + 128], z[:, u, :], ident)
                        last.then_inc(S["zt_done"], 1)
                        wait("xn1_ready")
                        nc.tensor.matmul(banks[1], w_qkv0[:, 0:128], xn1[:], start=True, stop=True)
                        nc.tensor.matmul(banks[2], w_qkv0[:, 128:256], xn1[:], start=True, stop=True
                                         ).then_inc(S["qk_done"], 1)
                        for n in range(2 * U):
                            for half in range(2):
                                last = nc.tensor.matmul(ps_d[64 * half:64 * half + 64, 128 * n:128 * n + 128],
                                                        xn1[:, 64 * n:64 * n + 64], w_qkv0[:, 256:384],
                                                        start=True, stop=True)
                        last.then_inc(S["v_done"], 1)
                        wait("xn3_ready")
                        for j in range(4):
                            if j >= 2:
                                wait("up_ready", j - 1)
                            nc.tensor.matmul(banks[4 + j % 2], w_up0[:, 128 * j:128 * j + 128], xn3[:], start=True,
                                             stop=True).then_inc(S["up_done"], 1)
                        wait("q0_ready")
                        for u in range(U):
                            wait("k_ready", u + 1)
                            if u >= 2:
                                wait("s0_max", u - 1)
                            if u == 1:
                                wait("up_ready", 4)
                            ps = (ps_a, ps_c)[u % 2]
                            for half in range(2):
                                for b2 in range(2):
                                    last = nc.tensor.matmul(ps[64 * b2:64 * b2 + 64, 512 * half:512 * half + 512],
                                                            q0[:, 128 * u + 64 * b2:128 * u + 64 * b2 + 64],
                                                            k_wide[u % 2][:, b2, 8 * half:8 * half + 8, :].rearrange("p h s -> p (h s)"),
                                                            start=True, stop=True)
                            last.then_inc(S["s0_done"], 1)
                        wait("v_ready")
                        for u in range(U):
                            for j in range(4):
                                last = nc.tensor.matmul(banks[6][:, 128 * u:128 * u + 128], up0[:, j, 128 * u:128 * u + 128],
                                                        w_down0[:, j, :], start=(j == 0), stop=(j == 3))
                        last.then_inc(S["down_done"], 1)
                        for u in range(U):
                            wait("e0_ready", u + 1)
                            if u == 0:
                                wait("s0_max", U)
                            for part in range(2):
                                n = 2 * u + part
                                if n >= 2:
                                    wait("et_ready", n - 1)
                                for c in range(4):
                                    last = nc.tensor.transpose(banks[4 + part][:, 128 * c:128 * c + 128],
                                                               s0[u][:, 8 * part + 2 * c:8 * part + 2 * c + 2, :].rearrange("p h s -> p (h s)"),
                                                               ident)
                                last.then_inc(S["et_done"], 1)
                            if u > 0:
                                values0(pe, i, u - 1)
                        values0(pe, i, U - 1).then_inc(S["o0_done"], 1)
                        wait("o0_ready")
                        for u in range(U):
                            last = nc.tensor.transpose(banks[1][:, 128 * u:128 * u + 128], o0[:, 128 * u:128 * u + 128], ident)
                        last.then_inc(S["o0t_done"], 1)
                        wait("o0t_ready")
                        for u in range(U):
                            last = nc.tensor.matmul(banks[2][:, 128 * u:128 * u + 128], o0_t[:, 128 * u:128 * u + 128],
                                                    w_proj0[:], start=True, stop=True)
                        last.then_inc(S["sa_done"], 1)
                        wait("z2_ready")
                        for u in range(U):
                            last = nc.tensor.transpose(banks[3][:, 128 * u:128 * u + 128], z2[:, u, :], ident)
                        last.then_inc(S["z2t_done"], 1)
                        wait("xq_ready")
                        nc.tensor.matmul(banks[7], w_q[:], xq[:], start=True, stop=True).then_inc(S["q2_done"], 1)

                @block.scalar
                def _(act):
                    with act.Fori(0, NIT) as i:
                        wait = waiter1(act, i)
                        wait("zt_done")
                        nc.scalar.activation(xn3[:], banks[0], ACT.Identity, bias=cols[:, 5:6],
                                             scale=cols[:, 4:5]).then_inc(S["xn3_ready"], 1)
                        wait("qk_done")
                        nc.scalar.mul(q0[:], banks[1], float(C) ** -0.5).then_inc(S["q0_ready"], 1)
                        for j in range(4):
                            wait("up_done", j + 1)
                            nc.scalar.activation(up0[:, j, :], banks[4 + j % 2], ACT.Relu,
                                                 bias=b_up0[:, j:j + 1]).then_inc(S["up_ready"], 1)
                        for u in range(U):
                            wait("s0_ready", u + 1)
                            nc.scalar.activation(s0[u][:], s0[u][:], ACT.Exp).then_inc(S["e0_ready"], 1)
                        for u in range(U):
                            for part in range(2):
                                wait("et_done", 2 * u + part + 1)
                                if u >= 2:
                                    act.wait_ge(S["pv0_done"], i * (U - 1) + u - 1)
                                nc.scalar.copy(e0_t[u % 2][:, 4 * part:4 * part + 4, :],
                                               banks[4 + part].rearrange("p (c t) -> p c t", c=4)).then_inc(S["et_ready"], 1)
                        wait("o0t_done")
                        nc.scalar.copy(o0_t[:], banks[1]).then_inc(S["o0t_ready"], 1)
                        wait("q2_done")
                        nc.scalar.mul(q_halves[:, 0, :], banks[7], float(C) ** -0.5).then_inc(S["q_high"], 1)
                        wait("q_low")
                        q4 = q_split[:].rearrange("p (i b) s (h t) -> p i b s h t", b=2 * U, h=4)
                        for half in range(2):
                            for h in range(4):
                                last = nc.scalar.activation(q4[:, i, :, half, h, :],
                                                            q_halves[:, half, :].rearrange("p (b t) -> p b t", t=TP)[:, :, 0:T],
                                                            ACT.Identity, scale=own_in_group[:, h:h + 1])
                        last.then_inc(S["q_out"], 1)

                @block.gpsimd
                def _(pool):
                    with pool.Fori(0, NIT) as i:
                        wait = waiter1(pool, i)
                        for u in range(U):
                            wait("s0_max", u + 1)
                            nc.gpsimd.tensor_tensor(s0[u][:], s0[u][:], s_max[:, u, :].unsqueeze(2).broadcast_to([128, H0, TP]),
                                                    ALU.subtract).then_inc(S["s0_ready"], 1)

                @block.vector
                def _(ve):
                    with ve.Fori(0, NIT) as i:
                        wait = waiter1(ve, i)
                        link, ends = chain(ve, dve1, i * NL, NL)
                        x4 = x_all[:].rearrange("p (i u) c -> p i u c", u=U)[:, i, :, :]

                        def layernorm(out, x, done):
                            for u in range(U):
                                ins = nc.vector.bn_stats(stats[:, u, :], x[:, u, :])
                            link(ins)
                            alone(ve)
                            for u in range(U):
                                ins = nc.vector.bn_aggr(meanvar[:, u, :], stats[:, u, :])
                            link(ins)
                            rsqrt(ve, link, rstd[:], meanvar[:, :, 1], newton[:], EPS0)
                            for u in range(U):
                                ins = nc.vector.tensor_scalar(out[:, u, :], x[:, u, :], meanvar[:, u, 0:1], rstd[:, u:u + 1],
                                                              ALU.subtract, ALU.mult)
                            ins.then_inc(S[done], 1)

                        layernorm(z, x4, "z_ready")
                        wait("xn3_ready")
                        nc.vector.tensor_scalar(xn1[:], banks[0], cols[:, 0:1], cols[:, 1:2], ALU.mult,
                                                ALU.add).then_inc(S["xn1_ready"], 1)
                        wait("qk_done")

                        def widen(u):
                            if u >= 2:
                                wait("s0_done", u - 1)
                            for b2 in range(2):
                                ins = nc.vector.tensor_tensor(
                                    k_wide[u % 2][:, b2, :, :],
                                    banks[2][:, 128 * u + 64 * b2:128 * u + 64 * b2 + 64].unsqueeze(1).broadcast_to([128, H0, TP]),
                                    own_head.unsqueeze(2).broadcast_to([128, H0, TP]), ALU.mult)
                            ins.then_inc(S["k_ready"], 1)
                        widen(0)
                        widen(1)
                        wait("v_done")
                        nc.vector.tensor_tensor(v_wide[:].rearrange("p n c h d -> p (n c) h d"),
                                                ps_d[:, :].rearrange("p (n h d) -> p n h d", h=2, d=D0),
                                                own_half.unsqueeze(1).unsqueeze(3).broadcast_to([128, 16 * U, 2, D0]),
                                                ALU.mult).then_inc(S["v_ready"], 1)
                        widen(2)
                        widen(3)
                        for u in range(U):
                            wait("s0_done", u + 1)
                            link(nc.vector.tensor_tensor(s0[u][:], (ps_a, ps_c)[u % 2][:, :].rearrange("p (h s) -> p h s", h=H0),
                                                         mask0[:].rearrange("p (i u) s -> p i u s", u=U)[:, i, u, :].unsqueeze(1).broadcast_to([128, H0, TP]), ALU.add))
                            nc.vector.reduce_max(s_max[:, u, :], s0[u][:], AX.X).then_inc(S["s0_max"], 1)
                        for u in range(U):
                            wait("e0_ready", u + 1)
                            ins = nc.vector.reduce_sum(s_sum[:, u, :], s0[u][:], AX.X)
                        link(ins)
                        link(nc.vector.reciprocal(s_sum[:], s_sum[:]))
                        wait("o0_done")
                        nc.vector.tensor_tensor(o0[:].rearrange("p (n d) -> p n d", d=D0),
                                                banks[0].rearrange("p (n d) -> p n d", d=D0),
                                                s_sum[:].rearrange("p u h -> p (u h)").unsqueeze(2).broadcast_to([128, U * H0, D0]),
                                                ALU.mult).then_inc(S["o0_ready"], 1)
                        link(nc.vector.tensor_tensor(r1[:], x4, rows0[:, 0, :].unsqueeze(1).broadcast_to([128, U, C]), ALU.add))
                        wait("sa_done")
                        link(nc.vector.tensor_tensor(r1[:], banks[2].rearrange("p (u c) -> p u c", u=U), r1[:], ALU.add))
                        layernorm(z2, r1, "z2_ready")
                        ve.wait_ge(S["z2_ready"], i + 1)
                        link(nc.vector.tensor_tensor(r1[:], r1[:], b_rest[:].unsqueeze(1).broadcast_to([128, U, C]), ALU.add))
                        wait("down_done")
                        link(nc.vector.tensor_tensor(x4, banks[6].rearrange("p (u c) -> p u c", u=U), r1[:], ALU.add))
                        wait("z2t_done")
                        nc.vector.tensor_scalar(xq[:], banks[3], cols[:, 2:3], cols[:, 3:4], ALU.mult,
                                                ALU.add).then_inc(S["xq_ready"], 1)
                        wait("q_high")
                        nc.vector.scalar_tensor_tensor(q_halves[:, 1, :], banks[7], float(C) ** -0.5, q_halves[:, 0, :],
                                                       ALU.mult, ALU.subtract).then_inc(S["q_low"], 1)
                        ve.wait_ge(S["q_low"], i + 1)
                        ends()

        with ExitStack() as p2:
            def sb2(name, shape, dt=F32):
                return p2.enter_context(nc.sbuf_tensor(name + "_sb", shape, dt))
            GROUPS, GN = 4, 4 * T
            ROWS = 96
            W = H0 * T
            context = [sb2(f"context{r}", [KP, KT, C]) for r in range(3)]
            keys = [sb2(f"keys{r}", [ROWS + 2, GROUPS, J], F16) for r in range(3)]
            queries = [sb2(f"queries{r}", [ROWS + 2, W], F16) for r in range(3)]
            values = [sb2(f"values{r}", [KP, KT, 8, 32]) for r in range(3)]
            xs_t = sb2("xs_t", [128, J])
            k_split = sb2("k_split", [128, 2, J], F16)
            best = sb2("best", [KP, W])
            probs = [sb2(f"probs{r}", [KP, W]) for r in range(2)]
            neg_max = sb2("neg_max", [128, 7])
            shift = sb2("shift", [7, 2, 128], F16)
            o_wide = sb2("o_wide", [128, 4 * T])
            o_rec = sb2("o_rec", [T, 16])
            o_rows = sb2("o_rows", [T, C])
            st = sb2("st", [KP, KT, 6])
            ln = sb2("ln", [KP, 6, KT])
            ones = sb2("ones", [KP, 1])
            per = dict(context_in=16, pool_done=1, pooled=1, stats_ready=1, z_ready=3, t_done=3, xs_ready=3,
                       k_done=3, khigh_ready=3, klow_ready=3, keys_in=192, v_done=3, values_ready=3,
                       queries_in=192, scan_done=12, best_ready=12, best_t_done=2, neg_ready=2, neg_t_done=1,
                       shift_ready=1, shift_in=32, scores_done=12, probs_ready=12, pv_done=12, o_read=1,
                       o_t_done=1, o_rows_ready=1, o_rows_t_done=1, on_ready=1)
            Q = {n: [sem(f"cross_{n}{r}") for r in range(3)] if n.endswith("_in") else sem("cross_" + n) for n in per}
            cleared = sem("cleared")
            ln_chain = sem("ln_chain")
            o_chain = sem("o_chain")
            m_chain = sem("m_chain")
            NLN = 7 + 11
            ring = [ps_c[:, 0:512], ps_c[:, 512:1024]]
            o_bank = ps_d[:, 0:4 * T]
            misc = ps_d[:, 512:1024]

            def halves(ps):
                return ps.rearrange("p (e n) -> p e n", e=2)[:, :, 0:448]

            def steps(eng, emit):
                def one(b, r, turn):
                    emit(b, r, lambda d, b=b: not isinstance(b, int) or 0 <= b + d < B, turn)
                for b in range(-4, 1):
                    one(b, b % 3, lambda d, b=b: (b + d) // 3)
                with eng.Fori(0, 9) as i:
                    for r in range(1, 4):
                        one(i * 3 + r, r % 3, lambda d, r=r: i + (r + d) // 3)
                for b in range(28, B + 1):
                    one(b, b % 3, lambda d, b=b: (b + d) // 3)

            def landed(n, d, r):
                return Q[n][(r + d) % 3]

            def waiter(eng, b, r, turn):
                def wait(n, d, k):
                    if n.endswith("_in"):
                        if k == 0:
                            d, k = d - 1, per[n]
                            if isinstance(b, int) and b + d < 0:
                                return
                        eng.wait_ge(landed(n, d, r), turn(d) * per[n] + k)
                        return
                    value = (b + d) * per[n] + k
                    assert isinstance(b, int) or (1 + d) * per[n] + k > 0, "the loop starts at batch 1"
                    if not isinstance(value, int) or value > 0:
                        eng.wait_ge(Q[n], value)
                return wait

            with nc.Block() as block:
                @block.gpsimd
                def _(pool):
                    fills = [(ones[:], 1.0), (on_all[:], 0.0)]
                    for r in range(3):
                        fills += [(keys[r][ROWS:ROWS + 2, :, :], 1.0), (values[r][:, :, :, 17:32], 0.0),
                                  (values[r][:, :, :, 16:17], 1.0)]
                    for n, (where, value) in enumerate(fills):
                        nc.gpsimd.memset(where, value).then_inc(cleared, 1)
                        pool.wait_ge(cleared, n + 1)

                    def emit(b, r, has, turn):
                        wait = waiter(pool, b, r, turn)
                        if has(3):
                            wait("stats_ready", 3, 1)
                            wait("pool_done", 3, 1)
                            alone(pool)
                            for k in range(KT):
                                tile = context[r][:, k, :]
                                ins = nc.gpsimd.tensor_scalar(tile, tile, ln[:, 4, k:k + 1], ln[:, 5, k:k + 1],
                                                              ALU.mult, ALU.add)
                                if k % 4 == 3:
                                    ins.then_inc(Q["z_ready"], 1)
                    steps(pool, emit)

                @block.sync
                def _(sp):
                    def emit(b, r, has, turn):
                        wait = waiter(sp, b, r, turn)
                        r1, r2 = (r + 1) % 3, (r + 2) % 3
                        if has(4):
                            wait("t_done", 1, 3)
                            sp.dma_start(context[r1][:], dram["ctx"][b + 4].rearrange("(p k) c -> p k c", k=KT)
                                         ).then_inc(landed("context_in", 4, r), 16)
                        if has(2):
                            wait("scores_done", 0, 0)
                            for block_, half in ((0, 0), (1, 1), (2, 0)):
                                for g in range(GROUPS):
                                    sp.dma_start(queries[r2][32 * block_:32 * block_ + 32, GN * g:GN * g + GN],
                                                 q_split[32 * g:32 * g + 32, b + 2, half, :]).then_inc(landed("queries_in", 2, r), 16)
                            wait("khigh_ready", 2, 3)
                            for block_, half in ((0, 0), (1, 0), (2, 1)):
                                if half:
                                    wait("klow_ready", 2, 3)
                                for g in range(GROUPS):
                                    sp.dma_start(keys[r2][32 * block_:32 * block_ + 32, g, :],
                                                 k_split[32 * g:32 * g + 32, half, :]).then_inc(landed("keys_in", 2, r), 16)
                        if has(1):
                            wait("shift_ready", 1, 1)
                            for half in range(2):
                                sp.dma_start(queries[r1][ROWS + half:ROWS + half + 1, :],
                                             shift[:, half, :]).then_inc(landed("shift_in", 1, r), 16)
                    steps(sp, emit)

                @block.tensor
                def _(pe):
                    pe.wait_ge(cleared, 11)

                    def pv(b, d, k, r, wait):
                        wait("probs_ready", d, k + 1)
                        if k == 0:
                            wait("values_ready", d, 3)
                            wait("o_read", d, 0)
                        for g in range(8):
                            last = nc.tensor.matmul(o_bank[32 * (g % 4):32 * (g % 4) + 32, 112 * (g // 4):112 * (g // 4) + 112],
                                                    values[r][:, k, g, :], probs[k % 2][:, 112 * g:112 * g + 112],
                                                    start=(k == 0 and g < 4), stop=(k == KT - 1),
                                                    tile_position=(0, 32 * (g % 4)), skip_group_check=True)
                        last.then_inc(Q["pv_done"], 1)

                    def scores(out, r, k, rows):
                        for g in range(GROUPS):
                            col = 512 * (g // 2) + GN * (g % 2)
                            last = nc.tensor.matmul(out[0:KP, col:col + GN], keys[r][0:rows, g, KP * k:KP * k + KP],
                                                    queries[r][0:rows, GN * g:GN * g + GN], start=True, stop=True)
                        return last

                    def emit(b, r, has, turn):
                        wait = waiter(pe, b, r, turn)
                        r1, r2 = (r + 1) % 3, (r + 2) % 3

                        def scan(k):
                            if k == 0:
                                wait("keys_in", 1, 192)
                                wait("queries_in", 1, 192)
                            wait("best_ready", 1, k)
                            scores(ps_b, r1, k, ROWS).then_inc(Q["scan_done"], 1)

                        for s in range(KT):
                            if has(0):
                                if s == 0:
                                    wait("shift_in", 0, 32)
                                wait("probs_ready", 0, s)
                                scores(ps_a, r, s, ROWS + 2).then_inc(Q["scores_done"], 1)
                            if has(1) and s < 6:
                                scan(2 * s)
                            if s == 0 and has(-1):
                                pv(b, -1, KT - 1, r2, wait)
                            if s > 0 and has(0):
                                pv(b, 0, s - 1, r, wait)
                            if has(1) and s < 6:
                                scan(2 * s + 1)
                            if has(2) and s < 3:
                                wait("z_ready", 2, s + 1)
                                if s == 0:
                                    wait("values_ready", 1, 3)
                                elif s == 1:
                                    wait("pooled", 2, 1)
                                else:
                                    wait("xs_ready", 2, 1)
                                for k in range(4):
                                    last = nc.tensor.transpose(ring[s % 2][:, KP * k:KP * k + KP],
                                                               context[r2][:, 4 * s + k, :], ident[0:KP, 0:KP])
                                last.then_inc(Q["t_done"], 1)
                            if has(2) and 3 <= s < 6:
                                u = s - 3
                                wait("xs_ready", 2, 2 if u == 0 else 3)
                                if u == 2:
                                    wait("klow_ready", 2, 1)
                                nc.tensor.matmul(ring[s % 2][:, 0:500], w_kv[:, 0:128], xs_t[:, 500 * u:500 * u + 500],
                                                 start=True, stop=True).then_inc(Q["k_done"], 1)
                            if has(2) and 6 <= s < 9:
                                u = s - 6
                                if u < 2:
                                    wait("klow_ready", 2, u + 2)
                                else:
                                    wait("values_ready", 2, 1)
                                for k in range(4):
                                    last = nc.tensor.matmul(ring[s % 2][0:KP, 128 * k:128 * k + 128],
                                                            xs_t[:, 500 * u + KP * k:500 * u + KP * k + KP],
                                                            w_kv[:, 128:256], start=True, stop=True)
                                last.then_inc(Q["v_done"], 1)
                            if has(3) and s == 9:
                                wait("context_in", 3, 16)
                                wait("values_ready", 2, 2)
                                for k in range(KT):
                                    last = nc.tensor.matmul(ring[1][:, 0:1], context[r][:, k, :], ones[:],
                                                            start=(k == 0), stop=(k == KT - 1))
                                last.then_inc(Q["pool_done"], 1)
                            if has(-1) and s == 2:
                                wait("o_read", -1, 1)
                                if has(0):
                                    wait("shift_ready", 0, 1)
                                else:
                                    wait("on_ready", -2, 1)
                                alone(pe)
                                for e in range(4):
                                    last = nc.tensor.transpose(misc[0:T, 128 * e:128 * e + 128],
                                                               o_wide[:, T * e:T * e + T], ident)
                                last.then_inc(Q["o_t_done"], 1)
                            if has(-1) and s == 4:
                                wait("o_rows_ready", -1, 1)
                                alone(pe)
                                nc.tensor.transpose(misc[:, 0:T], o_rows[:], ident[0:T, 0:T]).then_inc(Q["o_rows_t_done"], 1)
                            if has(1) and s in (6, 7):
                                if s == 6:
                                    wait("best_ready", 1, KT)
                                    wait("on_ready", -1, 1)
                                else:
                                    wait("neg_ready", 1, 1)
                                chunks = range(0, 4) if s == 6 else range(4, 7)
                                for n, c in enumerate(chunks):
                                    last = nc.tensor.transpose(misc[:, KP * n:KP * n + KP],
                                                               best[:, 128 * c:128 * c + 128], ident[0:KP, 0:KP])
                                last.then_inc(Q["best_t_done"], 1)
                            if has(1) and s == 8:
                                wait("neg_ready", 1, 2)
                                nc.tensor.transpose(misc[0:7, 0:128], neg_max[:], ident).then_inc(Q["neg_t_done"], 1)
                    steps(pe, emit)

                @block.scalar
                def _(act):
                    act.wait_ge(cleared, 11)

                    def emit(b, r, has, turn):
                        wait = waiter(act, b, r, turn)
                        r1, r2 = (r + 1) % 3, (r + 2) % 3
                        for s in range(KT):
                            if has(0):
                                wait("scores_done", 0, s + 1)
                                wait("pv_done", 0, s - 1)
                                nc.scalar.activation(probs[s % 2][:].rearrange("p (e n) -> p e n", e=2),
                                                     halves(ps_a[0:KP, :]), ACT.Exp).then_inc(Q["probs_ready"], 1)
                            if s == 0 and has(-1):
                                wait("pv_done", -1, KT)
                                nc.scalar.copy(o_wide[:], o_bank).then_inc(Q["o_read"], 1)
                            if has(2) and s < 3:
                                wait("t_done", 2, s + 1)
                                wait("v_done", 2, 0)
                                nc.scalar.activation(xs_t[:, 500 * s:500 * s + 500], ring[s % 2][:, 0:500], ACT.Identity,
                                                     bias=cols[:, 3:4], scale=cols[:, 2:3]).then_inc(Q["xs_ready"], 1)
                            if has(2) and 3 <= s < 6:
                                u = s - 3
                                wait("k_done", 2, u + 1)
                                wait("keys_in", 2, 0)
                                nc.scalar.copy(k_split[:, 0, 500 * u:500 * u + 500], ring[s % 2][:, 0:500]
                                               ).then_inc(Q["khigh_ready"], 1)
                            if has(2) and 6 <= s < 9:
                                u = s - 6
                                wait("v_done", 2, u + 1)
                                wait("pv_done", -1, KT)
                                nc.scalar.copy(values[r2][:, 4 * u:4 * u + 4, :, 0:16],
                                               ring[s % 2][0:KP, :].rearrange("p (k g n) -> p k g n", k=4, g=8)
                                               ).then_inc(Q["values_ready"], 1)
                            if has(3) and s == 9:
                                wait("pool_done", 3, 1)
                                nc.scalar.copy(pool_all[:, bass.ds(b + 3, 1)] if not isinstance(b, int) else
                                               pool_all[:, b + 3:b + 4], ring[1][:, 0:1]).then_inc(Q["pooled"], 1)
                    steps(act, emit)

                @block.vector
                def _(ve):
                    ve.wait_ge(cleared, 11)

                    def emit(b, r, has, turn):
                        wait = waiter(ve, b, r, turn)
                        ln_link, ln_ends = chain(ve, ln_chain, (b + 3) * NLN, NLN)
                        o_link, _ = chain(ve, o_chain, b - 1, 1)
                        m_link, _ = chain(ve, m_chain, b + 1, 1)

                        def keep_best(k):
                            wait("scan_done", 1, k + 1)
                            both = best[:].rearrange("p (e n) -> p e n", e=2)
                            if k == 0:
                                wait("best_t_done", 1, 0)
                                ins = nc.vector.tensor_copy(both, halves(ps_b[0:KP, :]))
                            else:
                                wait("best_ready", 1, k)
                                ins = nc.vector.tensor_tensor(both, halves(ps_b[0:KP, :]), both, ALU.max)
                            ins.then_inc(Q["best_ready"], 1)

                        for s in range(KT):
                            if has(1) and s < 6:
                                keep_best(2 * s)
                                keep_best(2 * s + 1)
                            if has(-1) and s == 2:
                                wait("o_t_done", -1, 1)
                                t4 = misc[0:T, :].rearrange("p (e h q r) -> p e h q r", e=2, h=2, q=4)
                                rec = o_rec[:].rearrange("p (e h q) -> p e h q", e=2, h=2)
                                o_link(nc.vector.reciprocal(o_rec[:], misc[0:T, :].rearrange("p (n r) -> p n r", r=32)[:, :, 16]))
                                rows = o_rows[:].rearrange("p (e q h d) -> p e q h d", e=2, q=4, h=2)
                                for h in range(2):
                                    ins = nc.vector.tensor_tensor(rows[:, :, :, h, :], t4[:, :, h, :, 8 * h:8 * h + 8],
                                                                  rec[:, :, h, :].unsqueeze(3).broadcast_to([T, 2, 4, 8]),
                                                                  ALU.mult)
                                ins.then_inc(Q["o_rows_ready"], 1)
                            if has(-1) and s == 4:
                                wait("o_rows_t_done", -1, 1)
                                nc.vector.tensor_copy(on_all[:, b - 1, 0:T], misc[:, 0:T]).then_inc(Q["on_ready"], 1)
                            if has(2) and 3 <= s < 6:
                                u = s - 3
                                wait("khigh_ready", 2, u + 1)
                                wait("keys_in", 2, 0)
                                nc.vector.tensor_tensor(k_split[:, 1, 500 * u:500 * u + 500], ring[s % 2][:, 0:500],
                                                        k_split[:, 0, 500 * u:500 * u + 500], ALU.subtract
                                                        ).then_inc(Q["klow_ready"], 1)
                            if has(1) and s in (6, 7):
                                wait("best_t_done", 1, s - 5)
                                n = 4 if s == 6 else 3
                                nc.vector.tensor_reduce(neg_max[:, 4 * (s - 6):4 * (s - 6) + n],
                                                        misc[:, 0:KP * n].rearrange("p (c j) -> p c j", c=n),
                                                        axis=AX.X, op=ALU.max, negate=True).then_inc(Q["neg_ready"], 1)
                            if has(1) and s == 8:
                                wait("neg_t_done", 1, 1)
                                wait("shift_in", 1, 0)
                                m_link(nc.vector.tensor_copy(shift[:, 0, :], misc[0:7, 0:128]))
                                nc.vector.tensor_tensor(shift[:, 1, :], misc[0:7, 0:128], shift[:, 0, :],
                                                        ALU.subtract).then_inc(Q["shift_ready"], 1)
                            if has(3) and 5 <= s < 9:
                                if s == 5:
                                    wait("context_in", 3, 16)
                                for k in range(3 * (s - 5), 3 * (s - 5) + 3):
                                    ins = nc.vector.bn_stats(st[:, k, :], context[r][:, k, :])
                                if s == 8:
                                    ln_link(ins)
                            if has(3) and s == 9:
                                mu, var, rstd, tmp = ln[:, 0, :], ln[:, 1, :], ln[:, 2, :], ln[:, 3, :]
                                wait("z_ready", 3, 0)
                                ln_link(nc.vector.tensor_tensor(mu, st[:, :, 1], st[:, :, 4], ALU.add))
                                ln_link(nc.vector.tensor_tensor(tmp, st[:, :, 1], st[:, :, 4], ALU.subtract))
                                ln_link(nc.vector.tensor_tensor(var, st[:, :, 2], st[:, :, 5], ALU.add))
                                ln_link(nc.vector.tensor_tensor(tmp, tmp, tmp, ALU.mult))
                                ln_link(nc.vector.tensor_scalar(tmp, tmp, 0.25, None, ALU.mult))
                                ln_link(nc.vector.scalar_tensor_tensor(var, var, 1.0 / C, tmp, ALU.mult, ALU.add))
                                rsqrt(ve, ln_link, ln[:, 4, :], var, tmp, EPS0)
                                nc.vector.scalar_tensor_tensor(ln[:, 5, :], mu, -0.5, ln[:, 4, :], ALU.mult,
                                                               ALU.mult).then_inc(Q["stats_ready"], 1)
                                ln_ends()
                    steps(ve, emit)

        early.close()

        with ExitStack() as p3:
            def sb3(name, shape, dt=F32):
                return p3.enter_context(nc.sbuf_tensor(name + "_sb", shape, dt))
            NJ, NB = 8, 2 * U
            NIT = NPAIR // U
            w_qk1 = sb3("w_qk1", [128, 2, 1024])
            w_turn = sb3("w_turn", [128, 2, 1024])
            w_v1 = sb3("w_v1", [128, 1024])
            w_out1 = sb3("w_out1", [128, NJ, C])
            w_mem = sb3("w_mem", [128, C])
            w_up1 = sb3("w_up1", [128, 6, 128])
            w_down1 = sb3("w_down1", [128, 3, C])
            cols1 = sb3("cols1", [128, 3 + 6])
            neg_gate_b = sb3("neg_gate_b", [128, 3])
            row_b1 = sb3("row_b1", [128, C])
            persist_v = sb3("persist_v", [PREFIX + TP, 1024])
            mem_rows = sb3("mem_rows", [B, C])
            mem_st = sb3("mem_st", [B, 12])
            mem_cols = sb3("mem_cols", [128, B])
            mem_t = sb3("mem_t", [128, B])
            mem_k = sb3("mem_k", [128, NJ, B])
            x0 = sb3("x0", [128, U, C])
            on_now = sb3("on_now", [128, U * 128])
            st1 = sb3("st1", [128, U, 6])
            mv1 = sb3("mv1", [128, U, 2])
            ms1 = sb3("ms1", [128, 3, U])
            normed = sb3("normed", [128, U, C])
            xm = sb3("xm", [128, NB, NK1])
            turn_a = [sb3(f"turn_a{n}", [128, NB, TP]) for n in range(2)]
            turn_b = [sb3(f"turn_b{n}", [128, NB, TP]) for n in range(2)]
            q1 = sb3("q1", [128, NJ, U * 128])
            k1 = sb3("k1", [128, NJ, NB, NK1])
            v1 = sb3("v1", [NK1, NB, 1024])
            s1 = [sb3(f"s1_{u}", [128, 16, NK1]) for u in range(U)]
            s1_max = sb3("s1_max", [128, U, 16])
            s1_sum = sb3("s1_sum", [128, U, 16])
            e1_t = [sb3(f"e1_t{n}", [NK1, 16, 128]) for n in range(2)]
            o1_t = [sb3(f"o1_t{n}", [128, NJ, 128]) for n in range(2)]
            h_t = sb3("h_t", [128, U * 128])
            gate_e = sb3("gate_e", [128, 3, U * 128])
            up1 = sb3("up1", [128, 3, U * 128])
            y = sb3("y", [128, U, C])
            per3 = dict(turn_done=16, turn_read=16, rotated=16, v_done=NB, v_copied=NB, v_ready=NB, s_done=2 * U,
                        s_read=2 * U, s_max=U, s_ready=U, e_ready=U, sum_ready=U, e_normal=U, et_done=2 * U,
                        et_ready=2 * U, o_done=2 * U, o_ready=2 * U, up_done=3, gate_exp=3, up_ready=3,
                        out_done=U)
            names = ["on_now", "projx_done", "xn_ready", "xnt_done", "xnt_ready", "mem_ready",
                     "hn_ready", "ht_done", "ht_ready", "down_done", "y_ready", *per3]
            R = {n: sem("segment_" + n) for n in names}
            stored = sem("stored")
            loaded1 = sem("loaded1")
            dve3 = sem("dve3")
            mem_pe = sem("mem_pe")
            mem_dve = sem("mem_dve")
            ND3 = 47
            n_loads1 = 16 * (10 + NB)

            def waiter3(eng, i):
                def wait(n, k=1):
                    eng.wait_ge(R[n], i * per3.get(n, 1) + k)
                return wait

            with nc.Block() as block:
                @block.sync
                def _(sp):
                    def load(dst, src):
                        sp.dma_start(dst, src).then_inc(loaded1, 16)
                    load(w_mem[:], dram["w_mem"])
                    load(cols1[:], dram["cols1"])
                    load(w_qk1[:], dram["w_qkv1"][:, 0:2048].rearrange("p (a n) -> p a n", a=2))
                    load(w_turn[:], dram["w_turn"])
                    load(w_v1[:], dram["w_qkv1"][:, 2048:3072])
                    load(w_out1[:], dram["w_out1"].rearrange("(j p) n -> p j n", p=128))
                    load(w_up1[:], dram["w_up1"])
                    load(w_down1[:], dram["w_down1"].rearrange("(j p) n -> p j n", p=128))
                    load(row_b1[:], dram["row_b1"].broadcast_to([128, C]))
                    sp.wait_ge(mem_dve, 1)
                    load(persist_v[TP + NM:NK1, :], dram["persist_v"])
                    for b2 in range(NB):
                        load(k1[:, :, b2, TP + NM:NK1], dram["persist_k"])
                    sp.wait_ge(loaded1, n_loads1)
                    sp.sem_inc(stored, 1)
                    with sp.Fori(0, NIT) as i:
                        sp.wait_ge(R["y_ready"], i + 1)
                        for b2 in range(2):
                            sp.dma_start(dram["out"].rearrange("(i u b) t c -> i b t u c", b=2, u=U)[i, b2],
                                         y[64 * b2:64 * b2 + T, :, :]).then_inc(stored, 16)
                    sp.wait_ge(stored, 32 * NIT + 1)

                @block.gpsimd
                def _(pool):
                    with pool.Fori(0, NIT) as i:
                        wait = waiter3(pool, i)
                        for n in range(16):
                            wait("turn_read", n + 1)
                            if n < NJ:
                                dst = q1[:, n, :].rearrange("p (b t) -> p b t", t=TP)
                            else:
                                dst = k1[:, n - NJ, :, 0:TP]
                            nc.gpsimd.tensor_tensor(dst, turn_a[n % 2][:], turn_b[n % 2][:], ALU.add).then_inc(R["rotated"], 1)
                        for u in range(U + 1):
                            if u < U:
                                wait("s_max", u + 1)
                                nc.gpsimd.tensor_tensor(s1[u][:], s1[u][:], s1_max[:, u, :].unsqueeze(2).broadcast_to([128, 16, NK1]),
                                                        ALU.subtract).then_inc(R["s_ready"], 1)
                            if u > 0:
                                wait("sum_ready", u)
                                nc.gpsimd.tensor_tensor(s1[u - 1][:], s1[u - 1][:],
                                                        s1_sum[:, u - 1, :].unsqueeze(2).broadcast_to([128, 16, NK1]),
                                                        ALU.mult).then_inc(R["e_normal"], 1)

                @block.tensor
                def _(pe):
                    nc.tensor.transpose(ps_a[0:B, 0:128], pool_all[:], ident).then_inc(mem_pe, 1)
                    pe.wait_ge(mem_dve, 2)
                    nc.tensor.transpose(ps_a[:, 512:512 + B], mem_rows[:], ident[0:B, 0:B]).then_inc(mem_pe, 1)
                    pe.wait_ge(mem_dve, 3)
                    nc.tensor.matmul(ps_b[:, 0:B], w_mem[:], mem_cols[:], start=True, stop=True).then_inc(mem_pe, 1)
                    pe.wait_ge(mem_dve, 4)
                    for j in range(NJ):
                        last = nc.tensor.matmul(ps_b[:, 512 + B * j:512 + B * j + B], w_qk1[:, 1, 128 * j:128 * j + 128],
                                                mem_t[:], start=True, stop=True)
                    last.then_inc(mem_pe, 1)
                    pe.wait_ge(mem_dve, 5)
                    with pe.Fori(0, NIT) as i:
                        wait = waiter3(pe, i)
                        wait("on_now")
                        for u in range(U):
                            last = nc.tensor.matmul(banks[0][:, 128 * u:128 * u + 128], on_now[:, 128 * u:128 * u + 128],
                                                    w_projx[:], start=True, stop=True)
                        last.then_inc(R["projx_done"], 1)
                        wait("xn_ready")
                        for u in range(U):
                            last = nc.tensor.transpose(banks[1][:, 128 * u:128 * u + 128], normed[:, u, :], ident)
                        last.then_inc(R["xnt_done"], 1)
                        wait("xnt_ready")

                        def values1(b):
                            if b >= 2:
                                wait("v_ready", b - 1)
                            ps = (ps_c, ps_d)[b % 2]
                            for half in range(2):
                                last = nc.tensor.matmul(ps[0:NK1, 512 * half:512 * half + 512], xm[:, b, :],
                                                        w_v1[:, 512 * half:512 * half + 512], start=True, stop=True)
                            last.then_inc(R["v_done"], 1)

                        for n in range(16):
                            ps = (ps_a, ps_b)[n % 2]
                            if n >= 2:
                                wait("turn_read", n - 1)
                            cut = slice(128 * (n % NJ), 128 * (n % NJ) + 128)
                            rows = xm[:, :, 0:TP]
                            nc.tensor.matmul(ps[:, 0:512], w_qk1[:, n // NJ, cut], rows, start=True, stop=True)
                            nc.tensor.matmul(ps[:, 512:1024], w_turn[:, n // NJ, cut], rows, start=True, stop=True
                                             ).then_inc(R["turn_done"], 1)
                            if n == 1:
                                wait("mem_ready")
                            if n % 2 == 1:
                                values1(n // 2)
                        wait("rotated", 16)
                        for u in range(U):
                            for half in range(2):
                                if u == 0:
                                    wait("turn_read", 15 + half)
                                else:
                                    wait("s_read", 2 * u + half - 1)
                                if u == 0 and half == 0:
                                    alone(pe)
                                if u > 0:
                                    alone(pe)
                                elif half == 1:
                                    alone(pe)
                                ps = (ps_a, ps_b)[half]
                                for j4 in range(4):
                                    j = 4 * half + j4
                                    for r in range(2):
                                        for b2 in range(2):
                                            last = nc.tensor.matmul(ps[64 * b2:64 * b2 + 64, 512 * r + NK1 * j4:512 * r + NK1 * j4 + NK1],
                                                                    q1[64 * r:64 * r + 64, j, 128 * u + 64 * b2:128 * u + 64 * b2 + 64],
                                                                    k1[64 * r:64 * r + 64, j, 2 * u + b2, :], start=True, stop=True)
                                last.then_inc(R["s_done"], 1)

                        def weighted(u):
                            ps = (ps_c, ps_d)[u % 2]
                            if u == 0:
                                wait("v_ready", NB)
                            for half in range(2):
                                wait("et_ready", 2 * u + half + 1)
                                if u >= 2:
                                    wait("o_ready", 2 * u - 3 + half)
                                for r in range(2):
                                    for j4 in range(4):
                                        j = 4 * half + j4
                                        h = 2 * j + r
                                        for b2 in range(2):
                                            last = nc.tensor.matmul(ps[64 * r:64 * r + 64, 128 * j + 64 * b2:128 * j + 64 * b2 + 64],
                                                                    v1[:, 2 * u + b2, D1 * h:D1 * h + D1],
                                                                    e1_t[u % 2][:, 8 * half + 4 * r + j4, 64 * b2:64 * b2 + 64],
                                                                    start=True, stop=True)
                                last.then_inc(R["o_done"], 1)

                        for u in range(U):
                            wait("e_normal", u + 1)
                            for half in range(2):
                                if u == 0:
                                    wait("s_read", 2 * U)
                                else:
                                    wait("et_ready", 2 * u - 1 + half)
                                ps = (ps_a, ps_b)[half]
                                for n in range(8):
                                    last = nc.tensor.transpose(ps[0:NK1, 128 * n:128 * n + 128], s1[u][:, 8 * half + n, :], ident)
                                last.then_inc(R["et_done"], 1)
                            if u > 0:
                                weighted(u - 1)
                        weighted(U - 1)
                        wait("et_ready", 2 * U)
                        for u in range(U):
                            wait("o_ready", 2 * u + 2)
                            for j in range(NJ):
                                last = nc.tensor.matmul(banks[0][:, 128 * u:128 * u + 128], o1_t[u % 2][:, j, :], w_out1[:, j, :],
                                                        start=(j == 0), stop=(j == NJ - 1))
                            last.then_inc(R["out_done"], 1)
                        wait("hn_ready")
                        for u in range(U):
                            last = nc.tensor.transpose(banks[1][:, 128 * u:128 * u + 128], normed[:, u, :], ident)
                        last.then_inc(R["ht_done"], 1)
                        wait("ht_ready")
                        for n in range(3):
                            ps = (ps_b, ps_c, ps_d)[n]
                            nc.tensor.matmul(ps[:, 0:512], w_up1[:, n, :], h_t[:], start=True, stop=True)
                            nc.tensor.matmul(ps[:, 512:1024], w_up1[:, 3 + n, :], h_t[:], start=True, stop=True
                                             ).then_inc(R["up_done"], 1)
                        wait("up_ready", 3)
                        for u in range(U):
                            for n in range(3):
                                last = nc.tensor.matmul(banks[0][:, 128 * u:128 * u + 128], up1[:, n, 128 * u:128 * u + 128],
                                                        w_down1[:, n, :], start=(n == 0), stop=(n == 2))
                        last.then_inc(R["down_done"], 1)

                @block.scalar
                def _(act):
                    with act.Fori(0, NIT) as i:
                        wait = waiter3(act, i)
                        wait("xnt_done")
                        nc.scalar.activation(xm[:, :, 0:TP], banks[1].rearrange("p (b t) -> p b t", t=TP), ACT.Identity,
                                             scale=cols1[:, 0:1]).then_inc(R["xnt_ready"], 1)
                        for b in range(NB):
                            wait("v_done", b + 1)
                            nc.scalar.copy(v1[0:TP, b, :], (ps_c, ps_d)[b % 2][0:TP, :]).then_inc(R["v_copied"], 1)
                        for u in range(U):
                            wait("s_ready", u + 1)
                            nc.scalar.activation(s1[u][:], s1[u][:], ACT.Exp, scale=float(D1) ** -0.5).then_inc(R["e_ready"], 1)
                        for u in range(U + 1):
                            for half in range(2):
                                if u < U:
                                    wait("et_done", 2 * u + half + 1)
                                    if u >= 2:
                                        wait("o_done", 2 * u - 3 + half)
                                    nc.scalar.copy(e1_t[u % 2][:, 8 * half:8 * half + 8, :],
                                                   (ps_a, ps_b)[half][0:NK1, :].rearrange("p (n t) -> p n t", n=8)).then_inc(R["et_ready"], 1)
                            for half in range(2):
                                if u > 0:
                                    v = u - 1
                                    wait("o_done", 2 * v + half + 1)
                                    if v >= 2:
                                        wait("out_done", v - 1)
                                    nc.scalar.copy(o1_t[v % 2][:, 4 * half:4 * half + 4, :],
                                                   (ps_c, ps_d)[v % 2][:, 512 * half:512 * half + 512].rearrange("p (n t) -> p n t", n=4)
                                                   ).then_inc(R["o_ready"], 1)
                        wait("ht_done")
                        nc.scalar.activation(h_t[:], banks[1], ACT.Identity, scale=cols1[:, 2:3]).then_inc(R["ht_ready"], 1)
                        for n in range(3):
                            wait("up_done", n + 1)
                            nc.scalar.activation(gate_e[:, n, :], (ps_b, ps_c, ps_d)[n][:, 512:1024], ACT.Exp,
                                                 bias=neg_gate_b[:, n:n + 1], scale=-1.0).then_inc(R["gate_exp"], 1)

                @block.vector
                def _(ve):
                    link, _ = chain(ve, sem("mem_chain"), 0, 0)
                    link(nc.vector.memset(persist_v[:], 0.0))
                    nc.vector.memset(xm[:], 0.0).then_inc(mem_dve, 1)
                    ve.wait_ge(mem_pe, 1)
                    ve.wait_ge(loaded1, n_loads1)
                    link(nc.vector.tensor_scalar(neg_gate_b[:], cols1[:, 6:9], -1.0, None, ALU.mult))
                    link(nc.vector.tensor_scalar(mem_rows[:], ps_a[0:B, 0:128], 1.0 / J, None, ALU.mult))
                    link(nc.vector.bn_stats(mem_st[:, 0:6], mem_rows[:]))
                    link(nc.vector.bn_aggr(mem_st[:, 6:8], mem_st[:, 0:6]))
                    link(nc.vector.tensor_tensor(mem_st[:, 8:9], mem_st[:, 6:7], mem_st[:, 6:7], ALU.mult))
                    link(nc.vector.tensor_tensor(mem_st[:, 8:9], mem_st[:, 8:9], mem_st[:, 7:8], ALU.add))
                    rsqrt(ve, link, mem_st[:, 9:10], mem_st[:, 8:9], mem_st[:, 10:11], EPS1)
                    nc.vector.tensor_scalar(mem_rows[:], mem_rows[:], mem_st[:, 9:10], None, ALU.mult).then_inc(mem_dve, 1)
                    ve.wait_ge(mem_pe, 2)
                    nc.vector.tensor_scalar(mem_cols[:], ps_a[:, 512:512 + B], cols1[:, 1:2], None, ALU.mult).then_inc(mem_dve, 1)
                    ve.wait_ge(mem_pe, 3)
                    nc.vector.tensor_copy(mem_t[:], ps_b[:, 0:B]).then_inc(mem_dve, 1)
                    ve.wait_ge(mem_pe, 4)
                    nc.vector.tensor_copy(mem_k[:], ps_b[:, 512:768].rearrange("p (j b) -> p j b", j=NJ)).then_inc(mem_dve, 1)
                    ve.wait_ge(mem_dve, 5)
                    with ve.Fori(0, NIT) as i:
                        wait = waiter3(ve, i)
                        link, ends = chain(ve, dve3, i * ND3, ND3)

                        def rms(x, done):
                            for u in range(U):
                                ins = nc.vector.bn_stats(st1[:, u, :], x[:, u, :])
                            link(ins)
                            alone(ve)
                            for u in range(U):
                                ins = nc.vector.bn_aggr(mv1[:, u, :], st1[:, u, :])
                            link(ins)
                            ms, rstd, tmp = ms1[:, 0, :], ms1[:, 1, :], ms1[:, 2, :]
                            link(nc.vector.tensor_tensor(ms, mv1[:, :, 0], mv1[:, :, 0], ALU.mult))
                            link(nc.vector.tensor_tensor(ms, ms, mv1[:, :, 1], ALU.add))
                            rsqrt(ve, link, rstd, ms, tmp, EPS1)
                            for u in range(U):
                                ins = nc.vector.tensor_scalar(normed[:, u, :], x[:, u, :], ms1[:, 1, u:u + 1], None, ALU.mult)
                            ins.then_inc(R[done], 1)

                        nc.vector.tensor_copy(on_now[:], on_all[:].rearrange("p (i b) t -> p i (b t)", b=NB)[:, i, :]
                                              ).then_inc(R["on_now"], 1)
                        wait("projx_done")
                        link(nc.vector.tensor_tensor(x0[:], banks[0].rearrange("p (u c) -> p u c", u=U),
                                                     x_all[:].rearrange("p (i u) c -> p i u c", u=U)[:, i, :, :], ALU.add))
                        rms(x0, "xn_ready")
                        nc.vector.tensor_copy(xm[:, :, TP:TP + NM],
                                              mem_t[:].rearrange("p (i b) -> p i b", b=NB)[:, i, :].unsqueeze(2).broadcast_to([128, NB, NM])
                                              ).then_inc(R["mem_ready"], 1)
                        link(nc.vector.tensor_copy(k1[:, :, :, TP:TP + NM],
                                                   mem_k[:].rearrange("p j (i b) -> p i j b", b=NB)[:, i, :, :].unsqueeze(3).broadcast_to([128, NJ, NB, NM])))
                        for n in range(16):
                            ps = (ps_a, ps_b)[n % 2]
                            wait("turn_done", n + 1)
                            if n >= 2:
                                wait("rotated", n - 1)
                            for dst, half, table in ((turn_a, 0, cos), (turn_b, 1, sin)):
                                ins = nc.vector.tensor_tensor(dst[n % 2][:],
                                                              ps[:, 512 * half:512 * half + 512].rearrange("p (n t) -> p n t", n=NB),
                                                              table.unsqueeze(1).broadcast_to([128, NB, TP]), ALU.mult)
                            ins.then_inc(R["turn_read"], 1)
                            if n % 2 == 1:
                                b = n // 2
                                wait("v_copied", b + 1)
                                nc.vector.tensor_tensor(v1[TP:NK1, b, :], (ps_c, ps_d)[b % 2][TP:NK1, :],
                                                        persist_v[TP:NK1, :], ALU.add).then_inc(R["v_ready"], 1)

                        def total(u):
                            wait("e_ready", u + 1)
                            link(nc.vector.reduce_sum(s1_sum[:, u, :], s1[u][:], AX.X))
                            nc.vector.reciprocal(s1_sum[:, u, :], s1_sum[:, u, :]).then_inc(R["sum_ready"], 1)
                        for u in range(U):
                            for half in range(2):
                                wait("s_done", 2 * u + half + 1)
                                nc.vector.tensor_tensor(s1[u][:, 8 * half:8 * half + 8, :].rearrange("p (r j) k -> p r j k", r=2),
                                                        (ps_a, ps_b)[half][:, :].rearrange("p (r n) -> p r n", r=2)[:, :, 0:4 * NK1].rearrange("p r (j k) -> p r j k", j=4),
                                                        causal1.unsqueeze(1).unsqueeze(1).broadcast_to([128, 2, 4, NK1]),
                                                        ALU.add).then_inc(R["s_read"], 1)
                            wait("s_read", 2 * u + 2)
                            nc.vector.reduce_max(s1_max[:, u, :], s1[u][:], AX.X).then_inc(R["s_max"], 1)
                            if u > 0:
                                total(u - 1)
                        total(U - 1)
                        wait("out_done", U)
                        link(nc.vector.tensor_tensor(x0[:], banks[0].rearrange("p (u c) -> p u c", u=U), x0[:], ALU.add))
                        rms(x0, "hn_ready")
                        for n in range(3):
                            ps = (ps_b, ps_c, ps_d)[n]
                            g, m = gate_e[:, n, :], up1[:, n, :]
                            wait("gate_exp", n + 1)
                            link(nc.vector.tensor_scalar(g, g, 1.0, None, ALU.add))
                            link(nc.vector.reciprocal(g, g))
                            link(nc.vector.scalar_tensor_tensor(m, ps[:, 512:1024], cols1[:, 6 + n:7 + n], g, ALU.add, ALU.mult))
                            nc.vector.scalar_tensor_tensor(m, ps[:, 0:512], cols1[:, 3 + n:4 + n], m, ALU.add,
                                                           ALU.mult).then_inc(R["up_ready"], 1)
                        link(nc.vector.tensor_tensor(x0[:], x0[:], row_b1[:].unsqueeze(1).broadcast_to([128, U, C]), ALU.add))
                        wait("down_done")
                        ve.wait_ge(stored, i * 32 + 1)
                        nc.vector.tensor_tensor(y[:], banks[0].rearrange("p (u c) -> p u c", u=U), x0[:], ALU.add
                                                ).then_inc(R["y_ready"], 1)
                        ve.wait_ge(R["y_ready"], i + 1)
                        ends()


def as_words(a):
    words = np.zeros(a.shape + (4,), np.uint8)
    words[..., 0] = a.view(np.uint8)
    return words.view(np.int32)[..., 0]


INPUTS = {
    "x": ("x", lambda a: a),
    "ctx": ("ctx_1024", lambda a: a),
    "mask": ("mask_BxS_bf0", lambda a: as_words(a).reshape(1, B, T)),
    "w_qkv0": ("L0_xattn_sa_wqkv", lambda a: a),
    "w_proj0": ("L0_xattn_sa_wproj", lambda a: a),
    "w_kv": ("L0_xattn_ed_wkv", lambda a: a),
    "w_q": ("L0_xattn_ed_wq", lambda a: a),
    "w_projx": ("L0_xattn_ed_wproj", lambda a: a),
    "w_up0": ("L0_xattn_ff_w1", lambda a: a),
    "w_down0": ("L0_xattn_ff_w2", lambda a: a),
    "b_up0": ("L0_xattn_ff_b1", lambda a: a.reshape(4, 128).T),
}


def layout(inputs):
    g = {k: np.asarray(v) for k, v in inputs.items()}
    out = {n: np.ascontiguousarray(f(g[k])) for n, (k, f) in INPUTS.items()}
    out["cols"] = np.ascontiguousarray(np.stack(
        [g[f"L0_xattn_ln{n}_{v}"] for n in (1, 2, 3) for v in "gb"], 1))
    out["rows0"] = np.ascontiguousarray(np.stack(
        [g["L0_xattn_sa_bproj"], g["L0_xattn_ed_bproj"], g["L0_xattn_ff_b2"]]).reshape(1, 3, C))
    w = g["L1_xattn_to_qkv_w"]
    out["w_qkv1"] = w
    out["w_turn"] = w[:, :2048].reshape(128, 2, 512, 2)[..., ::-1].reshape(128, 2, 1024)
    out["w_out1"] = g["L1_xattn_to_out_w"]
    out["w_mem"] = g["L1_xattn_to_mem_tokens_w"]
    persist = g["L1_xattn_persist_mem"]
    out["persist_k"] = persist.reshape(8, 2, NM, D1).transpose(1, 3, 0, 2).reshape(128, 8, NM)
    out["persist_v"] = persist.transpose(1, 0, 2).reshape(NM, H1 * D1)
    up = np.zeros((128, 2, DFFP), np.float32)
    up[:, :, :DFF] = g["L1_xattn_ff_w1"].reshape(128, 2, DFF)
    out["w_up1"] = up.reshape(128, 6, 128)
    up_b = np.zeros((2, DFFP), np.float32)
    up_b[:, :DFF] = g["L1_xattn_ff_b1"].reshape(2, DFF)
    down = np.zeros((DFFP, C), np.float32)
    down[:DFF] = g["L1_xattn_ff_w2"]
    out["w_down1"] = down
    norms = np.stack([g[f"L1_xattn_{n}_norm_w"] for n in ("attn", "mem_pool", "ff")], 1)
    out["cols1"] = np.concatenate([norms, up_b.reshape(6, 128).T], 1)
    out["row_b1"] = g["L1_xattn_ff_b2"].reshape(1, C)
    out["const"] = constants()
    out = {n: np.ascontiguousarray(a) for n, a in out.items()}
    return out


def kernel(**inputs):
    import concourse.bacc as bacc
    from concourse.bass_utils import run_bass_kernel_spmd

    nc = bacc.Bacc("TRN2", target_bir_lowering=False, num_devices=1)
    arrays = layout(inputs)
    dram = {n: nc.dram_tensor(f"in_{n}", a.shape, mybir.dt.from_np(a.dtype), kind="ExternalInput").ap()
            for n, a in arrays.items()}
    dram["out"] = nc.dram_tensor("out", (B, T, C), F32, kind="ExternalOutput").ap()
    program(nc, dram)
    result = run_bass_kernel_spmd(nc, [{f"in_{n}": a for n, a in arrays.items()}], core_ids=[0])
    return result.results[0]["out"]
```

```python
from contextlib import ExitStack

import numpy as np

import concourse.bass as bass
from concourse import mybir

F32 = mybir.dt.float32
F16 = mybir.dt.float16
BF16 = mybir.dt.bfloat16
I32 = mybir.dt.int32
ALU = mybir.AluOpType
ACT = mybir.ActivationFunctionType
AX = mybir.AxisListType

B, T, C = 32, 56, 128
J = 1500
H0, D0 = 16, 8
H1, D1 = 16, 64
NPAIR = B // 2
TP = 64
KT, KP = 12, 125
FF0 = 512
U = 4
DFF, DFFP = 341, 384
PREFIX, NM = 32, 16
NK1 = TP + PREFIX
EPS0, EPS1 = 1e-5, 1.1920929e-07


def constants():
    p = np.arange(128)
    ident = np.eye(128, dtype=np.float32)
    own_head = (p[:, None] // D0 == np.arange(H0)[None]).astype(np.float32)
    own_in_group = ((p[:, None] % 32) // D0 == np.arange(4)[None]).astype(np.float32)
    own_half = (p[:, None] // 64 == np.arange(2)[None]).astype(np.float32)
    t = p % TP
    s = np.arange(TP)
    later = s[None] > t[:, None]
    causal0 = np.where(later, -1e30, 0.0).astype(np.float32)
    causal1 = np.zeros((128, NK1), np.float32)
    causal1[:, :TP] = np.where(later, -1e30, 0.0)
    d = p % D1
    inv = (1.0 / 10000.0 ** (np.arange(0, D1, 2, dtype=np.float32) / D1)).astype(np.float32)
    ang = (np.arange(TP, dtype=np.float32)[None] * inv[d // 2][:, None]).astype(np.float32)
    cos = np.cos(ang).astype(np.float32)
    sin = np.sin(ang).astype(np.float32)
    sin = np.where(d[:, None] % 2 == 0, -sin, sin).astype(np.float32)
    table = np.concatenate([ident, own_head, own_in_group, own_half, causal0, causal1, cos, sin], 1)
    return np.ascontiguousarray(table.astype(np.float32))


CONST_WIDTH = 128 + 16 + 4 + 2 + 64 + NK1 + 64 + 64


def program(nc, dram):
    ctx = ExitStack()
    with ctx:
        def sb(name, shape, dt=F32):
            return ctx.enter_context(nc.sbuf_tensor(name + "_sb", shape, dt))

        def sem(name):
            return ctx.enter_context(nc.semaphore(name))

        ps_a = ctx.enter_context(nc.psum_tensor("ps_a", [128, 1024], F32))
        ps_b = ctx.enter_context(nc.psum_tensor("ps_b", [128, 1024], F32))
        ps_c = ctx.enter_context(nc.psum_tensor("ps_c", [128, 1024], F32))
        ps_d = ctx.enter_context(nc.psum_tensor("ps_d", [128, 1024], F32))

        banks = [(ps_a, ps_b, ps_c, ps_d)[n // 2][:, 512 * (n % 2):512 * (n % 2) + 512] for n in range(8)]

        const = sb("const", [128, CONST_WIDTH])
        at = 0
        ident = const[:, at:at + 128]; at += 128
        own_head = const[:, at:at + 16]; at += 16
        own_in_group = const[:, at:at + 4]; at += 4
        own_half = const[:, at:at + 2]; at += 2
        causal0 = const[:, at:at + 64]; at += 64
        causal1 = const[:, at:at + NK1]; at += NK1
        cos = const[:, at:at + 64]; at += 64
        sin = const[:, at:at + 64]; at += 64
        w_projx = sb("w_projx", [128, C])
        x_all = sb("x_all", [128, NPAIR, C])
        on_all = sb("on_all", [128, B, TP])
        pool_all = sb("pool_all", [128, B])

        NJ = H1 // 2
        w_qk1 = sb("w_qk1", [128, 2, 1024])
        w_v1 = sb("w_v1", [128, 1024])
        w_out1 = sb("w_out1", [128, NJ, C])
        w_mem = sb("w_mem", [128, C])
        w_up1 = sb("w_up1", [128, 6, 128])
        w_down1 = sb("w_down1", [128, 3, C])
        cols1 = sb("cols1", [128, 3 + 6])
        row_b1 = sb("row_b1", [128, C])
        persist_k = sb("persist_k", [128, NJ, NM])
        loaded1 = sem("loaded1")
        n_loads1 = 16 * 9

        early = ExitStack()

        def sbe(name, shape, dt=F32):
            return early.enter_context(nc.sbuf_tensor(name + "_sb", shape, dt))
        w_kv = sbe("w_kv", [128, 2 * C])
        cols = sbe("cols", [128, 6])
        q_split = sbe("q_split", [128, B, 2, 4 * T], F16)

        context = [sbe(f"context{r}", [KP, KT, C]) for r in range(3)]
        st = sbe("st", [KP, KT, 6])
        ln = sbe("ln", [KP, 6, KT])
        ones = sbe("ones", [KP, 1])
        sums = sbe("sums", [KP, KT // 2, C])

        self_only = ExitStack()

        def sbm(name, shape, dt=F32):
            return self_only.enter_context(nc.sbuf_tensor(name + "_sb", shape, dt))
        w_qkv0 = sbm("w_qkv0", [128, 3 * C])
        w_proj0 = sbm("w_proj0", [128, C])
        w_q = sbm("w_q", [128, C])
        w_up0 = sbm("w_up0", [128, FF0])
        w_down0 = sbm("w_down0", [128, 4, C])
        b_up0 = sbm("b_up0", [128, 4])
        rows0 = sbm("rows0", [128, 3, C])
        b_rest = sbm("b_rest", [128, C])

        context_in = [sem(f"cross_context_in{r}") for r in range(3)]

        def load_context(sp, b, r):
            sp.dma_start(context[r][:], dram["ctx"][b].rearrange("(p k) c -> p k c", k=KT)).then_inc(context_in[r], 16)

        loaded = sem("loaded")
        steps_counted = sem("steps_counted")

        def alone(eng):
            eng.sem_inc(steps_counted, 1)

        def rsqrt_guess(link, y, v):
            link(nc.vector.tensor_scalar(y.bitcast(I32), v.bitcast(I32), -0.5, 1597463007.0, ALU.mult, ALU.add))

        def rsqrt_step(link, y, v, tmp):
            link(nc.vector.tensor_tensor(tmp, y, y, ALU.mult))
            link(nc.vector.scalar_tensor_tensor(tmp, tmp, -0.5, v, ALU.mult, ALU.mult))
            link(nc.vector.scalar_tensor_tensor(y, tmp, 1.5, y, ALU.add, ALU.mult))

        def rsqrt(ve, link, y, v, tmp, eps):
            link(nc.vector.tensor_scalar(v, v, eps, None, ALU.add))
            rsqrt_guess(link, y, v)
            for _ in range(3):
                rsqrt_step(link, y, v, tmp)

        def chain(eng, semaphore, base, per):
            count = [0]

            def link(ins):
                count[0] += 1
                ins.then_inc(semaphore, 1)
                eng.wait_ge(semaphore, base + count[0])

            def ends():
                assert count[0] == per, (count[0], per)
            return link, ends

        mask0 = sbm("mask0", [128, NPAIR, TP])
        x_clear, x_loaded = sem("x_clear"), sem("x_loaded")
        n_loads = 16 * 12

        per = dict(context_in=16, sums_ready=1, pool_done=1, pooled=1, stats_ready=1, z_ready=3, t_done=3, xs_ready=3,
                   k_done=3, khigh_ready=3, klow_ready=3, keys_in=192, v_done=3, values_ready=3,
                   queries_in=192, scan_done=24, best_ready=24, best_t_done=2, neg_ready=2, neg_t_done=1,
                   shift_ready=1, shift_in=32, scores_done=12, probs_ready=12, pv_done=12, o_read=1,
                   o_t_done=1, o_rows_ready=1, o_rows_t_done=1, on_ready=1)
        Q = {n: [sem(f"cross_{n}{r}") for r in range(3)] if n.endswith("_in") else sem("cross_" + n)
             for n in per if n != "context_in"}
        Q["context_in"] = context_in
        ln_chain, sum_chain, cleared = sem("ln_chain"), sem("sum_chain"), sem("cleared")
        NLN = 17

        def context_sums(pool, b, r):
            link, ends = chain(pool, sum_chain, b * 3, 3)
            rows = context[r]
            link(nc.gpsimd.tensor_tensor(sums[:], rows[:, 0:6, :], rows[:, 6:12, :], ALU.add))
            link(nc.gpsimd.tensor_tensor(sums[:, 0:3, :], sums[:, 0:3, :], sums[:, 3:6, :], ALU.add))
            link(nc.gpsimd.tensor_tensor(sums[:, 0, :], sums[:, 0, :], sums[:, 1, :], ALU.add))
            nc.gpsimd.tensor_tensor(sums[:, 0, :], sums[:, 0, :], sums[:, 2, :], ALU.add
                                    ).then_inc(Q["sums_ready"], 1)
            ends()

        def context_normed(r):
            for k in range(KT):
                tile = context[r][:, k, :]
                ins = nc.gpsimd.tensor_scalar(tile, tile, ln[:, 4, k:k + 1], ln[:, 5, k:k + 1],
                                              ALU.mult, ALU.add)
                if k % 4 == 3:
                    ins.then_inc(Q["z_ready"], 1)

        def context_deviation(part, link, ends):
            mu, var, y, tmp = ln[:, 0, :], ln[:, 1, :], ln[:, 4, :], ln[:, 3, :]
            if part == 0:
                link(nc.vector.tensor_tensor(mu, st[:, :, 1], st[:, :, 4], ALU.add))
                link(nc.vector.tensor_tensor(tmp, st[:, :, 1], st[:, :, 4], ALU.subtract))
                link(nc.vector.tensor_tensor(var, st[:, :, 2], st[:, :, 5], ALU.add))
                link(nc.vector.tensor_tensor(tmp, tmp, tmp, ALU.mult))
            elif part == 1:
                link(nc.vector.tensor_scalar(tmp, tmp, 0.25, EPS0, ALU.mult, ALU.add))
                link(nc.vector.scalar_tensor_tensor(var, var, 1.0 / C, tmp, ALU.mult, ALU.add))
                rsqrt_guess(link, y, var)
                rsqrt_step(link, y, var, tmp)
            elif part == 2:
                rsqrt_step(link, y, var, tmp)
                rsqrt_step(link, y, var, tmp)
            else:
                nc.vector.scalar_tensor_tensor(ln[:, 5, :], mu, -0.5, y, ALU.mult, ALU.mult).then_inc(Q["stats_ready"], 1)
                ends()

        with self_only, ExitStack() as p1:
            def sb1(name, shape, dt=F32):
                return p1.enter_context(nc.sbuf_tensor(name + "_sb", shape, dt))
            stats = sb1("stats", [128, NPAIR, 6])
            meanvar = sb1("meanvar", [128, NPAIR, 2])
            rstd = sb1("rstd", [128, NPAIR])
            newton = sb1("newton", [128, NPAIR])
            z = sb1("z", [128, NPAIR, C])
            xn = sb1("xn", [128, NPAIR // U, 2, U * 128])
            xn_now = sb1("xn_now", [128, 2, U * 128])
            q0 = sb1("q0", [128, U * 128])
            k0 = sb1("k0", [128, U * 128])
            k_bufs = [sb1(f"k_wide{n}", [128, 2, H0, TP])[:] for n in range(2)]
            k_bufs.append(z[:].rearrange("p n c -> p (n c)").rearrange("p (b h s) -> p b h s", b=2, h=H0))
            k_wide = [k_bufs[n] for n in (0, 1, 2, 0)]
            v_wide = sb1("v_wide", [128, 2 * U, 8, 2, D0])
            s0 = [sb1(f"s0_{u}", [128, H0, TP]) for u in range(U)]
            s_max = sb1("s_max", [128, U, H0])
            s_sum = sb1("s_sum", [128, U, H0])
            e0_t = [sb1(f"e0_t{n}", [128, 8, 128]) for n in range(2)]
            o0, o0_t = q0, k0
            r1 = sb1("r1", [128, NPAIR, C])
            q_halves = k_bufs[0].rearrange("p b h s -> p (b h s)").bitcast(F16).rearrange(
                "p (q a n) -> p q a n", q=NPAIR // U, a=2)
            up0 = sb1("up0", [128, 4, U * 128])
            pad_word = up0[:, 0:2, :].rearrange("p a n -> p (a n)").bitcast(I32).rearrange("p (n t) -> p n t", t=TP)
            NIT = NPAIR // U
            per1 = dict(k_ready=2, k_later=2, s0_done=U, s0_max=U, s0_ready=U, e0_ready=U, et_done=2 * U, et_ready=2 * U,
                        up_done=4, up_ready=4, pv0_done=U - 1)
            names = ["xn_ready", "qk_done", "v_done", "q0_ready", "k0_ready", "v_ready", "down_read",
                     "o0_done", "o0_ready", "o0t_done", "o0t_ready", "sa_done", "down_done", *per1]
            S = {n: sem("self_" + n) for n in names}
            A = {n: sem("rows_" + n) for n in ("z_ready", "zt_done", "xn3_ready", "xn1_ready", "r1_ready", "z2_ready", "z2t_done",
                                               "xq_ready", "q2_done", "q_high", "q_high_out", "q_low_out")}
            dve1, ln_rows = sem("dve1"), sem("ln_rows")
            NL = U + 2 + 2 + 1

            def waiter1(eng, i):
                def wait(n, k=1):
                    eng.wait_ge(S[n], i * per1.get(n, 1) + k)
                return wait
            with nc.Block() as block:
                @block.sync
                def _(sp):
                    sp.dma_start(const[:], dram["const"]).then_inc(x_loaded, 16)
                    sp.wait_ge(x_clear, 2)
                    for b2 in range(2):
                        sp.dma_start(x_all[64 * b2:64 * b2 + T, :, :],
                                     dram["x"].rearrange("(p b) t c -> b t p c", b=2)[b2]).then_inc(x_loaded, 16)

                    def load(dst, src, to=loaded):
                        sp.dma_start(dst, src).then_inc(to, 16)
                    load(cols[:], dram["cols"])
                    load(w_qkv0[:], dram["w_qkv0"])
                    load(w_up0[:], dram["w_up0"])
                    load(b_up0[:], dram["b_up0"])
                    for b2 in range(2):
                        load(pad_word[64 * b2:64 * b2 + 64, :, 0:T],
                             dram["mask"].rearrange("a (p b) t -> b a p t", b=2)[b2].broadcast_to([64, NPAIR, T]))
                    load(rows0[:], dram["rows0"].broadcast_to([128, 3, C]))
                    load(w_down0[:], dram["w_down0"].rearrange("(j p) n -> p j n", p=128))
                    load(w_proj0[:], dram["w_proj0"])
                    load(w_q[:], dram["w_q"])
                    load(w_kv[:], dram["w_kv"])
                    load(w_projx[:], dram["w_projx"])
                    for b in range(3):
                        load_context(sp, b, b)

                    load(w_mem[:], dram["w_mem"], loaded1)
                    load(cols1[:], dram["cols1"], loaded1)
                    load(w_qk1[:], dram["w_qkv1"][:, 0:2048].rearrange("p (a n) -> p a n", a=2), loaded1)
                    load(w_v1[:], dram["w_qkv1"][:, 2048:3072], loaded1)
                    load(persist_k[:], dram["persist_k"], loaded1)
                    load(w_out1[:], dram["w_out1"].rearrange("(j p) n -> p j n", p=128), loaded1)
                    load(w_up1[:], dram["w_up1"], loaded1)
                    load(w_down1[:], dram["w_down1"].rearrange("(j p) n -> p j n", p=128), loaded1)
                    load(row_b1[:], dram["row_b1"].broadcast_to([128, C]), loaded1)

                @block.tensor
                def _(pe):
                    def values0(pe, i, u):
                        wait = waiter1(pe, i)
                        wait("et_ready", 2 * u + 2)
                        for b2 in range(2):
                            for c in range(8):
                                last = nc.tensor.matmul(banks[0][64 * b2:64 * b2 + 64, 128 * u + 16 * c:128 * u + 16 * c + 16],
                                                        e0_t[u % 2][:, c, 64 * b2:64 * b2 + 64],
                                                        v_wide[:, 2 * u + b2, c, :, :].rearrange("p h d -> p (h d)"),
                                                        start=True, stop=True)
                        if u < U - 1:
                            last.then_inc(S["pv0_done"], 1)
                        return last

                    pe.wait_ge(x_loaded, 48)
                    for q in range(NIT):
                        pe.wait_ge(A["z_ready"], q + 1)
                        for u in range(U):
                            last = nc.tensor.transpose(banks[q][:, 128 * u:128 * u + 128], z[:, U * q + u, :], ident)
                        last.then_inc(A["zt_done"], 1)
                    pe.wait_ge(A["xn1_ready"], NIT)
                    pe.wait_ge(loaded, n_loads)
                    with pe.Fori(0, NIT) as i:
                        wait = waiter1(pe, i)
                        wait("xn_ready")
                        xn1, xn3 = xn_now[:, 0, :], xn_now[:, 1, :]
                        nc.tensor.matmul(banks[1], w_qkv0[:, 0:128], xn1, start=True, stop=True)
                        nc.tensor.matmul(banks[2], w_qkv0[:, 128:256], xn1, start=True, stop=True
                                         ).then_inc(S["qk_done"], 1)
                        wait("down_read")
                        alone(pe)
                        for n in range(2 * U):
                            for half in range(2):
                                last = nc.tensor.matmul(ps_d[64 * half:64 * half + 64, 128 * n:128 * n + 128],
                                                        xn1[:, 64 * n:64 * n + 64], w_qkv0[:, 256:384],
                                                        start=True, stop=True)
                        last.then_inc(S["v_done"], 1)
                        for j in range(4):
                            if j >= 2:
                                wait("up_ready", j - 1)
                            nc.tensor.matmul(banks[4 + j % 2], w_up0[:, 128 * j:128 * j + 128], xn3, start=True,
                                             stop=True).then_inc(S["up_done"], 1)
                        wait("q0_ready")
                        for u in range(U):
                            if u < 2:
                                wait("k_ready", u + 1)
                            else:
                                wait("k_later", u - 1)
                            if u >= 2:
                                wait("s0_max", u - 1)
                            if u == 1:
                                wait("up_ready", 4)
                            ps = (ps_a, ps_c)[u % 2]
                            for half in range(2):
                                for b2 in range(2):
                                    last = nc.tensor.matmul(ps[64 * b2:64 * b2 + 64, 512 * half:512 * half + 512],
                                                            q0[:, 128 * u + 64 * b2:128 * u + 64 * b2 + 64],
                                                            k_wide[u][:, b2, 8 * half:8 * half + 8, :].rearrange("p h s -> p (h s)"),
                                                            start=True, stop=True)
                            last.then_inc(S["s0_done"], 1)
                        wait("v_ready")
                        for u in range(U):
                            for j in range(4):
                                last = nc.tensor.matmul(banks[6][:, 128 * u:128 * u + 128], up0[:, j, 128 * u:128 * u + 128],
                                                        w_down0[:, j, :], start=(j == 0), stop=(j == 3))
                        last.then_inc(S["down_done"], 1)
                        for u in range(U):
                            wait("e0_ready", u + 1)
                            for part in range(2):
                                n = 2 * u + part
                                if n >= 2:
                                    wait("et_ready", n - 1)
                                for c in range(4):
                                    last = nc.tensor.transpose(banks[3 + 4 * part][:, 128 * c:128 * c + 128],
                                                               s0[u][:, 8 * part + 2 * c:8 * part + 2 * c + 2, :].rearrange("p h s -> p (h s)"),
                                                               ident)
                                last.then_inc(S["et_done"], 1)
                            if u > 0:
                                values0(pe, i, u - 1)
                        values0(pe, i, U - 1).then_inc(S["o0_done"], 1)
                        wait("o0_ready")
                        for u in range(U):
                            last = nc.tensor.transpose(banks[1][:, 128 * u:128 * u + 128], o0[:, 128 * u:128 * u + 128], ident)
                        last.then_inc(S["o0t_done"], 1)
                        wait("o0t_ready")
                        for u in range(U):
                            last = nc.tensor.matmul(banks[3][:, 128 * u:128 * u + 128], o0_t[:, 128 * u:128 * u + 128],
                                                    w_proj0[:], start=True, stop=True)
                        last.then_inc(S["sa_done"], 1)
                    pe.wait_ge(A["r1_ready"], 1)
                    for q in range(NIT):
                        pe.wait_ge(A["z2_ready"], q + 1)
                        for u in range(U):
                            last = nc.tensor.transpose(banks[q][:, 128 * u:128 * u + 128], z[:, U * q + u, :], ident)
                        last.then_inc(A["z2t_done"], 1)
                    for q in range(NIT):
                        pe.wait_ge(A["xq_ready"], q + 1)
                        nc.tensor.matmul(banks[4 + q], w_q[:], xn[:, q, 0, :], start=True, stop=True).then_inc(A["q2_done"], 1)

                @block.scalar
                def _(act):
                    act.wait_ge(loaded, n_loads)
                    for q in range(NIT):
                        act.wait_ge(A["zt_done"], q + 1)
                        nc.scalar.activation(xn[:, q, 1, :], banks[q], ACT.Identity, bias=cols[:, 5:6],
                                             scale=cols[:, 4:5]).then_inc(A["xn3_ready"], 1)
                    act.wait_ge(A["xn1_ready"], NIT)
                    act.wait_ge(A["xn3_ready"], NIT)
                    with act.Fori(0, NIT) as i:
                        wait = waiter1(act, i)
                        nc.scalar.copy(xn_now[:], xn[:, i, :, :]).then_inc(S["xn_ready"], 1)
                        wait("qk_done")
                        nc.scalar.copy(k0[:], banks[2]).then_inc(S["k0_ready"], 1)
                        nc.scalar.mul(q0[:], banks[1], float(C) ** -0.5).then_inc(S["q0_ready"], 1)
                        for j in range(4):
                            wait("up_done", j + 1)
                            nc.scalar.activation(up0[:, j, :], banks[4 + j % 2], ACT.Relu,
                                                 bias=b_up0[:, j:j + 1]).then_inc(S["up_ready"], 1)
                        for step in range(U + 2):
                            if step < U:
                                wait("s0_ready", step + 1)
                                nc.scalar.activation(s0[step][:], s0[step][:], ACT.Exp).then_inc(S["e0_ready"], 1)
                            u = step - 2
                            for part in range(2) if u >= 0 else []:
                                wait("et_done", 2 * u + part + 1)
                                if u >= 2:
                                    act.wait_ge(S["pv0_done"], i * (U - 1) + u - 1)
                                nc.scalar.copy(e0_t[u % 2][:, 4 * part:4 * part + 4, :],
                                               banks[3 + 4 * part].rearrange("p (c t) -> p c t", c=4)).then_inc(S["et_ready"], 1)
                        wait("o0t_done")
                        nc.scalar.copy(o0_t[:], banks[1]).then_inc(S["o0t_ready"], 1)
                    for q in range(NIT):
                        act.wait_ge(A["z2t_done"], q + 1)
                        nc.scalar.activation(xn[:, q, 0, :], banks[q], ACT.Identity, bias=cols[:, 3:4],
                                             scale=cols[:, 2:3]).then_inc(A["xq_ready"], 1)
                    for q in range(NIT):
                        act.wait_ge(A["q2_done"], q + 1)
                        nc.scalar.mul(q_halves[:, q, 0, :], banks[4 + q], float(C) ** -0.5).then_inc(A["q_high"], 1)
                        act.wait_ge(A["q_high"], q + 1)
                        for h in range(4):
                            last = nc.scalar.activation(q_split[:, 2 * U * q:2 * U * q + 2 * U, 0, T * h:T * h + T],
                                                        q_halves[:, q, 0, :].rearrange("p (b t) -> p b t", t=TP)[:, :, 0:T],
                                                        ACT.Identity, scale=own_in_group[:, h:h + 1])
                        last.then_inc(A["q_high_out"], 1)

                @block.gpsimd
                def _(pool):
                    nc.gpsimd.memset(x_all[:], 0.0).then_inc(x_clear, 1)
                    nc.gpsimd.memset(pad_word, 0).then_inc(x_clear, 1)
                    nc.gpsimd.memset(on_all[:], 0.0).then_inc(x_clear, 1)
                    nc.gpsimd.memset(ones[:], 1.0).then_inc(cleared, 1)
                    pool.wait_ge(x_loaded, 48)
                    with pool.Fori(0, NIT) as i:
                        wait = waiter1(pool, i)
                        wait("k0_ready")
                        for u in (2, 3):
                            if u == 3:
                                wait("s0_done", 1)
                            for b2 in range(2):
                                ins = nc.gpsimd.tensor_tensor(
                                    k_wide[u][:, b2, :, :],
                                    k0[:, 128 * u + 64 * b2:128 * u + 64 * b2 + 64].unsqueeze(1).broadcast_to([128, H0, TP]),
                                    own_head.unsqueeze(2).broadcast_to([128, H0, TP]), ALU.mult)
                            ins.then_inc(S["k_later"], 1)
                        for u in range(U):
                            wait("s0_max", u + 1)
                            nc.gpsimd.tensor_tensor(s0[u][:], s0[u][:], s_max[:, u, :].unsqueeze(2).broadcast_to([128, H0, TP]),
                                                    ALU.subtract).then_inc(S["s0_ready"], 1)
                    pool.wait_ge(context_in[0], 16)
                    context_sums(pool, 0, 0)
                    pool.wait_ge(Q["stats_ready"], 1)
                    pool.wait_ge(Q["sums_ready"], 1)
                    context_normed(0)

                @block.vector
                def _(ve):
                    link, _ = chain(ve, ln_rows, 0, 0)

                    def layernorm(out, x, done):
                        for n in range(NPAIR):
                            ins = nc.vector.bn_stats(stats[:, n, :], x[:, n, :])
                        link(ins)
                        for n in range(NPAIR):
                            ins = nc.vector.bn_aggr(meanvar[:, n, :], stats[:, n, :])
                        link(ins)
                        rsqrt(ve, link, rstd[:], meanvar[:, :, 1], newton[:], EPS0)
                        for n in range(NPAIR):
                            ins = nc.vector.tensor_scalar(out[:, n, :], x[:, n, :], meanvar[:, n, 0:1], rstd[:, n:n + 1],
                                                          ALU.subtract, ALU.mult)
                            if n % U == U - 1:
                                ins.then_inc(A[done], 1)

                    ve.wait_ge(x_loaded, 48)
                    layernorm(z, x_all, "z_ready")
                    ve.wait_ge(loaded, n_loads)
                    for q in range(NIT):
                        ve.wait_ge(A["xn3_ready"], q + 1)
                        nc.vector.tensor_scalar(xn[:, q, 0, :], banks[q], cols[:, 0:1], cols[:, 1:2], ALU.mult,
                                                ALU.add).then_inc(A["xn1_ready"], 1)
                    link(nc.vector.tensor_tensor(b_rest[:], rows0[:, 1, :], rows0[:, 2, :], ALU.add))
                    link(nc.vector.tensor_copy(mask0[:], pad_word))
                    link(nc.vector.tensor_scalar(mask0[:], mask0[:], -1e30, None, ALU.mult))
                    link(nc.vector.tensor_tensor(mask0[:], mask0[:],
                                                 causal0.unsqueeze(1).broadcast_to([128, NPAIR, TP]), ALU.add))
                    ve.sem_inc(S["down_read"], 1)
                    with ve.Fori(0, NIT) as i:
                        wait = waiter1(ve, i)
                        link, ends = chain(ve, dve1, i * NL, NL)
                        x4 = x_all[:].rearrange("p (i u) c -> p i u c", u=U)[:, i, :, :]
                        r4 = r1[:].rearrange("p (i u) c -> p i u c", u=U)[:, i, :, :]
                        wait("k0_ready")
                        for u in (0, 1):
                            for b2 in range(2):
                                ins = nc.vector.tensor_tensor(
                                    k_wide[u][:, b2, :, :],
                                    k0[:, 128 * u + 64 * b2:128 * u + 64 * b2 + 64].unsqueeze(1).broadcast_to([128, H0, TP]),
                                    own_head.unsqueeze(2).broadcast_to([128, H0, TP]), ALU.mult)
                            ins.then_inc(S["k_ready"], 1)
                        wait("v_done")
                        nc.vector.tensor_tensor(v_wide[:].rearrange("p n c h d -> p (n c) h d"),
                                                ps_d[:, :].rearrange("p (n h d) -> p n h d", h=2, d=D0),
                                                own_half.unsqueeze(1).unsqueeze(3).broadcast_to([128, 16 * U, 2, D0]),
                                                ALU.mult).then_inc(S["v_ready"], 1)
                        for u in range(U):
                            wait("s0_done", u + 1)
                            link(nc.vector.tensor_tensor(s0[u][:], (ps_a, ps_c)[u % 2][:, :].rearrange("p (h s) -> p h s", h=H0),
                                                         mask0[:].rearrange("p (i u) s -> p i u s", u=U)[:, i, u, :].unsqueeze(1).broadcast_to([128, H0, TP]), ALU.add))
                            nc.vector.reduce_max(s_max[:, u, :], s0[u][:], AX.X).then_inc(S["s0_max"], 1)
                        for u in range(U):
                            wait("e0_ready", u + 1)
                            ins = nc.vector.reduce_sum(s_sum[:, u, :], s0[u][:], AX.X)
                        link(ins)
                        link(nc.vector.reciprocal(s_sum[:], s_sum[:]))
                        link(nc.vector.tensor_tensor(r4, x4, rows0[:, 0, :].unsqueeze(1).broadcast_to([128, U, C]), ALU.add))
                        link(nc.vector.tensor_tensor(x4, r4, b_rest[:].unsqueeze(1).broadcast_to([128, U, C]), ALU.add))
                        wait("down_done")
                        nc.vector.tensor_tensor(x4, banks[6].rearrange("p (u c) -> p u c", u=U), x4, ALU.add
                                                ).then_inc(S["down_read"], 1)
                        wait("o0_done")
                        nc.vector.tensor_tensor(o0[:].rearrange("p (n d) -> p n d", d=D0),
                                                banks[0].rearrange("p (n d) -> p n d", d=D0),
                                                s_sum[:].rearrange("p u h -> p (u h)").unsqueeze(2).broadcast_to([128, U * H0, D0]),
                                                ALU.mult).then_inc(S["o0_ready"], 1)
                        wait("sa_done")
                        ve.wait_ge(S["down_read"], i + 2)
                        nc.vector.tensor_tensor(r4, banks[3].rearrange("p (u c) -> p u c", u=U), r4, ALU.add)
                        link(nc.vector.tensor_tensor(x4, banks[3].rearrange("p (u c) -> p u c", u=U), x4, ALU.add))
                        ends()
                    ve.sem_inc(A["r1_ready"], 1)
                    link, _ = chain(ve, ln_rows, 17, 0)
                    layernorm(z, r1, "z2_ready")
                    ve.wait_ge(context_in[0], 16)
                    ln_link, ln_ends = chain(ve, ln_chain, 0, NLN)
                    for k in range(KT):
                        ins = nc.vector.bn_stats(st[:, k, :], context[0][:, k, :])
                    ln_link(ins)
                    for part in range(4):
                        context_deviation(part, ln_link, ln_ends)
                    for q in range(NIT):
                        ve.wait_ge(A["q_high"], q + 1)
                        link(nc.vector.scalar_tensor_tensor(q_halves[:, q, 1, :], banks[4 + q], float(C) ** -0.5, q_halves[:, q, 0, :],
                                                            ALU.mult, ALU.subtract))
                        nc.vector.tensor_tensor(q_split[:, 2 * U * q:2 * U * q + 2 * U, 1, :].rearrange("p b (h t) -> p b h t", h=4),
                                                q_halves[:, q, 1, :].rearrange("p (b t) -> p b t", t=TP)[:, :, 0:T].unsqueeze(2).broadcast_to([128, 2 * U, 4, T]),
                                                own_in_group.unsqueeze(1).unsqueeze(3).broadcast_to([128, 2 * U, 4, T]),
                                                ALU.mult).then_inc(A["q_low_out"], 1)

        with ExitStack() as p2:
            def sb2(name, shape, dt=F32):
                return p2.enter_context(nc.sbuf_tensor(name + "_sb", shape, dt))
            GROUPS, GN = 4, 4 * T
            SCAN_SLOTS = 8
            BEST, NEG = 8, 9
            KEYS, VALUES = (1, 2, 3), (4, 5, 6)
            TURN = (9, 10, 11)
            STATS, NORM, SUM = (4, 5, 6, 7), (8, 9, 10, 11), 11
            O_TURN, O_BACK = 0, 7
            ROWS = 96
            W = H0 * T
            keys = [sb2(f"keys{r}", [ROWS + 2, GROUPS, J], F16) for r in range(3)]
            queries = [sb2(f"queries{r}", [ROWS + 2, W], F16) for r in range(3)]
            values = [sb2(f"values{r}", [KP, KT, 8, 32]) for r in range(3)]
            xs_t = sb2("xs_t", [128, J])
            k_split = sb2("k_split", [128, 2, J], F16)
            best = sb2("best", [KP, W])
            probs = [sb2(f"probs{r}", [KP, W]) for r in range(2)]
            neg_max = sb2("neg_max", [128, 7])
            shift = sb2("shift", [7, 2, 128], F16)
            o_wide = sb2("o_wide", [128, 4 * T])
            o_rec = sb2("o_rec", [T, 16])
            o_rows = sb2("o_rows", [T, C])
            keys_filled = sem("keys_filled")
            o_chain = sem("o_chain")
            m_chain = sem("m_chain")
            ring = [ps_c[:, 0:512], ps_c[:, 512:1024]]
            o_bank = ps_d[:, 0:4 * T]
            misc = ps_d[:, 512:1024]

            def halves(ps):
                return ps.rearrange("p (e n) -> p e n", e=2)[:, :, 0:448]

            def steps(eng, emit):
                def one(b, r, turn):
                    emit(b, r, lambda d, b=b: not isinstance(b, int) or 0 <= b + d < B, turn)
                for b in range(-5, 1):
                    one(b, b % 3, lambda d, b=b: (b + d) // 3)
                with eng.Fori(0, 8) as i:
                    for r in range(1, 4):
                        one(i * 3 + r, r % 3, lambda d, r=r: i + (r + d) // 3)
                for b in range(25, B + 1):
                    one(b, b % 3, lambda d, b=b: (b + d) // 3)

            def first(b):
                return isinstance(b, int) and b == 0

            def landed(n, d, r):
                return Q[n][(r + d) % 3]

            def waiter(eng, b, r, turn):
                def wait(n, d, k):
                    if n.endswith("_in"):
                        if k == 0:
                            d, k = d - 1, per[n]
                            if isinstance(b, int) and b + d < 0:
                                return
                        eng.wait_ge(landed(n, d, r), turn(d) * per[n] + k)
                        return
                    value = (b + d) * per[n] + k
                    assert isinstance(b, int) or (1 + d) * per[n] + k > 0, "the loop starts at batch 1"
                    if not isinstance(value, int) or value > 0:
                        eng.wait_ge(Q[n], value)
                return wait

            with nc.Block() as block:
                @block.gpsimd
                def _(pool):
                    def clear_values():
                        n = 1
                        for r in range(3):
                            for where, value in ((values[r][:, :, :, 17:32], 0.0), (values[r][:, :, :, 16:17], 1.0)):
                                pool.wait_ge(cleared, n)
                                nc.gpsimd.memset(where, value).then_inc(cleared, 1)
                                n += 1

                    def emit(b, r, has, turn):
                        wait = waiter(pool, b, r, turn)
                        if has(3) and not first(b + 3):
                            wait("stats_ready", 3, 1)
                            wait("sums_ready", 3, 1)
                            alone(pool)
                            context_normed(r)
                        if has(4) and not first(b + 4):
                            wait("context_in", 4, 16)
                            wait("pool_done", 4, 0)
                            alone(pool)
                            context_sums(pool, b + 4, (r + 1) % 3)
                        if isinstance(b, int) and b == -3:
                            clear_values()
                    steps(pool, emit)

                @block.sync
                def _(sp):
                    for r in range(3):
                        sp.dma_start(keys[r][ROWS:ROWS + 2, :, :], dram["ones"]).then_inc(keys_filled, 16)

                    def emit(b, r, has, turn):
                        wait = waiter(sp, b, r, turn)
                        r1, r2 = (r + 1) % 3, (r + 2) % 3
                        if has(5) and not (isinstance(b, int) and b + 5 < 3):
                            wait("t_done", 2, 3)
                            load_context(sp, b + 5, (r + 5) % 3)
                        if has(2):
                            wait("scores_done", 0, 0)
                            for block_, half in ((0, 0), (1, 1), (2, 0)):
                                for g in range(GROUPS):
                                    sp.dma_start(queries[r2][32 * block_:32 * block_ + 32, GN * g:GN * g + GN],
                                                 q_split[32 * g:32 * g + 32, b + 2, half, :]).then_inc(landed("queries_in", 2, r), 16)
                            wait("khigh_ready", 2, 3)
                            for block_, half in ((0, 0), (1, 0), (2, 1)):
                                if half:
                                    wait("klow_ready", 2, 3)
                                for g in range(GROUPS):
                                    sp.dma_start(keys[r2][32 * block_:32 * block_ + 32, g, :],
                                                 k_split[32 * g:32 * g + 32, half, :]).then_inc(landed("keys_in", 2, r), 16)
                        if has(1):
                            wait("shift_ready", 1, 1)
                            for half in range(2):
                                sp.dma_start(queries[r1][ROWS + half:ROWS + half + 1, :],
                                             shift[:, half, :]).then_inc(landed("shift_in", 1, r), 16)
                    steps(sp, emit)

                @block.tensor
                def _(pe):
                    pe.wait_ge(cleared, 1)

                    def pv(b, d, k, r, wait):
                        wait("probs_ready", d, k + 1)
                        if k == 0:
                            wait("values_ready", d, 3)
                            wait("o_read", d, 0)
                        for g in range(8):
                            last = nc.tensor.matmul(o_bank[32 * (g % 4):32 * (g % 4) + 32, 112 * (g // 4):112 * (g // 4) + 112],
                                                    values[r][:, k, g, :], probs[k % 2][:, 112 * g:112 * g + 112],
                                                    start=(k == 0 and g < 4), stop=(k == KT - 1),
                                                    tile_position=(0, 32 * (g % 4)), skip_group_check=True)
                        last.then_inc(Q["pv_done"], 1)

                    def scores(out, r, k, rows, groups):
                        for g in groups:
                            col = 512 * (g // 2) + GN * (g % 2)
                            last = nc.tensor.matmul(out[0:KP, col:col + GN], keys[r][0:rows, g, KP * k:KP * k + KP],
                                                    queries[r][0:rows, GN * g:GN * g + GN], start=True, stop=True)
                        return last

                    def emit(b, r, has, turn):
                        wait = waiter(pe, b, r, turn)
                        r1, r2 = (r + 1) % 3, (r + 2) % 3

                        def scan(n):
                            if n == 0:
                                wait("keys_in", 1, 192)
                                wait("queries_in", 1, 192)
                                wait("neg_ready", 1, 0)
                            if n > 1:
                                wait("best_ready", 1, n - 1)
                            scores(ps_b, r1, n // 2, ROWS, (2 * (n % 2), 2 * (n % 2) + 1)).then_inc(Q["scan_done"], 1)

                        for s in range(KT):
                            scans = has(1) and s < SCAN_SLOTS
                            if has(2) and s in KEYS:
                                u = KEYS.index(s)
                                if u == 0:
                                    wait("xs_ready", 2, 3)
                                elif u == 2:
                                    wait("klow_ready", 2, 1)
                                nc.tensor.matmul(ring[u % 2][:, 0:500], w_kv[:, 0:128], xs_t[:, 500 * u:500 * u + 500],
                                                 start=True, stop=True).then_inc(Q["k_done"], 1)
                            if scans:
                                scan(3 * s)
                            if s > 0 and has(0):
                                wait("probs_ready", 0, s)
                                scores(ps_a, r, s, ROWS + 2, range(GROUPS)).then_inc(Q["scores_done"], 1)
                            if scans:
                                scan(3 * s + 1)
                            if s == 0 and has(-1):
                                pv(b, -1, KT - 1, r2, wait)
                            if s > 0 and has(0):
                                pv(b, 0, s - 1, r, wait)
                            if scans:
                                scan(3 * s + 2)
                            if isinstance(b, int) and b == 0 and s == 0:
                                pe.wait_ge(cleared, 7)
                                pe.wait_ge(keys_filled, 48)
                            if s == 0 and has(0):
                                wait("shift_in", 0, 32)
                                wait("probs_ready", 0, 0)
                                scores(ps_a, r, s, ROWS + 2, range(GROUPS)).then_inc(Q["scores_done"], 1)
                            if has(2) and s in VALUES:
                                u = VALUES.index(s)
                                if u < 2:
                                    wait("klow_ready", 2, u + 2)
                                else:
                                    wait("values_ready", 2, 1)
                                for k in range(4):
                                    last = nc.tensor.matmul(ring[1 - u % 2][0:KP, 128 * k:128 * k + 128],
                                                            xs_t[:, 500 * u + KP * k:500 * u + KP * k + KP],
                                                            w_kv[:, 128:256], start=True, stop=True)
                                last.then_inc(Q["v_done"], 1)
                            if has(3) and s in TURN:
                                u = TURN.index(s)
                                wait("z_ready", 3, u + 1)
                                if u < 2:
                                    wait("values_ready", 2, u + 2)
                                else:
                                    wait("xs_ready", 3, 1)
                                for k in range(4):
                                    last = nc.tensor.transpose(ring[u % 2][:, KP * k:KP * k + KP],
                                                               context[r][:, 4 * u + k, :], ident[0:KP, 0:KP])
                                last.then_inc(Q["t_done"], 1)
                            if has(-1) and s == O_TURN:
                                wait("o_read", -1, 1)
                                if has(0):
                                    wait("shift_ready", 0, 1)
                                else:
                                    wait("on_ready", -2, 1)
                                if has(3):
                                    wait("pooled", 3, 1)
                                alone(pe)
                                for e in range(4):
                                    last = nc.tensor.transpose(misc[0:T, 128 * e:128 * e + 128],
                                                               o_wide[:, T * e:T * e + T], ident)
                                last.then_inc(Q["o_t_done"], 1)
                            if has(-1) and s == O_BACK:
                                wait("o_rows_ready", -1, 1)
                                alone(pe)
                                nc.tensor.transpose(misc[:, 0:T], o_rows[:], ident[0:T, 0:T]).then_inc(Q["o_rows_t_done"], 1)
                            if has(1) and s == BEST:
                                wait("best_ready", 1, 2 * KT)
                                for c in range(7):
                                    to = 512 * (c // 4) + KP * (c % 4)
                                    last = nc.tensor.transpose(ps_b[:, to:to + KP],
                                                               best[:, 128 * c:128 * c + 128], ident[0:KP, 0:KP])
                                    if c in (3, 6):
                                        last.then_inc(Q["best_t_done"], 1)
                            if has(1) and s == NEG:
                                wait("neg_ready", 1, 2)
                                if has(-1):
                                    wait("on_ready", -1, 1)
                                else:
                                    wait("pooled", 3, 1)
                                nc.tensor.transpose(misc[0:7, 0:128], neg_max[:], ident).then_inc(Q["neg_t_done"], 1)
                            if has(4) and s == SUM:
                                wait("sums_ready", 4, 1)
                                wait("pooled", 3, 1)
                                if has(1):
                                    wait("shift_ready", 1, 1)
                                nc.tensor.matmul(misc[:, 0:1], sums[:, 0, :], ones[:], start=True, stop=True
                                                 ).then_inc(Q["pool_done"], 1)
                    steps(pe, emit)

                @block.scalar
                def _(act):

                    def emit(b, r, has, turn):
                        wait = waiter(act, b, r, turn)
                        r1, r2 = (r + 1) % 3, (r + 2) % 3
                        for s in range(KT):
                            if has(2) and s in KEYS:
                                u = KEYS.index(s)
                                wait("k_done", 2, u + 1)
                                wait("keys_in", 2, 0)
                                nc.scalar.copy(k_split[:, 0, 500 * u:500 * u + 500], ring[u % 2][:, 0:500]
                                               ).then_inc(Q["khigh_ready"], 1)
                            if s > 0 and has(0):
                                wait("scores_done", 0, s + 1)
                                wait("pv_done", 0, s - 1)
                                nc.scalar.activation(probs[s % 2][:].rearrange("p (e n) -> p e n", e=2),
                                                     halves(ps_a[0:KP, :]), ACT.Exp).then_inc(Q["probs_ready"], 1)
                            if s == 0 and has(-1):
                                wait("pv_done", -1, KT)
                                nc.scalar.copy(o_wide[:], o_bank).then_inc(Q["o_read"], 1)
                            if has(4) and s == SUM:
                                wait("pool_done", 4, 1)
                                nc.scalar.copy(pool_all[:, bass.ds(b + 4, 1)] if not isinstance(b, int) else
                                               pool_all[:, b + 4:b + 5], misc[:, 0:1]).then_inc(Q["pooled"], 1)
                            if s == 0 and has(0):
                                wait("scores_done", 0, s + 1)
                                wait("pv_done", 0, s - 1)
                                nc.scalar.activation(probs[s % 2][:].rearrange("p (e n) -> p e n", e=2),
                                                     halves(ps_a[0:KP, :]), ACT.Exp).then_inc(Q["probs_ready"], 1)
                            if has(2) and s in VALUES:
                                u = VALUES.index(s)
                                wait("v_done", 2, u + 1)
                                wait("pv_done", -1, KT)
                                nc.scalar.copy(values[r2][:, 4 * u:4 * u + 4, :, 0:16],
                                               ring[1 - u % 2][0:KP, :].rearrange("p (k g n) -> p k g n", k=4, g=8)
                                               ).then_inc(Q["values_ready"], 1)
                            if has(3) and s in TURN:
                                u = TURN.index(s)
                                wait("t_done", 3, u + 1)
                                wait("v_done", 2, u + 1)
                                nc.scalar.activation(xs_t[:, 500 * u:500 * u + 500], ring[u % 2][:, 0:500], ACT.Identity,
                                                     bias=cols[:, 3:4], scale=cols[:, 2:3]).then_inc(Q["xs_ready"], 1)
                    steps(act, emit)

                @block.vector
                def _(ve):
                    def emit(b, r, has, turn):
                        wait = waiter(ve, b, r, turn)
                        ln_link, ln_ends = chain(ve, ln_chain, (b + 4) * NLN, NLN)
                        o_link, _ = chain(ve, o_chain, b - 1, 1)
                        m_link, _ = chain(ve, m_chain, b + 1, 1)

                        def keep_best(n):
                            e = n % 2
                            wait("scan_done", 1, n + 1)
                            mine, new = best[:, 448 * e:448 * e + 448], ps_b[0:KP, 512 * e:512 * e + 448]
                            if n < 2:
                                wait("best_t_done", 1, 0)
                                ins = nc.vector.tensor_copy(mine, new)
                            else:
                                wait("best_ready", 1, n - 1)
                                ins = nc.vector.tensor_tensor(mine, new, mine, ALU.max)
                            ins.then_inc(Q["best_ready"], 1)

                        for s in range(KT):
                            for n in range(3 * s, 3 * s + 3) if has(1) and s < SCAN_SLOTS else []:
                                keep_best(n)
                            if has(-1) and s == O_TURN:
                                wait("o_t_done", -1, 1)
                                t4 = misc[0:T, :].rearrange("p (e h q r) -> p e h q r", e=2, h=2, q=4)
                                rec = o_rec[:].rearrange("p (e h q) -> p e h q", e=2, h=2)
                                o_link(nc.vector.reciprocal(o_rec[:], misc[0:T, :].rearrange("p (n r) -> p n r", r=32)[:, :, 16]))
                                rows = o_rows[:].rearrange("p (e q h d) -> p e q h d", e=2, q=4, h=2)
                                for h in range(2):
                                    ins = nc.vector.tensor_tensor(rows[:, :, :, h, :], t4[:, :, h, :, 8 * h:8 * h + 8],
                                                                  rec[:, :, h, :].unsqueeze(3).broadcast_to([T, 2, 4, 8]),
                                                                  ALU.mult)
                                ins.then_inc(Q["o_rows_ready"], 1)
                            if has(-1) and s == O_BACK:
                                wait("o_rows_t_done", -1, 1)
                                nc.vector.tensor_copy(on_all[:, b - 1, 0:T], misc[:, 0:T]).then_inc(Q["on_ready"], 1)
                            if has(2) and s in KEYS:
                                u = KEYS.index(s)
                                wait("khigh_ready", 2, u + 1)
                                wait("keys_in", 2, 0)
                                nc.vector.tensor_tensor(k_split[:, 1, 500 * u:500 * u + 500], ring[u % 2][:, 0:500],
                                                        k_split[:, 0, 500 * u:500 * u + 500], ALU.subtract
                                                        ).then_inc(Q["klow_ready"], 1)
                            for part in range(2) if has(1) and s == BEST else []:
                                wait("best_t_done", 1, part + 1)
                                n = 4 - part
                                nc.vector.tensor_reduce(neg_max[:, 4 * part:4 * part + n],
                                                        ps_b[:, 512 * part:512 * part + KP * n].rearrange("p (c j) -> p c j", c=n),
                                                        axis=AX.X, op=ALU.max, negate=True).then_inc(Q["neg_ready"], 1)
                            if has(1) and s == NEG:
                                wait("neg_t_done", 1, 1)
                                wait("shift_in", 1, 0)
                                m_link(nc.vector.tensor_copy(shift[:, 0, :], misc[0:7, 0:128]))
                                nc.vector.tensor_tensor(shift[:, 1, :], misc[0:7, 0:128], shift[:, 0, :],
                                                        ALU.subtract).then_inc(Q["shift_ready"], 1)
                            if has(4) and s in STATS and not first(b + 4):
                                u = STATS.index(s)
                                if u == 0:
                                    wait("context_in", 4, 16)
                                for k in range(3 * u, 3 * u + 3):
                                    ins = nc.vector.bn_stats(st[:, k, :], context[(r + 1) % 3][:, k, :])
                                if u == 3:
                                    ln_link(ins)
                            if has(4) and s in NORM and not first(b + 4):
                                if s == NORM[0]:
                                    wait("z_ready", 4, 0)
                                context_deviation(NORM.index(s), ln_link, ln_ends)
                    steps(ve, emit)

        early.close()

        with ExitStack() as p3:
            def sb3(name, shape, dt=F32):
                return p3.enter_context(nc.sbuf_tensor(name + "_sb", shape, dt))
            NB = 2 * U
            NIT = NPAIR // U
            NKM = TP + NM
            SC = 4 * NK1
            neg_gate_b = sb3("neg_gate_b", [128, 3])
            ident16 = sb3("ident16", [128, 128], BF16)
            causal16 = sb3("causal16", [128, 4, NK1], BF16)
            mem_rows = sb3("mem_rows", [B, C])
            mem_cols = sb3("mem_cols", [128, B])
            mem_t = sb3("mem_t", [128, B])
            mem_k = sb3("mem_k", [128, NJ, B])
            st_all = sb3("st_all", [128, NPAIR + 1, 6])
            mv_all = sb3("mv_all", [128, NPAIR + 1, 2])
            ms_all = sb3("ms_all", [128, 3, NPAIR + 1])
            xm = sb3("xm", [128, B, NKM])
            xm_now = sb3("xm_now", [128, NB, NKM])
            st1 = sb3("st1", [128, U, 6])
            mv1 = sb3("mv1", [128, U, 2])
            ms1 = sb3("ms1", [128, 3, U])
            h = sb3("h", [128, U, C])
            normed = sb3("normed", [128, U, C])
            NTURN = 4
            turn_a = [sb3(f"turn_a{n}", [128, NB, TP]) for n in range(NTURN)]
            turn_b = [sb3(f"turn_b{n}", [128, NB, TP]) for n in range(NTURN)]
            q1 = sb3("q1", [128, NJ, U * 128])
            normed_all = q1[:, 0:4, :].rearrange("p q (u c) -> p (q u) c", u=U)
            k1 = sb3("k1", [128, NJ, NB, NK1])
            v1 = sb3("v1", [NK1, NB, 1024])
            s1 = [sb3(f"s1_{u}", [128, 16, NK1]) for u in range(U)]
            s1_max = sb3("s1_max", [128, U, 16])
            s1_sum = sb3("s1_sum", [128, U, 16])
            e1_t = [sb3(f"e1_t{n}", [NK1, 16, 128]) for n in range(2)]
            o1_t = [sb3(f"o1_t{n}", [128, NJ, 128]) for n in range(2)]
            h_t = sb3("h_t", [128, U * 128])
            gate_e = sb3("gate_e", [128, 3, U * 128])
            y = sb3("y", [128, U, C])
            per3 = dict(turn_done=16, turn_read=16, sines=16, rotated=16, v_done=2 * NB, v_ready=2 * NB, s_done=2 * U,
                        s_read=U, s_top=U, s_copied=U, s_shifted=U, e_ready=U, sum_ready=U, e_normal=U, et_done=2 * U,
                        et_ready=2 * U, o_done=2 * U, o_ready=2 * U, up_done=3, gate_exp=3, up_ready=3,
                        out_done=U)
            names = ["xm_ready", "h_ready", "hn_ready", "ht_done", "ht_ready", "down_done", "y_ready", *per3]
            R = {n: sem("segment_" + n) for n in names}
            stored = sem("stored")
            loaded_v = sem("loaded_v")
            persist_ready = sem("persist_ready")
            tail_chain, main_chain = sem("tail_chain"), sem("main_chain")
            mem_pe, mem_dve = sem("mem_pe"), sem("mem_dve")
            head_pe, head_act, head_dve = sem("head_pe"), sem("head_act"), sem("head_dve")
            NTAIL, NMAIN = 2 + 2 + 11 + 3 * 3 + 1, 1 + U + U
            UP_AT, HT_AT, DOWN_AT = (4, 8, 12), 3, 15

            def waiter3(eng, i):
                def wait(n, k=1, d=0):
                    value = (i + d) * per3.get(n, 1) + k
                    if not isinstance(value, int) or value > 0:
                        eng.wait_ge(R[n], value)
                return wait

            def slice_of(n):
                return n // 4 % 2, n % 4 + 4 * (n // 8)

            def scores1(u):
                return (ps_a, ps_b)[u % 2][:, :].rearrange("p (r n) -> p r n", r=2)[:, :, 0:SC].rearrange(
                    "p r (j k) -> p r j k", j=4)

            def s1_view(u, half):
                return s1[u][:, 8 * half:8 * half + 8, :].rearrange("p (r j) k -> p r j k", r=2)

            def top1(u, half):
                return s1_max[:, u, 8 * half:8 * half + 8].rearrange("p (r j) -> p r j", r=2)

            def passes(eng, emit):
                emit(0, False, True)
                with eng.Fori(0, NIT - 1) as n:
                    emit(n + 1, True, True)
                emit(NIT, True, False)

            with nc.Block() as block:
                @block.sync
                def _(sp):
                    for b2 in range(NB):
                        sp.dma_start(v1[NKM:NK1, b2, :], dram["persist_v"]).then_inc(loaded_v, 16)
                    sp.wait_ge(loaded_v, 16 * NB)
                    sp.sem_inc(stored, 1)
                    with sp.Fori(0, NIT) as i:
                        sp.wait_ge(R["y_ready"], i + 1)
                        for b2 in range(2):
                            sp.dma_start(dram["out"].rearrange("(i u b) t c -> i b t u c", b=2, u=U)[i, b2],
                                         y[64 * b2:64 * b2 + T, :, :]).then_inc(stored, 16)
                    sp.wait_ge(stored, 32 * NIT + 1)

                @block.gpsimd
                def _(pool):
                    pool.wait_ge(loaded1, n_loads1)
                    nc.gpsimd.tensor_copy(k1[:, :, :, NKM:NK1], persist_k[:].unsqueeze(2).broadcast_to([128, NJ, NB, NM])
                                          ).then_inc(persist_ready, 1)

                    def emit(i, mlp, attention):
                        wait = waiter3(pool, i)
                        if not attention:
                            return
                        for n in range(16):
                            wait("turn_read", n + 1)
                            kind, j = slice_of(n)
                            dst = k1[:, j, :, 0:TP] if kind else q1[:, j, :].rearrange("p (b t) -> p b t", t=TP)
                            a, b = turn_a[n % NTURN], turn_b[n % NTURN]
                            nc.gpsimd.tensor_tensor(b[:], b[:], sin.unsqueeze(1).broadcast_to([128, NB, TP]), ALU.mult
                                                    ).then_inc(R["sines"], 1)
                            wait("sines", n + 1)
                            nc.gpsimd.tensor_tensor(dst, a[:], b[:], ALU.add).then_inc(R["rotated"], 1)

                        def normalise(u):
                            wait("sum_ready", u + 1)
                            nc.gpsimd.tensor_tensor(s1[u][:], s1[u][:],
                                                    s1_sum[:, u, :].unsqueeze(2).broadcast_to([128, 16, NK1]),
                                                    ALU.mult).then_inc(R["e_normal"], 1)

                        for u in range(U):
                            if u == U - 1:
                                normalise(0)
                            wait("s_top", u + 1)
                            wait("s_copied", u + 1)
                            nc.gpsimd.tensor_tensor(s1_view(u, 1), s1_view(u, 1),
                                                    top1(u, 1).unsqueeze(3).broadcast_to([128, 2, 4, NK1]),
                                                    ALU.subtract).then_inc(R["s_shifted"], 1)
                        for u in range(1, U):
                            normalise(u)
                    passes(pool, emit)

                @block.tensor
                def _(pe):
                    nc.tensor.transpose(ps_a[0:B, 0:128], pool_all[:], ident).then_inc(mem_pe, 1)
                    for q in range(4):
                        for u in range(U):
                            pair = U * q + u
                            last = nc.tensor.matmul(banks[4 + q][:, 128 * u:128 * u + 128],
                                                    on_all[:, 2 * pair:2 * pair + 2, :].rearrange("p b t -> p (b t)"),
                                                    w_projx[:], start=True, stop=True)
                        last.then_inc(head_pe, 1)
                    pe.wait_ge(mem_dve, 1)
                    nc.tensor.transpose(ps_a[:, 512:512 + B], mem_rows[:], ident[0:B, 0:B]).then_inc(mem_pe, 1)
                    pe.wait_ge(mem_dve, 2)
                    pe.wait_ge(loaded1, n_loads1)
                    nc.tensor.matmul(ps_b[:, 0:B], w_mem[:], mem_cols[:], start=True, stop=True).then_inc(mem_pe, 1)
                    for q in range(4):
                        pe.wait_ge(head_dve, q + 1)
                        for u in range(U):
                            last = nc.tensor.transpose(banks[4 + q][:, 128 * u:128 * u + 128], normed_all[:, U * q + u, :], ident)
                        last.then_inc(head_pe, 1)
                    pe.wait_ge(mem_dve, 3)
                    pe.wait_ge(loaded1, n_loads1)
                    for j in range(NJ):
                        last = nc.tensor.matmul(ps_b[:, 512 + B * j:512 + B * j + B], w_qk1[:, 1, 128 * j:128 * j + 128],
                                                mem_t[:], start=True, stop=True)
                    last.then_inc(mem_pe, 1)
                    pe.wait_ge(mem_dve, 5)
                    pe.wait_ge(head_act, 4)

                    def emit(i, mlp, attention):
                        wait = waiter3(pe, i)

                        def values1(b):
                            for half in range(2):
                                if 2 * b + half >= 2:
                                    wait("v_ready", 2 * b + half - 1)
                                    alone(pe)
                                nc.tensor.matmul(ps_c[0:NKM, 512 * half:512 * half + 512], xm_now[:, b, :],
                                                 w_v1[:, 512 * half:512 * half + 512], start=True, stop=True
                                                 ).then_inc(R["v_done"], 1)

                        def mlp_step(n):
                            if n == HT_AT:
                                wait("hn_ready", 1, -1)
                                for u in range(U):
                                    last = nc.tensor.transpose(banks[6][:, 128 * u:128 * u + 128], normed[:, u, :], ident)
                                last.then_inc(R["ht_done"], 1)
                            if n in UP_AT:
                                m = UP_AT.index(n)
                                if m == 0:
                                    wait("ht_ready", 1, -1)
                                else:
                                    wait("up_ready", m, -1)
                                nc.tensor.matmul(banks[6], w_up1[:, m, :], h_t[:], start=True, stop=True)
                                nc.tensor.matmul(banks[7], w_up1[:, 3 + m, :], h_t[:], start=True, stop=True
                                                 ).then_inc(R["up_done"], 1)
                            if n == DOWN_AT:
                                wait("up_ready", 3, -1)
                                for u in range(U):
                                    for m in range(3):
                                        last = nc.tensor.matmul(banks[6][:, 128 * u:128 * u + 128], gate_e[:, m, 128 * u:128 * u + 128],
                                                                w_down1[:, m, :], start=(m == 0), stop=(m == 2))
                                last.then_inc(R["down_done"], 1)

                        for n in range(16):
                            if attention:
                                if n == 0:
                                    wait("xm_ready")
                                if n >= 4:
                                    wait("turn_read", n - 3)
                                    alone(pe)
                                elif n == 3 and mlp:
                                    wait("h_ready", 1, -1)
                                    alone(pe)
                                kind, j = slice_of(n)
                                nc.tensor.matmul(banks[n % 4], w_qk1[:, kind, 128 * j:128 * j + 128],
                                                 xm_now[:, :, 0:TP], start=True, stop=True).then_inc(R["turn_done"], 1)
                                if n % 2 == 1:
                                    values1(n // 2)
                            if mlp:
                                mlp_step(n)
                        if not attention:
                            return
                        if not mlp:
                            pe.wait_ge(persist_ready, 1)
                            pe.wait_ge(loaded_v, 16 * NB)
                        for half in range(2):
                            wait("rotated", 8 + 8 * half)
                            for u in range(U):
                                if half == 0:
                                    if u < 2:
                                        wait("turn_read", 14 + 2 * u)
                                    else:
                                        wait("s_read", u - 1)
                                elif u < 2:
                                    wait("s_read", u + 3)
                                else:
                                    wait("s_copied", u - 1)
                                alone(pe)
                                ps = (ps_a, ps_b)[u % 2]
                                for r in range(2):
                                    nc.tensor.matmul(ps[:, 512 * r:512 * r + SC], ident16[:],
                                                     causal16[:].rearrange("p j k -> p (j k)"), start=True, stop=False,
                                                     skip_group_check=True)
                                for j4 in range(4):
                                    j = 4 * half + j4
                                    for r in range(2):
                                        for b2 in range(2):
                                            last = nc.tensor.matmul(ps[64 * b2:64 * b2 + 64, 512 * r + NK1 * j4:512 * r + NK1 * j4 + NK1],
                                                                    q1[64 * r:64 * r + 64, j, 128 * u + 64 * b2:128 * u + 64 * b2 + 64],
                                                                    k1[64 * r:64 * r + 64, j, 2 * u + b2, :], start=False, stop=True,
                                                                    skip_group_check=True)
                                last.then_inc(R["s_done"], 1)

                        def weighted(u):
                            ps = (ps_c, ps_d)[u % 2]
                            if u == 0:
                                wait("v_ready", 2 * NB)
                            if u == 1 and mlp:
                                wait("y_ready", 1, -1)
                            for half in range(2):
                                wait("et_ready", 2 * u + half + 1)
                                if u >= 2:
                                    wait("o_ready", 2 * u - 3 + half)
                                for r in range(2):
                                    for j4 in range(4):
                                        j = 4 * half + j4
                                        head = 2 * j + r
                                        for b2 in range(2):
                                            last = nc.tensor.matmul(ps[64 * r:64 * r + 64, 128 * j + 64 * b2:128 * j + 64 * b2 + 64],
                                                                    v1[:, 2 * u + b2, D1 * head:D1 * head + D1],
                                                                    e1_t[u % 2][:, 8 * half + 4 * r + j4, 64 * b2:64 * b2 + 64],
                                                                    start=True, stop=True)
                                last.then_inc(R["o_done"], 1)

                        for u in range(U):
                            wait("e_normal", u + 1)
                            for half in range(2):
                                if u > 0:
                                    wait("et_ready", 2 * u - 1 + half)
                                else:
                                    wait("s_copied", U - 1 + half)
                                ps = (ps_a, ps_b)[half]
                                for n in range(8):
                                    last = nc.tensor.transpose(ps[0:NK1, 128 * n:128 * n + 128], s1[u][:, 8 * half + n, :], ident)
                                last.then_inc(R["et_done"], 1)
                            if u > 0:
                                weighted(u - 1)
                        weighted(U - 1)
                        wait("et_ready", 2 * U)
                        for u in range(U):
                            wait("o_ready", 2 * u + 2)
                            for j in range(NJ):
                                last = nc.tensor.matmul(banks[3][:, 128 * u:128 * u + 128], o1_t[u % 2][:, j, :], w_out1[:, j, :],
                                                        start=(j == 0), stop=(j == NJ - 1))
                            last.then_inc(R["out_done"], 1)
                    passes(pe, emit)

                @block.scalar
                def _(act):
                    act.wait_ge(loaded1, n_loads1)
                    for q in range(4):
                        act.wait_ge(head_pe, 4 + q + 1)
                        nc.scalar.activation(xm[:, NB * q:NB * q + NB, 0:TP], banks[4 + q].rearrange("p (b t) -> p b t", t=TP),
                                             ACT.Identity, scale=cols1[:, 0:1]).then_inc(head_act, 1)
                    act.wait_ge(head_act, 4)
                    act.wait_ge(mem_dve, 5)

                    def emit(i, mlp, attention):
                        wait = waiter3(act, i)
                        if attention:
                            nc.scalar.copy(xm_now[:], xm[:].rearrange("p (i b) k -> p i b k", b=NB)[:, i, :, :]
                                           ).then_inc(R["xm_ready"], 1)
                        for n in range(16):
                            for half in range(2) if attention and n % 2 == 1 else []:
                                b = n // 2
                                wait("v_done", 2 * b + half + 1)
                                nc.scalar.copy(v1[0:NKM, b, 512 * half:512 * half + 512], ps_c[0:NKM, 512 * half:512 * half + 512]
                                               ).then_inc(R["v_ready"], 1)
                            if mlp and n == HT_AT:
                                wait("ht_done", 1, -1)
                                nc.scalar.activation(h_t[:], banks[6], ACT.Identity, scale=cols1[:, 2:3]).then_inc(R["ht_ready"], 1)
                            if mlp and n in UP_AT:
                                m = UP_AT.index(n)
                                wait("up_done", m + 1, -1)
                                nc.scalar.activation(gate_e[:, m, :], banks[7], ACT.Exp,
                                                     bias=neg_gate_b[:, m:m + 1], scale=-1.0).then_inc(R["gate_exp"], 1)
                        if not attention:
                            return

                        def exp1(u):
                            wait("s_read", u + 1)
                            wait("s_shifted", u + 1)
                            nc.scalar.activation(s1[u][:], s1[u][:], ACT.Exp, scale=float(D1) ** -0.5).then_inc(R["e_ready"], 1)

                        for u in range(U + 1):
                            if u < U:
                                wait("s_top", u + 1)
                                nc.scalar.copy(s1_view(u, 1), scores1(u)).then_inc(R["s_copied"], 1)
                            if u > 0:
                                exp1(u - 1)
                        for u in range(U + 1):
                            for half in range(2):
                                if u < U:
                                    wait("et_done", 2 * u + half + 1)
                                    if u >= 2:
                                        wait("o_done", 2 * u - 3 + half)
                                    nc.scalar.copy(e1_t[u % 2][:, 8 * half:8 * half + 8, :],
                                                   (ps_a, ps_b)[half][0:NK1, :].rearrange("p (n t) -> p n t", n=8)).then_inc(R["et_ready"], 1)
                            for half in range(2):
                                if u > 0:
                                    v = u - 1
                                    wait("o_done", 2 * v + half + 1)
                                    if v >= 2:
                                        wait("out_done", v - 1)
                                    nc.scalar.copy(o1_t[v % 2][:, 4 * half:4 * half + 4, :],
                                                   (ps_c, ps_d)[v % 2][:, 512 * half:512 * half + 512].rearrange("p (n t) -> p n t", n=4)
                                                   ).then_inc(R["o_ready"], 1)
                    passes(act, emit)

                @block.vector
                def _(ve):
                    link, _ = chain(ve, sem("mem_chain"), 0, 0)
                    link(nc.vector.memset(st_all[:, NPAIR, :], 1.0))
                    ve.wait_ge(mem_pe, 1)
                    link(nc.vector.tensor_scalar(mem_rows[:], ps_a[0:B, 0:128], 1.0 / J, None, ALU.mult))
                    nc.vector.bn_stats(st_all[0:B, NPAIR, :], mem_rows[:])
                    for q in range(4):
                        ve.wait_ge(head_pe, q + 1)
                        rows = x_all[:, U * q:U * q + U, :]
                        link(nc.vector.tensor_tensor(rows, banks[4 + q].rearrange("p (u c) -> p u c", u=U), rows, ALU.add))
                    for pair in range(NPAIR):
                        ins = nc.vector.bn_stats(st_all[:, pair, :], x_all[:, pair, :])
                    link(ins)
                    for pair in range(NPAIR + 1):
                        ins = nc.vector.bn_aggr(mv_all[:, pair, :], st_all[:, pair, :])
                    link(ins)
                    ms, rstd, tmp = ms_all[:, 0, :], ms_all[:, 1, :], ms_all[:, 2, :]
                    link(nc.vector.tensor_tensor(ms, mv_all[:, :, 0], mv_all[:, :, 0], ALU.mult))
                    link(nc.vector.tensor_tensor(ms, ms, mv_all[:, :, 1], ALU.add))
                    rsqrt(ve, link, rstd, ms, tmp, EPS1)
                    nc.vector.tensor_scalar(mem_rows[:], mem_rows[:], ms_all[0:B, 1, NPAIR:NPAIR + 1], None, ALU.mult
                                            ).then_inc(mem_dve, 1)
                    for pair in range(NPAIR):
                        ins = nc.vector.tensor_scalar(normed_all[:, pair, :], x_all[:, pair, :], ms_all[:, 1, pair:pair + 1],
                                                      None, ALU.mult)
                        if pair % U == U - 1:
                            ins.then_inc(head_dve, 1)
                    ve.wait_ge(mem_pe, 2)
                    ve.wait_ge(loaded1, n_loads1)
                    nc.vector.tensor_scalar(mem_cols[:], ps_a[:, 512:512 + B], cols1[:, 1:2], None, ALU.mult).then_inc(mem_dve, 1)
                    link(nc.vector.tensor_scalar(neg_gate_b[:], cols1[:, 6:9], -1.0, None, ALU.mult))
                    link(nc.vector.tensor_copy(ident16[:], ident))
                    link(nc.vector.tensor_copy(causal16[:], causal1.unsqueeze(1).broadcast_to([128, 4, NK1])))
                    ve.wait_ge(mem_pe, 3)
                    nc.vector.tensor_copy(mem_t[:], ps_b[:, 0:B]).then_inc(mem_dve, 1)
                    ve.wait_ge(mem_dve, 3)
                    nc.vector.tensor_copy(xm[:, :, TP:NKM], mem_t[:].unsqueeze(2).broadcast_to([128, B, NM])).then_inc(mem_dve, 1)
                    ve.wait_ge(mem_pe, 4)
                    nc.vector.tensor_copy(mem_k[:], ps_b[:, 512:768].rearrange("p (j b) -> p j b", j=NJ)).then_inc(mem_dve, 1)
                    ve.wait_ge(mem_dve, 5)

                    def emit(i, mlp, attention):
                        wait = waiter3(ve, i)
                        if mlp:
                            link, ends = chain(ve, tail_chain, (i - 1) * NTAIL, NTAIL)
                            wait("out_done", U, -1)
                            nc.vector.tensor_tensor(h[:], banks[3].rearrange("p (u c) -> p u c", u=U),
                                                    x_all[:].rearrange("p (i u) c -> p i u c", u=U)[:, i - 1, :, :],
                                                    ALU.add).then_inc(R["h_ready"], 1)
                            wait("h_ready", 1, -1)
                            for u in range(U):
                                ins = nc.vector.bn_stats(st1[:, u, :], h[:, u, :])
                            link(ins)
                            alone(ve)
                            for u in range(U):
                                ins = nc.vector.bn_aggr(mv1[:, u, :], st1[:, u, :])
                            link(ins)
                            ms, rstd, tmp = ms1[:, 0, :], ms1[:, 1, :], ms1[:, 2, :]
                            link(nc.vector.tensor_tensor(ms, mv1[:, :, 0], mv1[:, :, 0], ALU.mult))
                            link(nc.vector.tensor_tensor(ms, ms, mv1[:, :, 1], ALU.add))
                            rsqrt(ve, link, rstd, ms, tmp, EPS1)
                            for u in range(U):
                                ins = nc.vector.tensor_scalar(normed[:, u, :], h[:, u, :], ms1[:, 1, u:u + 1], None, ALU.mult)
                            ins.then_inc(R["hn_ready"], 1)
                            mlp_link, mlp_ends = link, ends

                        def gate(m, part):
                            g = gate_e[:, m, :]
                            if part == 0:
                                wait("gate_exp", m + 1, -1)
                                mlp_link(nc.vector.tensor_scalar(g, g, 1.0, None, ALU.add))
                                mlp_link(nc.vector.reciprocal(g, g))
                            else:
                                mlp_link(nc.vector.scalar_tensor_tensor(g, banks[7], cols1[:, 6 + m:7 + m], g, ALU.add, ALU.mult))
                                nc.vector.scalar_tensor_tensor(g, banks[6], cols1[:, 3 + m:4 + m], g, ALU.add,
                                                               ALU.mult).then_inc(R["up_ready"], 1)

                        if attention:
                            link, ends = chain(ve, main_chain, i * NMAIN, NMAIN)
                            link(nc.vector.tensor_copy(k1[:, :, :, TP:NKM],
                                                       mem_k[:].rearrange("p j (i b) -> p i j b", b=NB)[:, i, :, :].unsqueeze(3).broadcast_to([128, NJ, NB, NM])))
                        for n in range(16):
                            if attention:
                                ps = banks[n % 4].rearrange("p (b t) -> p b t", t=TP)
                                wait("turn_done", n + 1)
                                if n >= NTURN:
                                    wait("rotated", n - NTURN + 1)
                                nc.vector.tensor_tensor(turn_a[n % NTURN][:], ps, cos.unsqueeze(1).broadcast_to([128, NB, TP]),
                                                        ALU.mult)
                                ins = nc.vector.stream_shuffle(turn_b[n % NTURN][:], ps, [p ^ 1 for p in range(32)])
                                ins.then_inc(R["turn_read"], 1)
                            for part in range(2):
                                if mlp and n - 1 - part in UP_AT:
                                    gate(UP_AT.index(n - 1 - part), part)
                            if mlp and n == HT_AT:
                                wait("hn_ready", 1, -1)
                                mlp_link(nc.vector.tensor_tensor(h[:], h[:], row_b1[:].unsqueeze(1).broadcast_to([128, U, C]), ALU.add))
                            if mlp and n == 15:
                                wait("down_done", 1, -1)
                                ve.wait_ge(stored, (i - 1) * 32 + 1)
                                nc.vector.tensor_tensor(y[:], banks[6].rearrange("p (u c) -> p u c", u=U), h[:], ALU.add
                                                        ).then_inc(R["y_ready"], 1)
                                wait("y_ready", 1, -1)
                                mlp_ends()
                        if not attention:
                            return

                        def total(u):
                            wait("e_ready", u + 1)
                            link(nc.vector.reduce_sum(s1_sum[:, u, :], s1[u][:], AX.X))
                            nc.vector.reciprocal(s1_sum[:, u, :], s1_sum[:, u, :]).then_inc(R["sum_ready"], 1)
                        for u in range(U):
                            wait("s_done", u + 1)
                            link(nc.vector.reduce_max(top1(u, 0), scores1(u), AX.X))
                            nc.vector.tensor_tensor(s1_view(u, 0), scores1(u),
                                                    top1(u, 0).unsqueeze(3).broadcast_to([128, 2, 4, NK1]),
                                                    ALU.subtract).then_inc(R["s_read"], 1)
                        for u in range(U):
                            wait("s_done", U + u + 1)
                            nc.vector.reduce_max(top1(u, 1), scores1(u), AX.X).then_inc(R["s_top"], 1)
                            if u >= 2:
                                total(u - 2)
                        total(U - 2)
                        total(U - 1)
                        ends()
                    passes(ve, emit)


def as_words(a):
    words = np.zeros(a.shape + (4,), np.uint8)
    words[..., 0] = a.view(np.uint8)
    return words.view(np.int32)[..., 0]


INPUTS = {
    "x": ("x", lambda a: a),
    "ctx": ("ctx_1024", lambda a: a),
    "mask": ("mask_BxS_bf0", lambda a: as_words(a).reshape(1, B, T)),
    "w_qkv0": ("L0_xattn_sa_wqkv", lambda a: a),
    "w_proj0": ("L0_xattn_sa_wproj", lambda a: a),
    "w_kv": ("L0_xattn_ed_wkv", lambda a: a),
    "w_q": ("L0_xattn_ed_wq", lambda a: a),
    "w_projx": ("L0_xattn_ed_wproj", lambda a: a),
    "w_up0": ("L0_xattn_ff_w1", lambda a: a),
    "w_down0": ("L0_xattn_ff_w2", lambda a: a),
    "b_up0": ("L0_xattn_ff_b1", lambda a: a.reshape(4, 128).T),
}


def layout(inputs):
    g = {k: np.asarray(v) for k, v in inputs.items()}
    out = {n: np.ascontiguousarray(f(g[k])) for n, (k, f) in INPUTS.items()}
    out["cols"] = np.ascontiguousarray(np.stack(
        [g[f"L0_xattn_ln{n}_{v}"] for n in (1, 2, 3) for v in "gb"], 1))
    out["rows0"] = np.ascontiguousarray(np.stack(
        [g["L0_xattn_sa_bproj"], g["L0_xattn_ed_bproj"], g["L0_xattn_ff_b2"]]).reshape(1, 3, C))
    w = g["L1_xattn_to_qkv_w"]
    out["w_qkv1"] = w
    out["w_out1"] = g["L1_xattn_to_out_w"]
    out["w_mem"] = g["L1_xattn_to_mem_tokens_w"]
    persist = g["L1_xattn_persist_mem"]
    out["persist_k"] = persist.reshape(8, 2, NM, D1).transpose(1, 3, 0, 2).reshape(128, 8, NM)
    out["persist_v"] = persist.transpose(1, 0, 2).reshape(NM, H1 * D1)
    up = np.zeros((128, 2, DFFP), np.float32)
    up[:, :, :DFF] = g["L1_xattn_ff_w1"].reshape(128, 2, DFF)
    out["w_up1"] = up.reshape(128, 6, 128)
    up_b = np.zeros((2, DFFP), np.float32)
    up_b[:, :DFF] = g["L1_xattn_ff_b1"].reshape(2, DFF)
    down = np.zeros((DFFP, C), np.float32)
    down[:DFF] = g["L1_xattn_ff_w2"]
    out["w_down1"] = down
    norms = np.stack([g[f"L1_xattn_{n}_norm_w"] for n in ("attn", "mem_pool", "ff")], 1)
    out["cols1"] = np.concatenate([norms, up_b.reshape(6, 128).T], 1)
    out["row_b1"] = g["L1_xattn_ff_b2"].reshape(1, C)
    out["const"] = constants()
    out["ones"] = np.ones((2, 4, J), np.float16)
    out = {n: np.ascontiguousarray(a) for n, a in out.items()}
    return out


def kernel(**inputs):
    import concourse.bacc as bacc
    from concourse.bass_utils import run_bass_kernel_spmd

    nc = bacc.Bacc("TRN2", target_bir_lowering=False, num_devices=1)
    arrays = layout(inputs)
    dram = {n: nc.dram_tensor(f"in_{n}", a.shape, mybir.dt.from_np(a.dtype), kind="ExternalInput").ap()
            for n, a in arrays.items()}
    dram["out"] = nc.dram_tensor("out", (B, T, C), F32, kind="ExternalOutput").ap()
    program(nc, dram)
    result = run_bass_kernel_spmd(nc, [{f"in_{n}": a for n, a in arrays.items()}], core_ids=[0])
    return result.results[0]["out"]
```
